# Optimizing a Trainium2 kernel written in Bass

```python
import numpy as np
import jax
import jax.numpy as jnp

def _softmax(x, axis=-1):
    return jax.nn.softmax(x, axis=axis)

def _gelu(x):
    return jax.nn.gelu(x, approximate=True)

def _silu(x):
    return jax.nn.silu(x)

def _sigmoid(x):
    return jax.nn.sigmoid(x)

def _layernorm(x, axis=-1, eps=1e-05):
    m = jnp.mean(x, axis=axis, keepdims=True)
    v = jnp.var(x, axis=axis, keepdims=True)
    return (x - m) / jnp.sqrt(v + eps)

def _scatter_add(tgt, idx, src, axis=0):
    return tgt.at[idx].add(src)

def _segment_sum(src, seg, n):
    return jax.ops.segment_sum(src, seg, n)
kernel_name = 'mk_macaron_d2_jaxref_r8_c272fb'

def setup_inputs(seed: int=0):
    np.random.seed(seed)
    _w = jnp.asarray

    def _L0_attn_setup():
        import jax, jax.numpy as jnp
        import numpy as np
        import math
        N_HEAD = 16
        ATTN_THRESHOLD = -0.1
        EPS = 1e-06
        key = jax.random.key(seed)
        ks = jax.random.split(key, 5)
        B, T, C = (2, 256, 256)
        s = 1.0 / math.sqrt(C)
        return {'x': jax.random.normal(ks[0], (B, T, C), dtype=jnp.float32), 'Wq': jax.random.normal(ks[1], (C, C), dtype=jnp.float32) * s, 'Wk': jax.random.normal(ks[2], (C, C), dtype=jnp.float32) * s, 'Wv': jax.random.normal(ks[3], (C, C), dtype=jnp.float32) * s, 'Wo': jax.random.normal(ks[4], (C, C), dtype=jnp.float32) * s}
    _L0_attn_in = _L0_attn_setup()

    def _L0_ffn_setup():
        import jax, jax.numpy as jnp
        import numpy as np
        LORA_ALPHA = 16.0
        TOP_K = 2
        key = jax.random.key(seed)
        k_x, k_w, k_g, k_a, k_b = jax.random.split(key, 5)
        B, S, H, O, E, R = (2, 256, 256, 256, 8, 16)
        x = jax.random.normal(k_x, (B, S, H), dtype=jnp.float32)
        weight = jax.random.normal(k_w, (O, H), dtype=jnp.float32)
        gate_w = jax.random.normal(k_g, (E, H), dtype=jnp.float32) * 0.02
        A_w = jax.random.normal(k_a, (E, R, H), dtype=jnp.float32) * (1.0 / np.sqrt(H))
        B_w = jax.random.normal(k_b, (E, O, R), dtype=jnp.float32) * 0.01
        return {'x': x, 'weight': weight, 'gate_w': gate_w, 'A_w': A_w, 'B_w': B_w}
    _L0_ffn_in = _L0_ffn_setup()

    def _L1_attn_setup():
        import jax, jax.numpy as jnp
        import numpy as np
        DECAY = 0.95

        def smear(x, decay):
            a = jnp.full_like(x, decay)

            def combine(c1, c2):
                a1, b1 = c1
                a2, b2 = c2
                return (a1 * a2, a2 * b1 + b2)
            _, y = jax.lax.associative_scan(combine, (a, x), axis=1)
            return y
        key = jax.random.key(seed)
        ks = jax.random.split(key, 5)
        B, S, E, M = (4, 512, 256, 256)
        x = jax.random.normal(ks[0], (B, S, E), dtype=jnp.float32)
        s = 0.02
        Wv = jax.random.normal(ks[1], (E, M), dtype=jnp.float32) * s
        Wg = jax.random.normal(ks[2], (E, M), dtype=jnp.float32) * s
        bg = jnp.zeros((M,), dtype=jnp.float32)
        Wq = jax.random.normal(ks[3], (E, M), dtype=jnp.float32) * s
        bq = jnp.zeros((M,), dtype=jnp.float32)
        Wo = jax.random.normal(ks[4], (M, E), dtype=jnp.float32) * s
        return {'x': x, 'Wv': Wv, 'Wg': Wg, 'bg': bg, 'Wq': Wq, 'bq': bq, 'Wo': Wo}
    _L1_attn_in = _L1_attn_setup()

    def _L1_ffn_setup():
        import jax, jax.numpy as jnp
        import numpy as np
        TOP_K = 4
        key = jax.random.key(seed)
        ks = jax.random.split(key, 9)
        B, T, D, H, NE = (2, 128, 256, 176, 16)
        s = 0.02
        return {'x': jax.random.normal(ks[0], (B, T, D), jnp.float32), 'gate_w': jax.random.normal(ks[1], (NE, D), jnp.float32) * s, 'gate_b': jax.random.normal(ks[2], (NE,), jnp.float32) * s, 'w1_shared': jax.random.normal(ks[3], (D, H), jnp.float32) * s, 'w2_shared': jax.random.normal(ks[4], (H, D), jnp.float32) * s, 'w3_shared': jax.random.normal(ks[5], (D, H), jnp.float32) * s, 'w1_routed': jax.random.normal(ks[6], (NE, D, H), jnp.float32) * s, 'w2_routed': jax.random.normal(ks[7], (NE, H, D), jnp.float32) * s, 'w3_routed': jax.random.normal(ks[8], (NE, D, H), jnp.float32) * s}
    _L1_ffn_in = _L1_ffn_setup()
    _d = {'L0_attn_x': _L0_attn_in['x'], 'L0_attn_Wq': _L0_attn_in['Wq'], 'L0_attn_Wk': _L0_attn_in['Wk'], 'L0_attn_Wv': _L0_attn_in['Wv'], 'L0_attn_Wo': _L0_attn_in['Wo'], 'L0_ffn_weight': _L0_ffn_in['weight'], 'L0_ffn_gate_w': _L0_ffn_in['gate_w'], 'L0_ffn_A_w': _L0_ffn_in['A_w'], 'L0_ffn_B_w': _L0_ffn_in['B_w'], 'L1_attn_Wv': _L1_attn_in['Wv'], 'L1_attn_Wg': _L1_attn_in['Wg'], 'L1_attn_bg': _L1_attn_in['bg'], 'L1_attn_Wq': _L1_attn_in['Wq'], 'L1_attn_bq': _L1_attn_in['bq'], 'L1_attn_Wo': _L1_attn_in['Wo'], 'L1_ffn_gate_w': _L1_ffn_in['gate_w'], 'L1_ffn_gate_b': _L1_ffn_in['gate_b'], 'L1_ffn_w1_shared': _L1_ffn_in['w1_shared'], 'L1_ffn_w2_shared': _L1_ffn_in['w2_shared'], 'L1_ffn_w3_shared': _L1_ffn_in['w3_shared'], 'L1_ffn_w1_routed': _L1_ffn_in['w1_routed'], 'L1_ffn_w2_routed': _L1_ffn_in['w2_routed'], 'L1_ffn_w3_routed': _L1_ffn_in['w3_routed']}
    _x0 = _d['L0_attn_x']
    _d['L0_attn_x'] = jax.random.normal(jax.random.fold_in(jax.random.key(seed), 1), (4, 1024, 256), dtype=_x0.dtype)
    del _x0
    return _d

def reference(L0_attn_x, L0_attn_Wq, L0_attn_Wk, L0_attn_Wv, L0_attn_Wo, L0_ffn_weight, L0_ffn_gate_w, L0_ffn_A_w, L0_ffn_B_w, L1_attn_Wv, L1_attn_Wg, L1_attn_bg, L1_attn_Wq, L1_attn_bq, L1_attn_Wo, L1_ffn_gate_w, L1_ffn_gate_b, L1_ffn_w1_shared, L1_ffn_w2_shared, L1_ffn_w3_shared, L1_ffn_w1_routed, L1_ffn_w2_routed, L1_ffn_w3_routed):

    def _L0_attn_ref(x, Wq, Wk, Wv, Wo):
        import jax, jax.numpy as jnp
        import numpy as np
        import math
        N_HEAD = 16
        ATTN_THRESHOLD = -0.1
        EPS = 1e-06
        B, T, C = x.shape
        H = N_HEAD
        hd = C // H
        scale = 1.0 / math.sqrt(hd)

        def proj(W):
            return jnp.einsum('btc,oc->bto', x, W).reshape(B, T, H, hd).swapaxes(1, 2)
        q, k, v = (proj(Wq), proj(Wk), proj(Wv))
        scores = jnp.einsum('bhqd,bhkd->bhqk', q, k) * scale
        causal = jnp.tril(jnp.ones((T, T), dtype=bool))
        w = jnp.where(causal, jax.nn.relu(scores - ATTN_THRESHOLD), 0.0)
        w = w / (jnp.sum(w, axis=-1, keepdims=True) + EPS)
        out = jnp.einsum('bhqk,bhkd->bhqd', w, v)
        out = out.swapaxes(1, 2).reshape(B, T, C)
        return jnp.einsum('btc,oc->bto', out, Wo)

    def _L0_ffn_ref(x, weight, gate_w, A_w, B_w):
        import jax, jax.numpy as jnp
        import numpy as np
        LORA_ALPHA = 16.0
        TOP_K = 2
        E = gate_w.shape[0]
        out = jnp.einsum('bsh,oh->bso', x, weight)
        logits = jnp.einsum('bsh,eh->bse', x, gate_w)
        probs = jax.nn.softmax(logits, axis=-1)
        topk_w, topk_idx = jax.lax.top_k(probs, TOP_K)
        topk_w = topk_w / jnp.sum(topk_w, axis=-1, keepdims=True)
        onehot = jax.nn.one_hot(topk_idx, E, dtype=x.dtype)
        cw = jnp.einsum('bsk,bske->bse', topk_w, onehot)
        t = jnp.einsum('bsh,erh->bser', x, A_w)
        t = t * cw[..., None]
        lora = jnp.einsum('bser,eor->bso', t, B_w)
        return out + LORA_ALPHA * lora

    def _L1_attn_ref(x, Wv, Wg, bg, Wq, bq, Wo):
        import jax, jax.numpy as jnp
        import numpy as np
        DECAY = 0.95

        def smear(x, decay):
            a = jnp.full_like(x, decay)

            def combine(c1, c2):
                a1, b1 = c1
                a2, b2 = c2
                return (a1 * a2, a2 * b1 + b2)
            _, y = jax.lax.associative_scan(combine, (a, x), axis=1)
            return y
        scale = jnp.float32(np.sqrt(1.0 - DECAY))
        gate = jax.nn.sigmoid(jnp.einsum('bse,em->bsm', x, Wg) + bg)
        store = jnp.einsum('bse,em->bsm', x, Wv) * gate * scale
        mem = smear(store, DECAY)
        que = jax.nn.sigmoid(jnp.einsum('bse,em->bsm', x, Wq) + bq)
        load = mem * que * scale
        return jnp.einsum('bsm,me->bse', load, Wo)

    def _L1_ffn_ref(x, gate_w, gate_b, w1_shared, w2_shared, w3_shared, w1_routed, w2_routed, w3_routed):
        import jax, jax.numpy as jnp
        import numpy as np
        TOP_K = 4
        n_experts = w1_routed.shape[0]
        logits = jnp.einsum('ed,btd->bte', gate_w, x)
        scores = jax.nn.sigmoid(logits) + gate_b
        weights, indices = jax.lax.top_k(scores, TOP_K)
        weights = weights / weights.sum(-1, keepdims=True)
        shared_out = jax.nn.silu(x @ w1_shared) * (x @ w3_shared) @ w2_shared
        one_hot = jax.nn.one_hot(indices, n_experts, dtype=x.dtype)
        router_probs = (weights[..., None] * one_hot).sum(-2)
        h1 = jnp.einsum('btd,edc->btec', x, w1_routed)
        h2 = jnp.einsum('btd,edc->btec', x, w3_routed)
        h3 = jax.nn.silu(h1 * h2)
        experts_out = jnp.einsum('btec,ecd->bted', h3, w2_routed)
        routed_out = jnp.einsum('bted,bte->btd', experts_out, router_probs)
        return shared_out + routed_out
    x = L0_attn_x
    x = x + 0.5 * _L0_ffn_ref(_layernorm(x, axis=-1), L0_ffn_weight, L0_ffn_gate_w, L0_ffn_A_w, L0_ffn_B_w)
    x = x + _L0_attn_ref(_layernorm(x, axis=-1), L0_attn_Wq, L0_attn_Wk, L0_attn_Wv, L0_attn_Wo)
    x = x + 0.5 * _L0_ffn_ref(_layernorm(x, axis=-1), L0_ffn_weight, L0_ffn_gate_w, L0_ffn_A_w, L0_ffn_B_w)
    x = x + 0.5 * _L1_ffn_ref(_layernorm(x, axis=-1), L1_ffn_gate_w, L1_ffn_gate_b, L1_ffn_w1_shared, L1_ffn_w2_shared, L1_ffn_w3_shared, L1_ffn_w1_routed, L1_ffn_w2_routed, L1_ffn_w3_routed)
    x = x + _L1_attn_ref(_layernorm(x, axis=-1), L1_attn_Wv, L1_attn_Wg, L1_attn_bg, L1_attn_Wq, L1_attn_bq, L1_attn_Wo)
    x = x + 0.5 * _L1_ffn_ref(_layernorm(x, axis=-1), L1_ffn_gate_w, L1_ffn_gate_b, L1_ffn_w1_shared, L1_ffn_w2_shared, L1_ffn_w3_shared, L1_ffn_w1_routed, L1_ffn_w2_routed, L1_ffn_w3_routed)
    return x

_drawn_inputs = setup_inputs


def setup_inputs(seed=0):
    import zlib

    import numpy as np

    out = dict(_drawn_inputs(seed))
    spreads = {'L1_attn_bg': (0.0, 0.8), 'L1_attn_bq': (0.0, 0.8)}
    factors = {'L0_attn_Wq': 3.311,
     'L0_attn_Wk': 3.235,
     'L0_attn_Wv': 2.895,
     'L0_attn_Wo': 2.913,
     'L1_attn_Wv': 8.0,
     'L1_attn_Wg': 8.0,
     'L1_attn_Wq': 8.0,
     'L1_attn_Wo': 8.0,
     'L1_ffn_gate_w': 8.0,
     'L1_ffn_gate_b': 8.0,
     'L1_ffn_w1_shared': 8.0,
     'L1_ffn_w2_shared': 8.0,
     'L1_ffn_w3_shared': 8.0,
     'L1_ffn_w1_routed': 8.0,
     'L1_ffn_w2_routed': 8.0,
     'L1_ffn_w3_routed': 8.0}
    for name, (base, spread) in spreads.items():
        noise = np.random.default_rng([zlib.crc32(name.encode()), seed]).standard_normal(out[name].shape)
        drawn = base * np.exp(spread * noise) if base else spread * noise
        out[name] = jnp.asarray(drawn.astype(out[name].dtype))
    for name, factor in factors.items():
        out[name] = (out[name] * factor).astype(out[name].dtype)
    return out
```

```python
import concourse.bass as bass
from concourse import mybir
from contextlib import ExitStack

P = 128
F32, F32R, BF16 = mybir.dt.float32, mybir.dt.float32r, mybir.dt.bfloat16
I32, U32 = mybir.dt.int32, mybir.dt.uint32
ACT, ALU, AX = mybir.ActivationFunctionType, mybir.AluOpType, mybir.AxisListType
EPS_NORM = 1e-5

BATCH, SEQ, DIM = 4, 1024, 256
TOKENS = BATCH * SEQ
TILES = TOKENS // P
KD = DIM // P
GT = 4
GROUPS = TILES // GT
GTOK = GT * P


def some(count):
    return not isinstance(count, int) or count > 0


def live(step, count):
    return not isinstance(step, int) or 0 <= step < count


def steps(eng, count, step, tail=0, ways=2):
    for p in range(ways):
        step(0, p)
    with eng.Fori(1, count // ways) as u:
        for p in range(ways):
            step(u, p)
    for n in range(count, count + tail):
        step(n // ways, n % ways)


def back(u, p):
    return (u, 0) if p else (u - 1, 1)


class Chain:

    def __init__(self, eng, sem, per_item):
        self.eng, self.sem, self.per_item = eng, sem, per_item

    def item(self, n):
        self.base, self.done = n * self.per_item, 0

    def link(self, instruction):
        self.done += 1
        assert self.done <= self.per_item
        instruction.then_inc(self.sem, 1)
        self.eng.wait_ge(self.sem, self.base + self.done)


class Norm:

    def __init__(self, nc, sb):
        self.nc = nc
        self.stats, self.mean, self.rstd = sb("stats", [P, TILES, 6]), sb("mean", [P, TILES]), sb("rstd", [P, TILES])
        self.var, self.work = sb("var", [P, TILES]), sb("work", [P, TILES])

    def statistics(self, x4, g):
        for j in range(GT):
            last = self.nc.vector.bn_stats(self.stats[:, bass.ds(GT * g + j, 1), :], x4[:, j, :])
        return last

    def finish(self, sem, name):
        nc, s, links = self.nc, self.stats, sem(name + "_norm_links")
        var_ready, root_ready = sem(name + "_var_ready"), sem(name + "_root_ready")
        mean, var, rstd, work = self.mean[:, :], self.var[:, :], self.rstd[:, :], self.work[:, :]
        with nc.Block() as block:
            @block.vector
            def _(dve):
                chain = Chain(dve, links, 11)
                chain.item(0)
                vec = nc.vector
                vec.tensor_tensor(mean, s[:, :, 1], s[:, :, 4], ALU.add)
                vec.tensor_tensor(var, s[:, :, 2], s[:, :, 5], ALU.add)
                chain.link(vec.tensor_tensor(work, s[:, :, 1], s[:, :, 4], ALU.subtract))
                vec.tensor_scalar(mean, mean, 0.5, None, ALU.mult)
                vec.tensor_scalar(var, var, 1.0 / DIM, EPS_NORM, ALU.mult, ALU.add)
                chain.link(vec.tensor_tensor(work, work, work, ALU.mult))
                chain.link(vec.scalar_tensor_tensor(out=var, in0=work, scalar=0.25, in1=var, op0=ALU.mult, op1=ALU.add))
                vec.tensor_copy(work, var).then_inc(var_ready, 1)
                dve.wait_ge(root_ready, 1)
                chain.link(vec.reciprocal(rstd, work))
                chain.link(vec.tensor_tensor(work, rstd, rstd, ALU.mult))
                chain.link(vec.tensor_tensor(work, work, var, ALU.mult))
                chain.link(vec.tensor_scalar(work, work, -0.5, 1.5, ALU.mult, ALU.add))
                chain.link(vec.tensor_tensor(rstd, rstd, work, ALU.mult))

            @block.scalar
            def _(act):
                act.wait_ge(var_ready, 1)
                nc.scalar.activation(work, var, ACT.Sqrt).then_inc(root_ready, 1)

    def apply_tile(self, X, out, t):
        return self.nc.vector.tensor_scalar(out, X[:, bass.ds(t, 1), :].rearrange("p a d -> p (a d)"),
                                            self.mean[:, bass.ds(t, 1)], self.rstd[:, bass.ds(t, 1)],
                                            ALU.subtract, ALU.mult)

    def apply(self, x4, xn4, g):
        for j in range(GT):
            last = self.nc.vector.tensor_scalar(xn4[:, j, :], x4[:, j, :], self.mean[:, bass.ds(GT * g + j, 1)],
                                                self.rstd[:, bass.ds(GT * g + j, 1)], ALU.subtract, ALU.mult)
        return last


LORA_E, LORA_R = 8, 16
LER = LORA_E * LORA_R
LA = LER + LORA_E


def lora_ffn(nc, name, sem, X, norm, w_lora, w_dense, w_b, ident, iota8):
    with ExitStack() as mem:
        def sb(n, shape, dt=F32):
            return mem.enter_context(nc.sbuf_tensor(f"{name}_{n}", shape, dt))

        def ps(n, shape):
            return mem.enter_context(nc.psum_tensor(f"{name}_{n}", shape, F32))

        xn, xT = sb("xn", [P, 2, GT, DIM]), sb("xT", [P, 2, KD, GTOK])
        top, idx, idxf = sb("top", [P, GT, 8]), sb("idx", [P, GT, 8], U32), sb("idxf", [P, GT, 2])
        gap, second, total = sb("gap", [P, GT]), sb("second", [P, GT]), sb("total", [P, GT])
        share, onehot, cw = sb("share", [P, GT, 2]), sb("onehot", [P, GT, 2, 8]), sb("cw", [P, GT, 8])
        tw, twT = sb("tw", [P, GT, LER]), sb("twT", [P, GTOK])
        ps_xT, ps_lora, ps_out = ps("ps_xT", [P, KD, GTOK]), ps("ps_lora", [P, 2, 512]), ps("ps_out", [P, 2, 512])
        ps_twT = ps("ps_twT", [P, GTOK])

        route_chain = sem(name + "_route_chain")
        xn_ready, xT_made, xT_ready = sem(name + "_xn_ready"), sem(name + "_xT_made"), sem(name + "_xT_ready")
        lora_made, gap_ready, second_ready = sem(name + "_lora_made"), sem(name + "_gap_ready"), sem(name + "_second_ready")
        tw_ready, twT_made, twT_ready = sem(name + "_tw_ready"), sem(name + "_twT_made"), sem(name + "_twT_ready")
        out_made, added = sem(name + "_out_made"), sem(name + "_added")

        def lora_cols(j, a, b):
            return ps_lora[:, j // 2, (j % 2) * LA + a:(j % 2) * LA + b]

        with nc.Block() as block:
            @block.vector
            def _(dve):
                route = Chain(dve, route_chain, 8)
                rstd_col = norm.rstd[:, 0:1]

                def step(u, p):
                    g = 2 * u + p
                    if live(g, GROUPS):
                        if some(g - 1):
                            dve.wait_ge(xT_made, g - 1)
                        norm.apply(X[:, bass.ds(GT * g, GT), :], xn[:, p], g).then_inc(xn_ready, 1)
                    if live(g - 1, GROUPS):
                        h = g - 1
                        route.item(h)
                        dve.wait_ge(lora_made, h + 1)
                        nc.vector.tensor_copy(total[:, 0:1], rstd_col)
                        for j in range(GT):
                            last = nc.vector.max(top[:, j, :], lora_cols(j, LER, LA))
                        route.link(last)
                        nc.vector.tensor_tensor(gap[:, :], top[:, :, 1], top[:, :, 0],
                                                ALU.subtract).then_inc(gap_ready, 1)
                        for j in range(GT):
                            last = nc.vector.max_index(idx[:, j, :], top[:, j, :], lora_cols(j, LER, LA))
                        route.link(last)
                        route.link(nc.vector.tensor_copy(idxf[:, :, :], idx[:, :, 0:2]))
                        dve.wait_ge(second_ready, h + 1)
                        route.link(nc.vector.tensor_scalar(total[:, :], second[:, :], 1.0, None, ALU.add))
                        route.link(nc.vector.reciprocal(share[:, :, 0], total[:, :]))
                        nc.vector.tensor_tensor(share[:, :, 1], second[:, :], share[:, :, 0], ALU.mult)
                        route.link(nc.vector.tensor_tensor(
                            onehot[:, :, :, :], iota8[:, :, :, :],
                            idxf[:, :, :].unsqueeze(3).to_broadcast([P, GT, 2, 8]), ALU.is_equal))
                        route.link(nc.vector.tensor_tensor(
                            onehot[:, :, :, :], onehot[:, :, :, :],
                            share[:, :, :].unsqueeze(3).to_broadcast([P, GT, 2, 8]), ALU.mult))
                        route.link(nc.vector.tensor_tensor(cw[:, :, :], onehot[:, :, 0, :], onehot[:, :, 1, :], ALU.add))
                        if some(h):
                            dve.wait_ge(twT_made, h)
                        for j in range(GT):
                            last = nc.vector.tensor_tensor(
                                tw[:, j, :].rearrange("p (e r) -> p e r", e=LORA_E),
                                lora_cols(j, 0, LER).rearrange("p (e r) -> p e r", e=LORA_E),
                                cw[:, j, :].unsqueeze(2).to_broadcast([P, LORA_E, LORA_R]), ALU.mult)
                        last.then_inc(tw_ready, 1)
                    if live(g - 2, GROUPS):
                        h = g - 2
                        dve.wait_ge(out_made, h + 1)
                        x4 = X[:, bass.ds(GT * h, GT), :]
                        nc.vector.tensor_tensor(x4, x4, ps_out[:, :, :].rearrange("p a (b d) -> p (a b) d", d=DIM),
                                                ALU.add).then_inc(added, 1)
                        dve.wait_ge(added, h + 1)
                        norm.statistics(x4, h)

                steps(dve, GROUPS, step, tail=2)

            @block.scalar
            def _(act):
                def step(u, p):
                    g = 2 * u + p
                    if live(g, GROUPS):
                        act.wait_ge(xT_made, g + 1)
                        nc.scalar.copy(xT[:, p], ps_xT[:, :, :]).then_inc(xT_ready, 1)
                    if live(g - 1, GROUPS):
                        if some(g):
                            act.wait_ge(gap_ready, g)
                        nc.scalar.activation(second[:, :], gap[:, :], ACT.Exp).then_inc(second_ready, 1)
                        if some(g):
                            act.wait_ge(twT_made, g)
                        nc.scalar.copy(twT[:, :], ps_twT[:, :]).then_inc(twT_ready, 1)

                steps(act, GROUPS, step, tail=1)

            @block.tensor
            def _(pe):
                def step(u, p):
                    g = 2 * u + p
                    if live(g, GROUPS):
                        pe.wait_ge(xn_ready, g + 1)
                        if some(g):
                            pe.wait_ge(xT_ready, g)
                        for j in range(GT):
                            for k in range(KD):
                                last = nc.tensor.transpose(ps_xT[:, k, j * P:(j + 1) * P],
                                                           xn[:, p, j, k * P:(k + 1) * P], ident)
                        last.then_inc(xT_made, 1)
                        pe.wait_ge(xT_ready, g + 1)
                        if some(g):
                            pe.wait_ge(tw_ready, g)
                        for j in range(GT):
                            for k in range(KD):
                                last = nc.tensor.matmul(lora_cols(j, 0, LA), xT[:, p, k, j * P:(j + 1) * P],
                                                        w_lora[:, k, :], start=(k == 0), stop=(k == KD - 1))
                        last.then_inc(lora_made, 1)
                    if live(g - 1, GROUPS):
                        h, q = g - 1, 1 - p
                        if some(h):
                            pe.wait_ge(added, h)
                        for j in range(GT):
                            for k in range(KD):
                                nc.tensor.matmul(ps_out[:, j // 2, (j % 2) * DIM:(j % 2 + 1) * DIM],
                                                 xT[:, q, k, j * P:(j + 1) * P], w_dense[:, k, :],
                                                 start=(k == 0 and j % 2 == 0), stop=False,
                                                 skip_group_check=True)
                        pe.wait_ge(tw_ready, h + 1)
                        if some(h):
                            pe.wait_ge(twT_ready, h)
                        for j in range(GT):
                            last = nc.tensor.transpose(ps_twT[:, j * P:(j + 1) * P], tw[:, j, :], ident)
                        last.then_inc(twT_made, 1)
                        pe.wait_ge(twT_ready, h + 1)
                        for j in range(GT):
                            last = nc.tensor.matmul(ps_out[:, j // 2, (j % 2) * DIM:(j % 2 + 1) * DIM],
                                                    twT[:, j * P:(j + 1) * P], w_b, start=False, stop=True,
                                                    skip_group_check=True)
                        last.then_inc(out_made, 1)

                steps(pe, GROUPS, step, tail=1)


HEADS = 16
HD = DIM // HEADS
GH = 4
HGROUPS = HEADS // GH
QK_SCALE = HD ** -0.5
THRESHOLD = -0.1
DEN_EPS = 1e-6
PARTS = 3
Q_ROWS, K_ROWS = (0, 0, 1, 0, 2, 1), (0, 1, 0, 2, 0, 1)
STACK = HD * len(Q_ROWS)
QBLOCKS = SEQ // GTOK
KTILES = SEQ // P


def project(nc, sem, X, norm, weights, ident, V, parts_dram):
    wq, wk, wv = weights
    with ExitStack() as mem:
        def sb(n, shape, dt=F32):
            return mem.enter_context(nc.sbuf_tensor("pr_" + n, shape, dt))

        def ps(n, shape):
            return mem.enter_context(nc.psum_tensor("pr_" + n, shape, F32))

        xn, xT = sb("xn", [P, 2, GT, DIM]), sb("xT", [P, 2, KD, GTOK])
        parts = sb("parts", [P, 2, 2, KD, PARTS, GTOK], BF16)
        rest = sb("rest", [P, 2, KD, GTOK])
        ps_xT, ps_v = ps("ps_xT", [P, KD, GTOK]), ps("ps_v", [P, GT, DIM])
        ps_qk = ps("ps_qk", [P, 2, KD, GTOK])
        xn_ready, xT_made, xT_ready = sem("pr_xn_ready"), sem("pr_xT_made"), sem("pr_xT_ready")
        qk_made, part1_ready, rest_ready, part2_ready, part3_ready = (
            sem("pr_" + n) for n in ("qk_made", "part1_ready", "rest_ready", "part2_ready", "part3_ready"))
        v_made, v_ready = sem("pr_v_made"), sem("pr_v_ready")
        stored = [sem(f"pr_stored{p}") for p in range(2)]
        scales = (QK_SCALE, 1.0)
        units = [(w, m) for w in range(2) for m in range(KD)]

        with nc.Block() as block:
            @block.vector
            def _(dve):
                def step(u, p):
                    g = 2 * u + p
                    if live(g, GROUPS):
                        if some(g - 1):
                            dve.wait_ge(xT_made, g - 1)
                        norm.apply(X[:, bass.ds(GT * g, GT), :], xn[:, p], g).then_inc(xn_ready, 1)
                    if live(g - 1, GROUPS):
                        for i, (w, m) in enumerate(units):
                            dve.wait_ge(part1_ready, 4 * (g - 1) + i + 1)
                            if some(4 * (g - 2) + i + 1):
                                dve.wait_ge(part3_ready, 4 * (g - 2) + i + 1)
                            nc.vector.scalar_tensor_tensor(
                                out=rest[:, w, m, :], in0=ps_qk[:, w, m, :], scalar=scales[w],
                                in1=parts[:, 1 - p, w, m, 0, :], op0=ALU.mult, op1=ALU.subtract).then_inc(rest_ready, 1)

                steps(dve, GROUPS, step, tail=1)

            @block.scalar
            def _(act):
                def step(u, p):
                    g = 2 * u + p
                    if live(g, GROUPS):
                        act.wait_ge(xT_made, g + 1)
                        nc.scalar.copy(xT[:, p], ps_xT[:, :, :]).then_inc(xT_ready, 1)
                    if live(g - 1, GROUPS):
                        hu, q = back(u, p)
                        for i, (w, m) in enumerate(units):
                            act.wait_ge(qk_made, 4 * (g - 1) + i + 1)
                            if i == 0:
                                if some(32 * hu):
                                    act.wait_ge(stored[q], 32 * hu)
                            nc.scalar.activation(parts[:, q, w, m, 0, :], ps_qk[:, w, m, :], ACT.Copy,
                                                 scale=scales[w]).then_inc(part1_ready, 1)
                        if some(g):
                            act.wait_ge(v_made, g)
                        nc.scalar.copy(V[:, bass.ds(GT * (g - 1), GT), :, 0:HD],
                                       ps_v[:, :, :].rearrange("p t (h d) -> p t h d", d=HD)).then_inc(v_ready, 1)
                        for i, (w, m) in enumerate(units):
                            act.wait_ge(rest_ready, 4 * (g - 1) + i + 1)
                            nc.scalar.copy(parts[:, q, w, m, 1, :], rest[:, w, m, :]).then_inc(part2_ready, 1)

                steps(act, GROUPS, step, tail=1)

            @block.gpsimd
            def _(pool):
                nc.gpsimd.memset(V[:, :, :, HD:], 1.0)

                def step(u, p):
                    g = 2 * u + p
                    for i, (w, m) in enumerate(units):
                        pool.wait_ge(part2_ready, 4 * g + i + 1)
                        nc.gpsimd.tensor_tensor(parts[:, p, w, m, 2, :], rest[:, w, m, :],
                                                parts[:, p, w, m, 1, :], ALU.subtract).then_inc(part3_ready, 1)

                steps(pool, GROUPS, step)

            @block.tensor
            def _(pe):
                def step(u, p):
                    g = 2 * u + p
                    if live(g, GROUPS):
                        pe.wait_ge(xn_ready, g + 1)
                        if some(g):
                            pe.wait_ge(xT_ready, g)
                        for j in range(GT):
                            for k in range(KD):
                                last = nc.tensor.transpose(ps_xT[:, k, j * P:(j + 1) * P],
                                                           xn[:, p, j, k * P:(k + 1) * P], ident)
                        last.then_inc(xT_made, 1)
                    if live(g - 1, GROUPS):
                        h, q = g - 1, 1 - p
                        pe.wait_ge(xT_ready, h + 1)
                        for i, (w, m) in enumerate(units):
                            if some(4 * (h - 1) + i + 1):
                                pe.wait_ge(rest_ready, 4 * (h - 1) + i + 1)
                            for k in range(KD):
                                last = nc.tensor.matmul(ps_qk[:, w, m, :], (wq, wk)[w][:, k, m * P:(m + 1) * P],
                                                        xT[:, q, k, :], start=(k == 0), stop=(k == KD - 1))
                            last.then_inc(qk_made, 1)
                        if some(h):
                            pe.wait_ge(v_ready, h)
                        for j in range(GT):
                            for k in range(KD):
                                last = nc.tensor.matmul(ps_v[:, j, :], xT[:, q, k, j * P:(j + 1) * P],
                                                        wv[:, k, :], start=(k == 0), stop=(k == KD - 1))
                        last.then_inc(v_made, 1)

                steps(pe, GROUPS, step, tail=1)

            @block.sync
            def _(sp):
                def step(u, p):
                    g = 2 * u + p
                    sp.wait_ge(part3_ready, 4 * (g + 1))
                    for w in range(2):
                        sp.dma_start(parts_dram[w, bass.ds(g, 1)].rearrange("o m p c t -> p (o m) c t"),
                                     parts[:, p, w]).then_inc(stored[p], 16)

                steps(sp, GROUPS, step)
                for p in range(2):
                    sp.wait_ge(stored[p], 32 * (GROUPS // 2))


SCORE_UNITS = [(qb, kt) for qb in range(QBLOCKS) for kt in range(GT * (qb + 1))]
S_BANKS, W_BUFS = 6, 8


def attend(nc, sem, V, parts_dram, diag, ident, heads_out):
    items = BATCH * HGROUPS
    units = len(SCORE_UNITS)
    last_of = {qb: max(k for k, (b, _) in enumerate(SCORE_UNITS) if b == qb) for qb in range(QBLOCKS)}
    with ExitStack() as mem:
        def sb(n, shape, dt=F32):
            return mem.enter_context(nc.sbuf_tensor("at_" + n, shape, dt))

        Q = [sb(f"Q{p}", [STACK, GH, SEQ], BF16) for p in range(2)]
        K = [sb(f"K{p}", [STACK, GH, SEQ], BF16) for p in range(2)]
        v = [sb(f"v{p}", [P, KTILES, GH * 2 * HD]) for p in range(2)]
        w = [sb(f"w{n}", [P, GTOK]) for n in range(W_BUFS)]
        o, rec = sb("o", [P, GTOK]), sb("rec", [P, GT * GH])
        ps_s = [mem.enter_context(nc.psum_tensor(f"at_s{n}", [P, GTOK], F32)) for n in range(S_BANKS)]
        ps_o = [mem.enter_context(nc.psum_tensor(f"at_o{n}", [P, GTOK], F32)) for n in range(QBLOCKS)]
        qk_loaded = [sem(f"at_qk_loaded{p}") for p in range(2)]
        v_ready, s_made, pv_done = sem("at_v_ready"), sem("at_s_made"), sem("at_pv_done")
        w_ready = [sem("at_w_even_ready"), sem("at_w_odd_ready")]
        o_copied, oT_made, normed, rec_chain = sem("at_o_copied"), sem("at_oT_made"), sem("at_normed"), sem("at_rec_chain")
        tri, big = diag

        def span(k):
            qb, kt = SCORE_UNITS[k]
            return max(0, kt * P - qb * GTOK)

        def evacuate(eng, it, k, j, write):
            n = GH * k + j
            if some(units * it + k - 1):
                eng.wait_ge(pv_done, units * it + k - 1)
            eng.wait_ge(s_made, GH * units * it + n + 1)
            c = span(k)
            write(w[n % W_BUFS][:, c:], ps_s[n % S_BANKS][:, c:]).then_inc(w_ready[j % 2], 1)

        with nc.Block() as block:
            @block.sync
            def _(sp):
                def step(u, p):
                    it = 2 * u + p
                    if some(GH * units * (it - 1)):
                        sp.wait_ge(s_made, GH * units * (it - 1))
                    for dst, which, rows in ((Q, 0, Q_ROWS), (K, 1, K_ROWS)):
                        for r, part in enumerate(rows):
                            for qb in range(QBLOCKS):
                                src = parts_dram[which, bass.ds((it // HGROUPS) * QBLOCKS + qb, 1),
                                                 bass.ds((it % HGROUPS) // 2, 1), bass.ds((it % 2) * 64, 64), part, :]
                                sp.dma_start(dst[p][r * HD:(r + 1) * HD, :, qb * GTOK:(qb + 1) * GTOK],
                                             src.rearrange("a b (h d) t -> (a b d) h t", d=HD)).then_inc(qk_loaded[p], 16)

                steps(sp, items, step)

            @block.gpsimd
            def _(pool):
                def step(u, p):
                    it = 2 * u + p
                    if some(units * (it - 1)):
                        pool.wait_ge(pv_done, units * (it - 1))
                    src = V[:, bass.ds((it // HGROUPS) * KTILES, KTILES), bass.ds((it % HGROUPS) * GH, GH), :]
                    nc.gpsimd.tensor_copy(v[p][:, :, :].rearrange("p t (h d) -> p t h d", h=GH), src).then_inc(v_ready, 1)

                steps(pool, items, step)

            @block.scalar
            def _(act):
                def copy_out(it, qb):
                    act.wait_ge(pv_done, units * it + last_of[qb] + 1)
                    if some(QBLOCKS * it + qb):
                        act.wait_ge(oT_made, QBLOCKS * it + qb)
                    nc.scalar.copy(o[:, :], ps_o[qb][:, :]).then_inc(o_copied, 1)

                def step(u, p):
                    it = 2 * u + p
                    for k in range(units):
                        if live(it, items):
                            for j in (0, 2):
                                evacuate(act, it, k, j, lambda out, s: nc.scalar.activation(
                                    out, s, ACT.Relu, bias=threshold_col))
                        if k == 0 and live(it - 1, items):
                            copy_out(it - 1, 1)
                        if k == 4 and live(it, items):
                            copy_out(it, 0)

                threshold_col = tri[1]
                steps(act, items, step, tail=1)

            @block.vector
            def _(dve):
                chain = Chain(dve, rec_chain, 2 * QBLOCKS)

                def norm_heads(it, qb, n):
                    dve.wait_ge(oT_made, QBLOCKS * it + qb + 1)
                    oT = ps_o[qb][:, :].rearrange("p (t h c) -> p t h c", t=GT, h=GH)
                    chain.base, chain.done = 2 * (QBLOCKS * it + qb), 0
                    recs = rec[:, :].rearrange("p (t h) -> p t h", t=GT)
                    chain.link(nc.vector.tensor_scalar(recs, oT[:, :, :, HD], DEN_EPS, None, ALU.add))
                    chain.link(nc.vector.reciprocal(recs, recs))
                    out = heads_out[:, bass.ds((it // HGROUPS) * QBLOCKS + qb, 1), bass.ds(it % HGROUPS, 1)]
                    nc.vector.tensor_tensor(out.rearrange("p a b (t h) d -> p (a b t) h d", h=GH), oT[:, :, :, 0:HD],
                                            recs.unsqueeze(3).to_broadcast([P, GT, GH, HD]),
                                            ALU.mult).then_inc(normed, 1)

                def step(u, p):
                    it = 2 * u + p
                    for k in range(units):
                        if live(it, items):
                            for j in (1, 3):
                                evacuate(dve, it, k, j, lambda out, s: nc.vector.tensor_scalar(
                                    out, s, -THRESHOLD, 0.0, ALU.add, ALU.max))
                        if k == 2 and live(it - 1, items):
                            norm_heads(it - 1, 1, k)
                        if k == 6 and live(it, items):
                            norm_heads(it, 0, k)

                steps(dve, items, step, tail=1)

            @block.tensor
            def _(pe):
                def score(it, p, k, j):
                    qb, kt = SCORE_UNITS[k]
                    n, c = GH * k + j, span(k)
                    before = n - S_BANKS
                    if some(2 * units * it + before // 2 + 1):
                        pe.wait_ge(w_ready[j % 2], 2 * units * it + before // 2 + 1)
                    s = ps_s[n % S_BANKS]
                    diagonal = kt >= GT * qb
                    last = nc.tensor.matmul(s[:, c:], K[p][:, j, kt * P:(kt + 1) * P],
                                            Q[p][:, j, qb * GTOK + c:(qb + 1) * GTOK],
                                            start=True, stop=not diagonal, skip_group_check=True)
                    if diagonal:
                        last = nc.tensor.matmul(s[:, c:c + P], big, tri[0], start=False, stop=True,
                                                skip_group_check=True)
                    last.then_inc(s_made, 1)

                def weigh(it, p, k):
                    qb, kt = SCORE_UNITS[k]
                    c = span(k)
                    if k == 0:
                        pe.wait_ge(v_ready, it + 1)
                    if kt == 0:
                        if some(QBLOCKS * (it - 1) + qb + 1):
                            pe.wait_ge(normed, QBLOCKS * (it - 1) + qb + 1)
                    for j in range(GH):
                        n = GH * k + j
                        pe.wait_ge(w_ready[j % 2], 2 * units * it + n // 2 + 1)
                        last = nc.tensor.matmul(ps_o[qb][32 * j:32 * (j + 1), c:],
                                                v[p][:, kt, j * 2 * HD:(j + 1) * 2 * HD], w[n % W_BUFS][:, c:],
                                                start=(kt == 0), stop=(k == last_of[qb]), skip_group_check=True)
                    last.then_inc(pv_done, 1)

                def transpose_out(it, qb):
                    pe.wait_ge(o_copied, QBLOCKS * it + qb + 1)
                    for t in range(GT):
                        last = nc.tensor.transpose(ps_o[qb][:, t * P:(t + 1) * P], o[:, t * P:(t + 1) * P], ident)
                    last.then_inc(oT_made, 1)

                def step(u, p):
                    it = 2 * u + p
                    for k in range(units):
                        if live(it, items):
                            if k == 0:
                                pe.wait_ge(qk_loaded[p], 16 * 2 * len(Q_ROWS) * QBLOCKS * (u + 1))
                            for j in range(GH):
                                score(it, p, k, j)
                        if k == 1 and live(it - 1, items):
                            transpose_out(it - 1, 1)
                        if k == 5 and live(it, items):
                            transpose_out(it, 0)
                        if k == 0 and live(it - 1, items):
                            weigh(it - 1, 1 - p, units - 1)
                        if k > 0 and live(it, items):
                            weigh(it, p, k - 1)

                steps(pe, items, step, tail=1)


def project_out(nc, sem, X, norm, wo, ident, heads_out):
    with ExitStack() as mem:
        aT = mem.enter_context(nc.sbuf_tensor("po_aT", [P, 2, KD, GTOK], F32))
        a = mem.enter_context(nc.sbuf_tensor("po_a", [P, 2, GT, DIM], F32))
        ps_aT = mem.enter_context(nc.psum_tensor("po_ps_aT", [P, KD, GTOK], F32))
        ps_y = [mem.enter_context(nc.psum_tensor(f"po_ps_y{p}", [P, GT, DIM], F32)) for p in range(2)]
        a_ready, aT_made, aT_ready, y_made, added = (sem("po_" + n) for n in ("a_ready", "aT_made", "aT_ready", "y_made", "added"))
        with nc.Block() as block:
            @block.gpsimd
            def _(pool):
                def step(u, p):
                    g = 2 * u + p
                    if some(g - 1):
                        pool.wait_ge(aT_made, g - 1)
                    for hg in range(HGROUPS):
                        last = nc.gpsimd.tensor_copy(
                            a[:, p, :, hg * GH * HD:(hg + 1) * GH * HD],
                            heads_out[:, bass.ds(g, 1), hg].rearrange("p a (t h) d -> p (a t) (h d)", h=GH))
                    last.then_inc(a_ready, 1)

                steps(pool, GROUPS, step)

            @block.scalar
            def _(act):
                def step(u, p):
                    act.wait_ge(aT_made, 2 * u + p + 1)
                    nc.scalar.copy(aT[:, p], ps_aT[:, :, :]).then_inc(aT_ready, 1)

                steps(act, GROUPS, step)

            @block.tensor
            def _(pe):
                def step(u, p):
                    g = 2 * u + p
                    if live(g, GROUPS):
                        pe.wait_ge(a_ready, g + 1)
                        if some(g):
                            pe.wait_ge(aT_ready, g)
                        for j in range(GT):
                            for k in range(KD):
                                last = nc.tensor.transpose(ps_aT[:, k, j * P:(j + 1) * P],
                                                           a[:, p, j, k * P:(k + 1) * P], ident)
                        last.then_inc(aT_made, 1)
                    if live(g - 1, GROUPS):
                        h, q = g - 1, 1 - p
                        pe.wait_ge(aT_ready, h + 1)
                        if some(h - 1):
                            pe.wait_ge(added, h - 1)
                        for j in range(GT):
                            for k in range(KD):
                                last = nc.tensor.matmul(ps_y[q][:, j, :], aT[:, q, k, j * P:(j + 1) * P], wo[:, k, :],
                                                        start=(k == 0), stop=(k == KD - 1))
                        last.then_inc(y_made, 1)

                steps(pe, GROUPS, step, tail=1)

            @block.vector
            def _(dve):
                def step(u, p):
                    g = 2 * u + p
                    dve.wait_ge(y_made, g + 1)
                    x4 = X[:, bass.ds(GT * g, GT), :]
                    nc.vector.tensor_tensor(x4, x4, ps_y[p][:, :, :], ALU.add).then_inc(added, 1)
                    dve.wait_ge(added, g + 1)
                    norm.statistics(x4, g)

                steps(dve, GROUPS, step)


def attention(nc, sem, X, norm, wq, wk, wv, wo, ident, inp):
    parts_dram = nc.dram_tensor("parts", [2, GROUPS, KD, P, PARTS, GTOK], BF16).ap()
    with ExitStack() as mem:
        heads_out = mem.enter_context(nc.sbuf_tensor(
            "heads_out", [P, BATCH * QBLOCKS, HGROUPS, GT * GH, HD], F32))
        with ExitStack() as inner:
            V = inner.enter_context(nc.sbuf_tensor("V", [P, TILES, HEADS, 2 * HD], F32))
            big = inner.enter_context(nc.sbuf_tensor("big", [P, P], BF16))
            tri = inner.enter_context(nc.sbuf_tensor("tri", [P, P], BF16))
            threshold = inner.enter_context(nc.sbuf_tensor("threshold", [P, 1], F32))
            make_mask(nc, sem, big, tri, threshold)
            project(nc, sem, X, norm, (wq, wk, wv), ident, V, parts_dram)
            attend(nc, sem, V, parts_dram, ((tri[:, :], threshold[:, 0:1]), big[:, :]), ident, heads_out)
        project_out(nc, sem, X, norm, wo, ident, heads_out)


def make_mask(nc, sem, big, tri, threshold):
    cleared = sem("mask_cleared")
    with nc.Block() as block:
        @block.gpsimd
        def _(pool):
            nc.gpsimd.memset(threshold[:, :], -THRESHOLD)
            nc.gpsimd.memset(big[:, :], 0.0)
            nc.gpsimd.memset(tri[:, :], 1.0).then_inc(cleared, 1)
            pool.wait_ge(cleared, 1)
            nc.gpsimd.affine_select(out=big[:, :], in_=big[:, :], compare_op=ALU.not_equal, fill=-1e30,
                                    base=0, pattern=[[-1, P]], channel_multiplier=1)
            nc.gpsimd.affine_select(out=tri[:, :], in_=tri[:, :], compare_op=ALU.is_gt, fill=0.0,
                                    base=0, pattern=[[-1, P]], channel_multiplier=1)


EXPERTS, TOP_K = 16, 4
HID = 176
HK = (P, HID - P)
SLOT_TILES = -(-(TOKENS * TOP_K + EXPERTS * (P - 1)) // P // 4) * 4
SLOTS = SLOT_TILES * P
WAYS = 4


def split_weights(nc, sem, name, jobs):
    piece = 1408
    pieces = [(d[:, c:min(c + piece, d.shape[1])], h[:, c:min(c + piece, d.shape[1])], l[:, c:min(c + piece, d.shape[1])])
              for d, h, l in jobs for c in range(0, d.shape[1], piece)]
    with ExitStack() as mem:
        raw = [mem.enter_context(nc.sbuf_tensor(f"{name}_raw{n}", [P, piece], F32)) for n in range(2)]
        loaded = [sem(f"{name}_raw_loaded{n}") for n in range(2)]
        high_ready, low_ready = sem(name + "_high_ready"), sem(name + "_low_ready")
        with nc.Block() as block:
            @block.sync
            def _(sp):
                for n, (d, _, _) in enumerate(pieces):
                    if some(n - 1):
                        sp.wait_ge(low_ready, n - 1)
                    sp.dma_start(raw[n % 2][0:d.shape[0], 0:d.shape[1]], d).then_inc(loaded[n % 2], 16)

            @block.scalar
            def _(act):
                for n, (d, h, _) in enumerate(pieces):
                    act.wait_ge(loaded[n % 2], 16 * (n // 2 + 1))
                    nc.scalar.copy(h, raw[n % 2][0:d.shape[0], 0:d.shape[1]]).then_inc(high_ready, 1)

            @block.vector
            def _(dve):
                for n, (d, h, l) in enumerate(pieces):
                    dve.wait_ge(high_ready, n + 1)
                    nc.vector.tensor_tensor(l, raw[n % 2][0:d.shape[0], 0:d.shape[1]], h.bitcast(F32),
                                            ALU.subtract).then_inc(low_ready, 1)


def expert_tiles(nc, sem, name, count, w13, w2, ident, source, shared=None, routed=None):
    cols = w13[0].shape[-1]
    with ExitStack() as mem:
        def sb(n, shape, dt=F32):
            return mem.enter_context(nc.sbuf_tensor(f"{name}_{n}", shape, dt))

        rows = [sb(f"rows{p}", [P, DIM]) for p in range(WAYS)]
        xT_hi, xT_lo = ([sb(f"xT_{n}{p}", [P, KD, P], F32R) for p in range(2)] for n in ("hi", "lo"))
        first, hid_in = sb("first", [P, HID]), sb("hid_in", [P, HID])
        hid = [sb(f"hid{p}", [P, 2 * P]) for p in range(2)]
        hT_hi, hT_lo = ([sb(f"hT_{n}{p}", [P, 2, P], F32R) for p in range(2)] for n in ("hi", "lo"))
        y = [sb(f"y{p}", [P, DIM]) for p in range(2)] if routed else None

        def ps(n):
            return [mem.enter_context(nc.psum_tensor(f"{name}_ps_{n}{p}", [P, 512], F32)) for p in range(2)]

        ps_x, ps_h, ps_t, ps_y = ps("x"), ps("h"), ps("t"), ps("y")
        names = ("zeroed", "rows_ready", "xT_hi_ready", "xT_lo_ready", "h_made", "first_ready", "prod_ready",
                 "hid_ready", "h_turned", "hT_hi_ready", "hT_lo_ready", "y_made", "y_ready")
        (zeroed, rows_ready, xT_hi_ready, xT_lo_ready, h_made, first_ready, prod_ready,
         hid_ready, h_turned, hT_hi_ready, hT_lo_ready, y_made, y_ready) = (sem(f"{name}_{n}") for n in names)
        x_turned = [sem(f"{name}_x_turned{p}") for p in range(WAYS)]
        rows_loaded = [sem(f"{name}_rows_loaded{p}") for p in range(WAYS)]
        copied = [sem(f"{name}_column_copied{p}") for p in range(WAYS)]
        first_copied = sem(name + "_first_columns_copied")
        stored = [sem(f"{name}_stored{p}") for p in range(2)]

        def run(eng, step, tail=0):
            steps(eng, count, step, tail, WAYS)

        def parts(act_like, hi, ps_in):
            return act_like(hi, ps_in)

        with nc.Block() as block:
            @block.scalar
            def _(act):
                def step(u, p):
                    i = WAYS * u + p
                    if live(i, count):
                        if some(i - 1):
                            act.wait_ge(h_made, i - 1)
                        act.wait_ge(x_turned[p], u + 1)
                        nc.scalar.copy(xT_hi[p % 2][:, :, :], ps_x[p % 2][:, 0:DIM].rearrange("p (k t) -> p k t", k=KD)
                                       ).then_inc(xT_hi_ready, 1)
                    if live(i - 1, count):
                        q = (p - 1) % 2
                        if some(i - 1):
                            act.wait_ge(prod_ready, i - 1)
                        if some(i):
                            act.wait_ge(h_made, i)
                        nc.scalar.activation(first[:, :], ps_h[q][:, 0:HID], ACT.Silu if shared else ACT.Copy
                                             ).then_inc(first_ready, 1)
                    if live(i - 2, count):
                        q = (p - 2) % 2
                        if some(i - 3):
                            act.wait_ge(y_made, i - 3)
                        if some(i - 1):
                            act.wait_ge(h_turned, i - 1)
                        nc.scalar.copy(hT_hi[q][:, :, :], ps_t[q][:, 0:2 * P].rearrange("p (k t) -> p k t", k=2)
                                       ).then_inc(hT_hi_ready, 1)
                    if routed and live(i - 1, count):
                        q = (p - 1) % 2
                        if some(i):
                            act.wait_ge(prod_ready, i)
                        if some(i - 2):
                            act.wait_ge(h_turned, i - 2)
                        if isinstance(i, int) and i - 1 < 2:
                            act.wait_ge(zeroed, 1)
                        nc.scalar.activation(hid[q][:, 0:HID], hid_in[:, :], ACT.Silu).then_inc(hid_ready, 1)

                run(act, step, 3)

            @block.vector
            def _(dve):
                for p in range(2):
                    last = nc.vector.memset(hid[p][:, HID:], 0.0)
                last.then_inc(zeroed, 1)

                def step(u, p):
                    i = WAYS * u + p
                    if shared and live(i, count):
                        if some(u):
                            dve.wait_ge(x_turned[p], u)
                        if some(16 * u):
                            dve.wait_ge(rows_loaded[p], 16 * u)
                        shared["norm"].apply_tile(shared["X"], rows[p][:, :], i).then_inc(rows_ready, 1)
                    if live(i - 1, count) or live(i, count):
                        pass
                    if live(i - lead, count):
                        n, q = i - lead, (p - lead) % 2
                        dve.wait_ge(xT_hi_ready, n + 1)
                        nc.vector.tensor_tensor(xT_lo[q][:, :, :], ps_x[q][:, 0:DIM].rearrange("p (k t) -> p k t", k=KD),
                                                xT_hi[q][:, :, :].bitcast(F32), ALU.subtract).then_inc(xT_lo_ready, 1)
                    if live(i - lead - 1, count):
                        n, q = i - lead - 1, (p - lead - 1) % 2
                        dve.wait_ge(first_ready, n + 1)
                        if routed:
                            if some(n):
                                dve.wait_ge(hid_ready, n)
                            out = hid_in[:, :]
                        else:
                            if some(n - 1):
                                dve.wait_ge(h_turned, n - 1)
                            out = hid[q][:, 0:HID]
                            nc.vector.tensor_copy(shared["logits"][:, bass.ds(n, 1), :].rearrange("p a e -> p (a e)"),
                                                  ps_h[q][:, 2 * HID:cols])
                        nc.vector.tensor_tensor(out, first[:, :], ps_h[q][:, HID:2 * HID], ALU.mult).then_inc(prod_ready, 1)
                    if live(i - lead - 2, count):
                        n, q = i - lead - 2, (p - lead - 2) % 2
                        dve.wait_ge(hT_hi_ready, n + 1)
                        nc.vector.tensor_tensor(hT_lo[q][:, :, :], ps_t[q][:, 0:2 * P].rearrange("p (k t) -> p k t", k=2),
                                                hT_hi[q][:, :, :].bitcast(F32), ALU.subtract).then_inc(hT_lo_ready, 1)
                    if live(i - lead - 3, count):
                        n, q = i - lead - 3, (p - lead - 3) % 2
                        dve.wait_ge(y_made, n + 1)
                        if routed:
                            un, qn = back_by(u, p, lead + 3)
                            if some(16 * stores_before(un, qn)):
                                dve.wait_ge(stored[q], 16 * stores_before(un, qn))
                            nc.vector.tensor_copy(y[q][:, :], ps_y[q][:, 0:DIM]).then_inc(y_ready, 1)
                        else:
                            xt = shared["X"][:, bass.ds(n, 1), :].rearrange("p a d -> p (a d)")
                            nc.vector.tensor_tensor(xt, xt, ps_y[q][:, 0:DIM], ALU.add).then_inc(y_ready, 1)

                lead = 1 if shared else 0
                run(dve, step, 3 + lead)

            @block.tensor
            def _(pe):
                def step(u, p):
                    i = WAYS * u + p
                    if live(i, count):
                        if routed:
                            pe.wait_ge(rows_loaded[p], 16 * (u + 1))
                        else:
                            pe.wait_ge(rows_ready, i + 1)
                        if some(i - 1):
                            pe.wait_ge(xT_lo_ready, i - 1)
                        for k in range(KD):
                            last = nc.tensor.transpose(ps_x[p % 2][:, k * P:(k + 1) * P], rows[p][:, k * P:(k + 1) * P], ident)
                        last.then_inc(x_turned[p], 1)
                    if live(i - 1, count):
                        n, q = i - 1, (p - 1) % 2
                        expert = routed["expert"](pe, n) if routed else None
                        pe.wait_ge(xT_lo_ready, n + 1)
                        if some(n - 1):
                            pe.wait_ge(prod_ready, n - 1)
                        terms = [(a, b, k) for k in range(KD) for a, b in ((xT_hi, 0), (xT_lo, 0), (xT_hi, 1))]
                        for m, (a, b, k) in enumerate(terms):
                            last = nc.tensor.matmul(ps_h[q][:, 0:cols], a[q][:, k, :], w13_of(b, k, expert),
                                                    start=(m == 0), stop=(m == len(terms) - 1))
                        last.then_inc(h_made, 1)
                    if live(i - 2, count):
                        n, q = i - 2, (p - 2) % 2
                        if routed:
                            pe.wait_ge(hid_ready, n + 1)
                        else:
                            pe.wait_ge(prod_ready, n + 1)
                            if isinstance(n, int) and n < 2:
                                pe.wait_ge(zeroed, 1)
                        if some(n - 1):
                            pe.wait_ge(hT_lo_ready, n - 1)
                        for k in range(2):
                            last = nc.tensor.transpose(ps_t[q][:, k * P:(k + 1) * P], hid[q][:, k * P:(k + 1) * P], ident)
                        last.then_inc(h_turned, 1)
                    if live(i - 3, count):
                        n, q = i - 3, (p - 3) % 2
                        expert = routed["expert"](pe, n) if routed else None
                        pe.wait_ge(hT_lo_ready, n + 1)
                        if some(n - 1):
                            pe.wait_ge(y_ready, n - 1)
                        terms = [(a, b, k) for k in range(2) for a, b in ((hT_hi, 0), (hT_lo, 0), (hT_hi, 1))]
                        for m, (a, b, k) in enumerate(terms):
                            last = nc.tensor.matmul(ps_y[q][:, 0:DIM], a[q][0:HK[k], k, :], w2_of(b, k, expert),
                                                    start=(m == 0), stop=(m == len(terms) - 1))
                        last.then_inc(y_made, 1)

                def w13_of(part, k, expert):
                    if expert is None:
                        return w13[part][:, k, :]
                    return w13[part][:, k, bass.ds(expert, 1), :].rearrange("p a n -> p (a n)")

                def w2_of(part, k, expert):
                    if expert is None:
                        return w2[part][0:HK[k], k, :]
                    return w2[part][0:HK[k], k, bass.ds(expert, 1), :].rearrange("p a n -> p (a n)")

                run(pe, step, 3)

            if shared:
                @block.sync
                def _(sp):
                    def step(u, p):
                        i = WAYS * u + p
                        sp.wait_ge(rows_ready, i + 1)
                        sp.dma_start(source[bass.ds(i * P, P), :], rows[p][:, :]).then_inc(rows_loaded[p], 16)

                    run(sp, step)
                    for p in range(WAYS):
                        sp.wait_ge(rows_loaded[p], 16 * (count // WAYS))

            if routed:
                @block.gpsimd
                def _(pool):
                    column = routed["column"]

                    def step(u, p):
                        i = WAYS * u + p
                        if some(u):
                            pool.wait_ge(x_turned[p], 1)
                            pool.wait_ge(x_turned[p], u)
                        copy = nc.gpsimd.tensor_copy(column[p][:, :], routed["tokens"][:, bass.ds(i, 1)])
                        if isinstance(u, int):
                            copy.then_inc(first_copied, 1)
                            pool.wait_ge(first_copied, p + 1)
                        else:
                            copy.then_inc(copied[p], 1)
                            if some(u):
                                pool.wait_ge(copied[p], 1)
                                pool.wait_ge(copied[p], u)
                        nc.gpsimd.indirect_dma_start(
                            out=rows[p][:, :], out_offset=None, in_=source[:, :],
                            in_offset=bass.IndirectOffsetOnAxis(ap=column[p][:, 0:1], axis=0)).then_inc(rows_loaded[p], 16)

                    run(pool, step)

                @block.sync
                def _(sp):
                    def step(u, p):
                        i = WAYS * u + p
                        sp.wait_ge(y_ready, i + 1)
                        sp.dma_start(routed["out"][bass.ds(i * P, P), :], y[p % 2][:, :]).then_inc(stored[p % 2], 16)

                    run(sp, step)
                    for p in range(2):
                        sp.wait_ge(stored[p], 16 * (count // 2))


def back_by(u, p, n):
    return u + (p - n) // WAYS, (p - n) % WAYS


def stores_before(u, p):
    return (WAYS // 2) * u + p // 2


def route(nc, sem, name, logits, gate_b, ident, tables, slots, shares, tokens, tile_expert):
    iota16, later, iota_slot, token_no, not_first = tables
    TE = TILES * EXPERTS
    with ExitStack() as mem:
        def sb(n, shape, dt=F32):
            return mem.enter_context(nc.sbuf_tensor(f"{name}_{n}", shape, dt))

        top, idx = sb("top", [P, TILES, 8]), sb("idx", [P, TILES, 8], U32)
        scores = sb("scores", [P, TILES, EXPERTS])
        idxf, total, inv = sb("idxf", [P, TOP_K, TILES]), sb("total", [P, TILES]), sb("inv", [P, TILES])
        onehot = sb("onehot", [P, TOP_K, TILES, EXPERTS])
        mask, mask16 = sb("mask", [P, TILES, EXPERTS]), sb("mask16", [P, TILES, EXPERTS], BF16)
        ones, later16 = sb("ones", [P, P], BF16), sb("later16", [P, P], BF16)
        totals, cum = sb("totals", [P, EXPERTS, TILES]), sb("cum", [P, EXPERTS, TILES])
        counts, counts_i = sb("counts", [P, EXPERTS]), sb("counts_i", [P, EXPERTS], I32)
        n_tiles, start, unit = sb("n_tiles", [P, EXPERTS]), sb("start", [P, EXPERTS]), sb("unit", [P, EXPERTS])
        slot = sb("slot", [P, TILES, EXPERTS])
        slotf, part_i = sb("slotf", [P, TOP_K, TILES]), sb("part_i", [P, TOP_K, TILES], I32)
        slot_i = sb("slot_i", [P, TOP_K, TILES], I32)
        low, high = sb("low", [P, TOP_K, TILES]), sb("high", [P, TOP_K, TILES])
        reached, tile_e = sb("reached", [P, SLOT_TILES, EXPERTS - 1]), sb("tile_e", [P, SLOT_TILES])
        ps_before = mem.enter_context(nc.psum_tensor(name + "_ps_before", [P, TE], F32))
        ps_total = mem.enter_context(nc.psum_tensor(name + "_ps_total", [P, TE], F32))
        links, logits_ready, mask_ready, counted = (sem(f"{name}_{n}") for n in ("links", "sig_ready", "mask_ready", "counted"))
        vec = nc.vector
        with nc.Block() as block:
            @block.scalar
            def _(act):
                nc.scalar.activation(scores[:, :, :], logits, ACT.Sigmoid).then_inc(logits_ready, 1)

            @block.tensor
            def _(pe):
                pe.wait_ge(mask_ready, 1)
                m = mask16[:, :, :].rearrange("p t e -> p (t e)")
                nc.tensor.matmul(ps_before[:, :], later16[:, :], m, start=True, stop=True)
                nc.tensor.matmul(ps_total[:, :], ones[:, :], m, start=True, stop=True).then_inc(counted, 1)

            @block.vector
            def _(dve):
                c = Chain(dve, links, 64)
                c.item(0)
                vec.memset(ones[:, :], 1.0)
                vec.tensor_copy(later16[:, :], later)
                vec.memset(unit[:, :], 1.0)
                dve.wait_ge(logits_ready, 1)
                c.link(vec.tensor_tensor(scores[:, :, :], scores[:, :, :],
                                         gate_b.unsqueeze(1).to_broadcast([P, TILES, EXPERTS]), ALU.add))
                for t in range(TILES):
                    last = vec.max(top[:, t, :], scores[:, t, :])
                c.link(last)
                for t in range(TILES):
                    last = vec.max_index(idx[:, t, :], top[:, t, :], scores[:, t, :])
                c.link(last)
                vec.tensor_reduce(total[:, :], top[:, :, 0:TOP_K], AX.X, ALU.add)
                c.link(vec.tensor_copy(idxf[:, :, :], idx[:, :, 0:TOP_K].rearrange("p t k -> p k t")))
                vec.tensor_scalar(total[:, :], total[:, :], 2.0, None, ALU.mult)
                for k in range(TOP_K):
                    last = vec.tensor_tensor(onehot[:, k], iota16,
                                             idxf[:, k, :].unsqueeze(2).to_broadcast([P, TILES, EXPERTS]), ALU.is_equal)
                c.link(last)
                vec.reciprocal(inv[:, :], total[:, :])
                vec.tensor_tensor(mask[:, :, :], onehot[:, 0], onehot[:, 1], ALU.add)
                c.link(vec.tensor_tensor(slot[:, :, :], onehot[:, 2], onehot[:, 3], ALU.add))
                vec.tensor_tensor(mask16[:, :, :], mask[:, :, :], slot[:, :, :], ALU.add).then_inc(mask_ready, 1)
                c.link(vec.tensor_tensor(shares, top[:, :, 0:TOP_K],
                                         inv[:, :].unsqueeze(2).to_broadcast([P, TILES, TOP_K]), ALU.mult))
                dve.wait_ge(counted, 1)
                c.link(vec.tensor_copy(totals[:, :, :], ps_total[:, :].rearrange("p (t e) -> p e t", t=TILES)))
                c.link(vec.tensor_tensor_scan(cum[:, :, :].rearrange("p e t -> p (e t)"), not_first,
                                              totals[:, :, :].rearrange("p e t -> p (e t)"), 0.0, ALU.mult, ALU.add))
                c.link(vec.tensor_scalar(counts_i[:, :], cum[:, :, TILES - 1], float(P - 1), None, ALU.add))
                c.link(vec.tensor_scalar(counts_i[:, :], counts_i[:, :], 7, None, ALU.arith_shift_right))
                c.link(vec.tensor_copy(n_tiles[:, :], counts_i[:, :]))
                c.link(vec.tensor_tensor_scan(start[:, :], unit[:, :], n_tiles[:, :], 0.0, ALU.mult, ALU.add))
                c.link(vec.tensor_tensor(start[:, :], start[:, :], n_tiles[:, :], ALU.subtract))
                vec.tensor_scalar(counts[:, :], start[:, :], float(P), None, ALU.mult)
                vec.tensor_tensor(reached[:, :, :], iota_slot.unsqueeze(2).to_broadcast([P, SLOT_TILES, EXPERTS - 1]),
                                  start[:, 1:].unsqueeze(1).to_broadcast([P, SLOT_TILES, EXPERTS - 1]), ALU.is_ge)
                c.link(vec.tensor_tensor(cum[:, :, :], cum[:, :, :], totals[:, :, :], ALU.subtract))
                vec.tensor_reduce(tile_e[:, :], reached[:, :, :], AX.X, ALU.add)
                c.link(vec.tensor_tensor(cum[:, :, :], cum[:, :, :],
                                         counts[:, :].unsqueeze(2).to_broadcast([P, EXPERTS, TILES]), ALU.add))
                vec.tensor_copy(tile_expert, tile_e[:, :])
                c.link(vec.tensor_tensor(slot[:, :, :], ps_before[:, :].rearrange("p (t e) -> p t e", t=TILES),
                                         cum[:, :, :].rearrange("p e t -> p t e"), ALU.add))
                for k in range(TOP_K):
                    last = vec.tensor_tensor(onehot[:, k], onehot[:, k], slot[:, :, :], ALU.mult)
                c.link(last)
                c.link(vec.tensor_reduce(slotf[:, :, :], onehot[:, :, :, :], AX.X, ALU.add))
                vec.tensor_copy(slots, slotf[:, :, :].rearrange("p k t -> p t k"))
                c.link(vec.tensor_copy(slot_i[:, :, :], slotf[:, :, :]))
                c.link(vec.tensor_scalar(part_i[:, :, :], slot_i[:, :, :], P - 1, None, ALU.bitwise_and))
                vec.tensor_scalar(slot_i[:, :, :], slot_i[:, :, :], 7, None, ALU.arith_shift_right)
                c.link(vec.tensor_copy(low[:, :, :], part_i[:, :, :]))
                vec.tensor_copy(high[:, :, :], slot_i[:, :, :])

        at = [sb(f"at{p}", [P, TOP_K, P], F32R) for p in range(2)]
        of = [sb(f"of{p}", [P, TOP_K, SLOT_TILES], F32R) for p in range(2)]
        ps_inv = mem.enter_context(nc.psum_tensor(name + "_ps_inv", [P, SLOT_TILES], F32))
        hot_ready, hot_used = sem(name + "_hot_ready"), sem(name + "_hot_used")
        with nc.Block() as block:
            @block.vector
            def _(dve):
                def step(u, p):
                    t = 2 * u + p
                    if some(t - 1):
                        dve.wait_ge(hot_used, t - 1)
                    for k in range(TOP_K):
                        vec.tensor_scalar(at[p][:, k, :], iota_slot[:, 0:P], low[:, k, bass.ds(t, 1)], None, ALU.is_equal)
                        last = vec.tensor_scalar(of[p][:, k, :], iota_slot, high[:, k, bass.ds(t, 1)],
                                                 token_no[:, bass.ds(t, 1)], ALU.is_equal, ALU.mult)
                    last.then_inc(hot_ready, 1)

                steps(dve, TILES, step)
                dve.wait_ge(hot_used, TILES)
                vec.tensor_copy(tokens, ps_inv[:, :])

            @block.tensor
            def _(pe):
                def step(u, p):
                    t = 2 * u + p
                    pe.wait_ge(hot_ready, t + 1)
                    for k in range(TOP_K):
                        last = nc.tensor.matmul(ps_inv[:, :], at[p][:, k, :], of[p][:, k, :],
                                                start=(isinstance(t, int) and t == 0 and k == 0), stop=(k == TOP_K - 1),
                                                skip_group_check=True)
                    last.then_inc(hot_used, 1)

                steps(pe, TILES, step)


def combine(nc, sem, name, X, norm, slots, shares, y_dram):
    with ExitStack() as mem:
        rows = [mem.enter_context(nc.sbuf_tensor(f"{name}_rows{p}", [P, TOP_K, DIM], F32)) for p in range(2)]
        index = [[mem.enter_context(nc.sbuf_tensor(f"{name}_index{p}{k}", [P, 1], I32)) for k in range(TOP_K)]
                 for p in range(2)]
        loaded = [sem(f"{name}_loaded{p}") for p in range(2)]
        used, copied = ([sem(f"{name}_{n}{p}") for p in range(2)] for n in ("used", "copied"))
        first_copied, links = sem(name + "_first_copied"), sem(name + "_links")
        with nc.Block() as block:
            @block.gpsimd
            def _(pool):
                def step(u, p):
                    t = 2 * u + p
                    if some(u):
                        pool.wait_ge(used[p], 1)
                        pool.wait_ge(used[p], u)
                    for k in range(TOP_K):
                        last = nc.gpsimd.tensor_copy(index[p][k][:, :], slots[:, bass.ds(t, 1), k])
                    if isinstance(u, int):
                        last.then_inc(first_copied, 1)
                        pool.wait_ge(first_copied, p + 1)
                    else:
                        last.then_inc(copied[p], 1)
                        if some(u):
                            pool.wait_ge(copied[p], 1)
                            pool.wait_ge(copied[p], u)
                    for k in range(TOP_K):
                        nc.gpsimd.indirect_dma_start(
                            out=rows[p][:, k, :], out_offset=None, in_=y_dram[:, :],
                            in_offset=bass.IndirectOffsetOnAxis(ap=index[p][k][:, 0:1], axis=0)).then_inc(loaded[p], 16)

                steps(pool, TILES, step)

            @block.vector
            def _(dve):
                chain = Chain(dve, links, TOP_K)

                def step(u, p):
                    t = 2 * u + p
                    chain.item(t)
                    dve.wait_ge(loaded[p], 16 * TOP_K * (u + 1))
                    xt = X[:, bass.ds(t, 1), :].rearrange("p a d -> p (a d)")
                    for k in range(TOP_K):
                        last = nc.vector.scalar_tensor_tensor(out=xt, in0=rows[p][:, k, :], scalar=shares[:, bass.ds(t, 1), k],
                                                              in1=xt, op0=ALU.mult, op1=ALU.add)
                        chain.link(last)
                    nc.vector.bn_stats(norm.stats[:, bass.ds(t, 1), :], xt).then_inc(used[p], 1)

                steps(dve, TILES, step)


def moe(nc, sem, name, X, norm, ident, inp, dram):
    xhat, y_dram = dram
    with ExitStack() as mem:
        def sb(n, shape, dt=F32):
            return mem.enter_context(nc.sbuf_tensor(f"{name}_{n}", shape, dt))

        slots, shares = sb("slots", [P, TILES, TOP_K], I32), sb("shares", [P, TILES, TOP_K])
        tokens, tile_expert = sb("tokens", [P, SLOT_TILES], I32), sb("tile_expert", [P, SLOT_TILES], I32)
        column = [sb(f"column{p}", [P, 1], I32) for p in range(WAYS)]
        with ExitStack() as scratch:
            def tmp(n, shape, dt=F32):
                return scratch.enter_context(nc.sbuf_tensor(f"{name}_{n}", shape, dt))

            cols = 2 * HID + EXPERTS
            w13 = [tmp(f"ws13_{n}", [P, KD, cols], F32R) for n in ("hi", "lo")]
            w2 = [tmp(f"ws2_{n}", [P, 2, DIM], F32R) for n in ("hi", "lo")]
            logits, gate_b = tmp("logits", [P, TILES, EXPERTS]), tmp("gate_b", [P, EXPERTS])
            iota16, iota_slot = tmp("iota16", [P, TILES, EXPERTS]), tmp("iota_slot", [P, SLOT_TILES])
            token_no, not_first = tmp("token_no", [P, TILES]), tmp("not_first", [P, EXPERTS * TILES])
            later = tmp("later", [P, P])
            tables(nc, sem, name, inp, gate_b, iota16, iota_slot, token_no, not_first, later)
            split_weights(nc, sem, name + "_ws", [
                (inp["ws13"][k * P:(k + 1) * P, :], w13[0][:, k, :], w13[1][:, k, :]) for k in range(KD)] + [
                (inp["ws2"][k * P:k * P + HK[k], :], w2[0][0:HK[k], k, :], w2[1][0:HK[k], k, :]) for k in range(2)])
            halve(nc, sem, name, [w[0:HK[k], k, :] for w in w2 for k in range(2)])
            expert_tiles(nc, sem, name + "_shared", TILES, w13, w2, ident, xhat,
                         shared={"X": X, "norm": norm, "logits": logits})
            route(nc, sem, name + "_route", logits[:, :, :], gate_b[:, :], ident,
                  (iota16[:, :, :], later[:, :], iota_slot[:, :], token_no[:, :], not_first[:, :]),
                  slots[:, :, :], shares[:, :, :], tokens[:, :], tile_expert[:, :])
        with ExitStack() as big:
            w13 = [big.enter_context(nc.sbuf_tensor(f"{name}_w13_{n}", [P, KD, EXPERTS, 2 * HID], F32R)) for n in ("hi", "lo")]
            w2 = [big.enter_context(nc.sbuf_tensor(f"{name}_w2_{n}", [P, 2, EXPERTS, DIM], F32R)) for n in ("hi", "lo")]

            def flat(t, rows, k):
                return t[0:rows, k].rearrange("p e n -> p (e n)")

            split_weights(nc, sem, name + "_w", [
                (inp["w13"][k * P:(k + 1) * P, :], flat(w13[0], P, k), flat(w13[1], P, k)) for k in range(KD)] + [
                (inp["w2"][k * P:k * P + HK[k], :], flat(w2[0], HK[k], k), flat(w2[1], HK[k], k)) for k in range(2)])

            def expert(pe, n):
                return pe.value_load(tile_expert[0:1, bass.ds(n, 1)], min_val=0, max_val=EXPERTS - 1)

            expert_tiles(nc, sem, name + "_routed", SLOT_TILES, w13, w2, ident, xhat,
                         routed={"tokens": tokens, "column": column,
                                 "expert": expert, "out": y_dram})
        combine(nc, sem, name + "_combine", X, norm, slots, shares, y_dram)


def halve(nc, sem, name, parts):
    with nc.Block() as block:
        @block.vector
        def _(dve):
            for w in parts:
                nc.vector.tensor_scalar(w, w.bitcast(F32), 0.5, None, ALU.mult)


def tables(nc, sem, name, inp, gate_b, iota16, iota_slot, token_no, not_first, later):
    loaded = sem(name + "_tables_loaded")
    pairs = [(gate_b[:, :], inp["gate_b"]), (iota16[:, :, :], inp["iota16"].rearrange("p (t e) -> p t e", e=EXPERTS)),
             (iota_slot[:, :], inp["iota_slot"]), (token_no[:, :], inp["token_no"]), (not_first[:, :], inp["not_first"]),
             (later[:, :], inp["later"])]
    with nc.Block() as block:
        @block.sync
        def _(sp):
            for to, of in pairs:
                sp.dma_start(to, of).then_inc(loaded, 16)
            sp.wait_ge(loaded, 16 * len(pairs))


DECAY = 0.95


def smear(nc, sem, X, norm, ident, inp):
    scale = float(nc_sqrt(1.0 - DECAY))
    with ExitStack() as mem:
        def sb(n, shape, dt=F32):
            return mem.enter_context(nc.sbuf_tensor("sm_" + n, shape, dt))

        def ps(n, shape):
            return mem.enter_context(nc.psum_tensor("sm_" + n, shape, F32))

        wg, wv, wq, wo = (sb(n, [P, KD, DIM]) for n in ("wg", "wv", "wq", "wo"))
        bias = sb("bias", [P, 2, KD])
        decay = sb("decay", [P, GTOK])
        xn, xT = sb("xn", [P, 2, GT, DIM]), sb("xT", [P, 2, KD, GTOK])
        gate, que, store = sb("gate", [P, KD, GTOK]), sb("que", [P, KD, GTOK]), sb("store", [P, KD, GTOK])
        kept = sb("kept", [P, 2, KD, GTOK])
        load = sb("load", [P, 2, KD, GTOK])
        ps_xT, ps_y = ps("ps_xT", [P, KD, GTOK]), ps("ps_y", [P, GT, DIM])
        ps_g, ps_v, ps_q = (ps("ps_" + n, [P, GTOK]) for n in "gvq")
        loaded = sem("sm_loaded")
        with nc.Block() as block:
            @block.sync
            def _(sp):
                for to, of in ((wg, "l1_wg"), (wv, "l1_wv"), (wq, "l1_wq"), (wo, "l1_wo")):
                    sp.dma_start(to[:, :, :], inp[of].rearrange("(k p) n -> p k n", p=P)).then_inc(loaded, 16)
                sp.dma_start(bias[:, :, :], inp["l1_bias"].rearrange("p (a b) -> p a b", a=2)).then_inc(loaded, 16)
                sp.wait_ge(loaded, 16 * 5)

            @block.vector
            def _(dve):
                nc.vector.memset(decay[:, :], DECAY)

        names = ("xn_ready", "xT_made", "xT_ready", "g_made", "v_made", "q_made", "gate_ready", "que_ready",
                 "store_ready", "kept_ready", "load_ready", "y_made", "added")
        (xn_ready, xT_made, xT_ready, g_made, v_made, q_made, gate_ready, que_ready,
         store_ready, kept_ready, load_ready, y_made, added) = (sem("sm_" + n) for n in names)
        with nc.Block() as block:
            @block.vector
            def _(dve):
                def step(u, p):
                    g = 2 * u + p
                    if live(g, GROUPS):
                        if some(g - 1):
                            dve.wait_ge(xT_made, g - 1)
                        norm.apply(X[:, bass.ds(GT * g, GT), :], xn[:, p], g).then_inc(xn_ready, 1)
                    if live(g - 1, GROUPS):
                        h, q = g - 1, 1 - p
                        for m in range(KD):
                            n = KD * h + m + 1
                            dve.wait_ge(v_made, n)
                            dve.wait_ge(gate_ready, n)
                            nc.vector.scalar_tensor_tensor(out=store[:, m, :], in0=ps_v[:, :], scalar=scale,
                                                           in1=gate[:, m, :], op0=ALU.mult, op1=ALU.mult
                                                           ).then_inc(store_ready, 1)
                            dve.wait_ge(store_ready, n)
                            initial = kept[:, 0, m, GTOK - 1:GTOK] if q == 1 else 0.0
                            nc.vector.tensor_tensor_scan(kept[:, q, m, :], decay[:, :], store[:, m, :], initial,
                                                         ALU.mult, ALU.add).then_inc(kept_ready, 1)
                            dve.wait_ge(que_ready, n)
                            if m == 0:
                                if some(h - 1):
                                    dve.wait_ge(y_made, h - 1)
                            dve.wait_ge(kept_ready, n)
                            nc.vector.scalar_tensor_tensor(out=load[:, q, m, :], in0=kept[:, q, m, :], scalar=scale,
                                                           in1=que[:, m, :], op0=ALU.mult, op1=ALU.mult
                                                           ).then_inc(load_ready, 1)
                    if live(g - 2, GROUPS):
                        h = g - 2
                        dve.wait_ge(y_made, h + 1)
                        x4 = X[:, bass.ds(GT * h, GT), :]
                        nc.vector.tensor_tensor(x4, x4, ps_y[:, :, :], ALU.add).then_inc(added, 1)
                        dve.wait_ge(added, h + 1)
                        norm.statistics(x4, h)

                steps(dve, GROUPS, step, tail=2)

            @block.scalar
            def _(act):
                def step(u, p):
                    g = 2 * u + p
                    if live(g, GROUPS):
                        act.wait_ge(xT_made, g + 1)
                        nc.scalar.copy(xT[:, p], ps_xT[:, :, :]).then_inc(xT_ready, 1)
                    if live(g - 1, GROUPS):
                        for m in range(KD):
                            n = KD * (g - 1) + m + 1
                            if some(n - KD):
                                act.wait_ge(store_ready, n - KD)
                            act.wait_ge(g_made, n)
                            nc.scalar.activation(gate[:, m, :], ps_g[:, :], ACT.Sigmoid, bias=bias[:, 0, m:m + 1]
                                                 ).then_inc(gate_ready, 1)
                            if some(n - KD):
                                act.wait_ge(load_ready, n - KD)
                            act.wait_ge(q_made, n)
                            nc.scalar.activation(que[:, m, :], ps_q[:, :], ACT.Sigmoid, bias=bias[:, 1, m:m + 1]
                                                 ).then_inc(que_ready, 1)

                steps(act, GROUPS, step, tail=1)

            @block.tensor
            def _(pe):
                def step(u, p):
                    g = 2 * u + p
                    if live(g, GROUPS):
                        pe.wait_ge(xn_ready, g + 1)
                        if some(g):
                            pe.wait_ge(xT_ready, g)
                        for j in range(GT):
                            for k in range(KD):
                                last = nc.tensor.transpose(ps_xT[:, k, j * P:(j + 1) * P],
                                                           xn[:, p, j, k * P:(k + 1) * P], ident)
                        last.then_inc(xT_made, 1)
                    if live(g - 1, GROUPS):
                        h, q = g - 1, 1 - p
                        pe.wait_ge(xT_ready, h + 1)
                        for m in range(KD):
                            n = KD * h + m
                            for w, out, made, read in ((wg, ps_g, g_made, gate_ready), (wv, ps_v, v_made, store_ready),
                                                       (wq, ps_q, q_made, que_ready)):
                                if some(n):
                                    pe.wait_ge(read, n)
                                for k in range(KD):
                                    last = nc.tensor.matmul(out[:, :], w[:, k, m * P:(m + 1) * P], xT[:, q, k, :],
                                                            start=(k == 0), stop=(k == KD - 1))
                                last.then_inc(made, 1)
                    if live(g - 2, GROUPS):
                        h, q = g - 2, p
                        pe.wait_ge(load_ready, KD * (h + 1))
                        if some(h):
                            pe.wait_ge(added, h)
                        for j in range(GT):
                            for k in range(KD):
                                last = nc.tensor.matmul(ps_y[:, j, :], load[:, q, k, j * P:(j + 1) * P], wo[:, k, :],
                                                        start=(k == 0), stop=(k == KD - 1))
                        last.then_inc(y_made, 1)

                steps(pe, GROUPS, step, tail=2)


def nc_sqrt(x):
    import numpy as np

    return np.float32(np.sqrt(x))


def load_x(nc, sem, x_dram, X, norm, consts):
    loaded = sem("loaded")
    x_loaded = [sem(f"x_loaded{g}") for g in range(GROUPS)]
    with nc.Block() as block:
        @block.sync
        def _(sp):
            for g in range(GROUPS):
                sp.dma_start(X[:, GT * g:GT * (g + 1), :],
                             x_dram[g * GTOK:(g + 1) * GTOK, :].rearrange("(j p) d -> p j d", p=P)).then_inc(x_loaded[g], 16)
            for to, of in consts:
                sp.dma_start(to, of).then_inc(loaded, 16)
            sp.wait_ge(loaded, 16 * len(consts))

        @block.vector
        def _(dve):
            for g in range(GROUPS):
                dve.wait_ge(x_loaded[g], 16)
                norm.statistics(X[:, GT * g:GT * (g + 1), :], g)


def scale_weights(nc, sem, w_dense, w_b):
    scaled = sem("scaled")
    with nc.Block() as block:
        @block.vector
        def _(dve):
            nc.vector.tensor_scalar(w_dense[:, :, :], w_dense[:, :, :], 0.5, None, ALU.mult).then_inc(scaled, 1)
            nc.vector.tensor_scalar(w_b[:, :], w_b[:, :], 0.5 * 16.0, None, ALU.mult).then_inc(scaled, 1)


def store_x(nc, sem, X, out):
    stored = sem("stored")
    with nc.Block() as block:
        @block.sync
        def _(sp):
            sp.dma_start(out.rearrange("(t p) d -> p t d", p=P), X[:, :, :]).then_inc(stored, 16)
            sp.wait_ge(stored, 16)


def macaron_kernel(nc, out, until=6, only=None, **inp):
    with ExitStack():
        taken = []

        def sem(name):
            taken.append(nc.alloc_semaphore(name))
            return taken[-1]

        def next_stage():
            nc.clear_and_free_semaphores(taken)
            nc.all_engine_barrier()
            taken.clear()

        with ExitStack() as outer:
            def keep(n, shape, dt=F32):
                return outer.enter_context(nc.sbuf_tensor(n, shape, dt))

            X = keep("X", [P, TILES, DIM])
            ident = keep("ident", [P, P])
            norm = Norm(nc, keep)
            with ExitStack() as mem:
                def sb(n, shape, dt=F32):
                    return mem.enter_context(nc.sbuf_tensor(n, shape, dt))

                w_lora, w_dense, w_b = sb("w_lora", [P, KD, LA]), sb("w_dense", [P, KD, DIM]), sb("w_b", [P, DIM])
                iota8 = sb("iota8", [P, GT, 2, 8])
                wq, wk, wv, wo = (sb(n, [P, KD, DIM]) for n in ("wq", "wk", "wv", "wo"))

                def chunks(w):
                    return w.rearrange("(k p) n -> p k n", p=P)

                load_x(nc, sem, inp["x"], X, norm, [
                    (w_lora[:, :, :], chunks(inp["w_lora"])), (w_dense[:, :, :], chunks(inp["w_dense"])),
                    (w_b[:, :], inp["w_b"]), (ident[:, :], inp["ident"]),
                    (iota8[:, :, :, :], inp["iota8"].rearrange("p (a b c) -> p a b c", a=GT, b=2)),
                    (wq[:, :, :], chunks(inp["wq"])), (wk[:, :, :], chunks(inp["wk"])),
                    (wv[:, :, :], chunks(inp["wv"])), (wo[:, :, :], chunks(inp["wo"]))])
                scale_weights(nc, sem, w_dense, w_b)
                if only is None:
                    norm.finish(sem, "ffn1")
                    lora_ffn(nc, "ffn1", sem, X, norm, w_lora, w_dense, w_b[:, :], ident[:, :], iota8)
                    norm.finish(sem, "attn")
                    attention(nc, sem, X, norm, wq, wk, wv, wo, ident[:, :], inp)
                    norm.finish(sem, "ffn2")
                    lora_ffn(nc, "ffn2", sem, X, norm, w_lora, w_dense, w_b[:, :], ident[:, :], iota8)
            xhat = nc.dram_tensor("xhat", [TOKENS, DIM], F32).ap()
            y_dram = nc.dram_tensor("y_slots", [SLOTS, DIM], F32).ap()
            next_stage()
            if until >= 4 and only in (None, 4):
                norm.finish(sem, "moe1")
                moe(nc, sem, "moe1", X, norm, ident[:, :], inp, (xhat, y_dram))
                next_stage()
            if until >= 5 and only in (None, 5):
                norm.finish(sem, "sm")
                smear(nc, sem, X, norm, ident[:, :], inp)
            if until >= 6 and only is None:
                norm.finish(sem, "moe2")
                moe(nc, sem, "moe2", X, norm, ident[:, :], inp, (xhat, y_dram))
            store_x(nc, sem, X, out)


def lay_out(a):
    import numpy as np

    c = np.ascontiguousarray
    f = np.float32
    d = {k: np.asarray(v) for k, v in a.items()}
    return {
        "x": c(d["L0_attn_x"].reshape(TOKENS, DIM)),
        "w_lora": c(np.concatenate([d["L0_ffn_A_w"].reshape(LER, DIM).T, d["L0_ffn_gate_w"].T], 1)),
        "w_dense": c(d["L0_ffn_weight"].T),
        "w_b": c(d["L0_ffn_B_w"].transpose(0, 2, 1).reshape(LER, DIM)),
        "wq": c(d["L0_attn_Wq"].T), "wk": c(d["L0_attn_Wk"].T), "wv": c(d["L0_attn_Wv"].T), "wo": c(d["L0_attn_Wo"].T),
        "ident": np.eye(P, dtype=f),
        "ws13": c(np.concatenate([d["L1_ffn_w1_shared"], d["L1_ffn_w3_shared"], d["L1_ffn_gate_w"].T], 1)),
        "ws2": c(d["L1_ffn_w2_shared"]),
        "w13": c(np.concatenate([d["L1_ffn_w1_routed"], d["L1_ffn_w3_routed"]], 2).transpose(1, 0, 2).reshape(DIM, -1)),
        "w2": c(d["L1_ffn_w2_routed"].transpose(1, 0, 2).reshape(HID, -1)),
        "gate_b": c(np.tile(d["L1_ffn_gate_b"], (P, 1))),
        "l1_wg": c(d["L1_attn_Wg"]), "l1_wv": c(d["L1_attn_Wv"]), "l1_wq": c(d["L1_attn_Wq"]), "l1_wo": c(d["L1_attn_Wo"]),
        "l1_bias": c(np.concatenate([d["L1_attn_bg"].reshape(KD, P), d["L1_attn_bq"].reshape(KD, P)]).T),
        "iota16": c(np.tile(np.arange(EXPERTS, dtype=f), (P, TILES))),
        "iota_slot": c(np.tile(np.arange(SLOT_TILES, dtype=f), (P, 1))),
        "token_no": c((np.arange(TILES)[None, :] * P + np.arange(P)[:, None]).astype(f)),
        "not_first": c(np.tile((np.arange(TILES) > 0).astype(f), (P, EXPERTS))),
        "later": np.triu(np.ones((P, P), f), 1),
        "iota8": c(np.tile(np.arange(8, dtype=f), (P, GT * 2))),
    }


def kernel(**inputs):
    import numpy as np
    import concourse.bacc as bacc
    from concourse.bass_utils import run_bass_kernel_spmd

    nc = bacc.Bacc("TRN2", target_bir_lowering=False, num_devices=1)
    arrays = lay_out(inputs)
    args = {n: nc.dram_tensor(f"in_{n}", a.shape, mybir.dt.from_np(a.dtype), kind="ExternalInput").ap()
            for n, a in arrays.items()}
    out = nc.dram_tensor("out", [TOKENS, DIM], F32, kind="ExternalOutput").ap()
    macaron_kernel(nc, out, **args)
    r = run_bass_kernel_spmd(nc, [{f"in_{n}": a for n, a in arrays.items()}], core_ids=[0])
    return r.results[0]["out"].reshape(BATCH, SEQ, DIM)
```

```python
import concourse.bass as bass
from concourse import mybir
from contextlib import ExitStack

P = 128
F32, F32R, BF16 = mybir.dt.float32, mybir.dt.float32r, mybir.dt.bfloat16
I32, U32 = mybir.dt.int32, mybir.dt.uint32
ACT, ALU, AX = mybir.ActivationFunctionType, mybir.AluOpType, mybir.AxisListType
EPS_NORM = 1e-5

BATCH, SEQ, DIM = 4, 1024, 256
TOKENS = BATCH * SEQ
TILES = TOKENS // P
KD = DIM // P
GT = 4
GROUPS = TILES // GT
GTOK = GT * P


def some(count):
    return not isinstance(count, int) or count > 0


def live(step, count):
    return not isinstance(step, int) or 0 <= step < count


def steps(eng, count, step, tail=0, ways=2, head=1):
    for n in range(ways * head):
        step(n // ways, n % ways)
    with eng.Fori(head, count // ways) as u:
        for p in range(ways):
            step(u, p)
    for n in range(count, count + tail):
        step(n // ways, n % ways)


def back(u, p):
    return (u, 0) if p else (u - 1, 1)


class Chain:

    def __init__(self, eng, sem, per_item):
        self.eng, self.sem, self.per_item = eng, sem, per_item

    def item(self, n):
        self.base, self.done = n * self.per_item, 0

    def link(self, instruction, wait=True):
        self.done += 1
        assert self.done <= self.per_item
        instruction.then_inc(self.sem, 1)
        if wait:
            self.eng.wait_ge(self.sem, self.base + self.done)


class Norm:

    def __init__(self, nc, sb):
        self.nc = nc
        self.stats, self.mean, self.rstd = sb("stats", [P, TILES, 6]), sb("mean", [P, TILES]), sb("rstd", [P, TILES])
        self.var, self.work = sb("var", [P, TILES]), sb("work", [P, TILES])

    def statistics(self, x4, g):
        for j in range(GT):
            last = self.nc.vector.bn_stats(self.stats[:, bass.ds(GT * g + j, 1), :], x4[:, j, :])
        return last

    def finish(self, sem, name):
        nc, s, links = self.nc, self.stats, sem(name + "_norm_links")
        var_ready, root_ready = sem(name + "_var_ready"), sem(name + "_root_ready")
        mean, var, rstd, work = self.mean[:, :], self.var[:, :], self.rstd[:, :], self.work[:, :]
        with nc.Block() as block:
            @block.vector
            def _(dve):
                chain = Chain(dve, links, 11)
                chain.item(0)
                vec = nc.vector
                vec.tensor_tensor(mean, s[:, :, 1], s[:, :, 4], ALU.add)
                vec.tensor_tensor(var, s[:, :, 2], s[:, :, 5], ALU.add)
                chain.link(vec.tensor_tensor(work, s[:, :, 1], s[:, :, 4], ALU.subtract))
                vec.tensor_scalar(mean, mean, 0.5, None, ALU.mult)
                vec.tensor_scalar(var, var, 1.0 / DIM, EPS_NORM, ALU.mult, ALU.add)
                chain.link(vec.tensor_tensor(work, work, work, ALU.mult))
                chain.link(vec.scalar_tensor_tensor(out=var, in0=work, scalar=0.25, in1=var, op0=ALU.mult, op1=ALU.add))
                vec.tensor_copy(work, var).then_inc(var_ready, 1)
                dve.wait_ge(root_ready, 1)
                chain.link(vec.reciprocal(rstd, work))
                chain.link(vec.tensor_tensor(work, rstd, rstd, ALU.mult))
                chain.link(vec.tensor_tensor(work, work, var, ALU.mult))
                chain.link(vec.tensor_scalar(work, work, -0.5, 1.5, ALU.mult, ALU.add))
                chain.link(vec.tensor_tensor(rstd, rstd, work, ALU.mult))

            @block.scalar
            def _(act):
                act.wait_ge(var_ready, 1)
                nc.scalar.activation(work, var, ACT.Sqrt).then_inc(root_ready, 1)

    def of_batch(self, chain, b, work, bits):
        vec, n = self.nc.vector, TILES // BATCH
        s = self.stats[:, bass.ds(n * b, n), :]
        mean, var, rstd = (a[:, bass.ds(n * b, n)] for a in (self.mean, self.var, self.rstd))
        vec.tensor_tensor(mean, s[:, :, 1], s[:, :, 4], ALU.add)
        vec.tensor_tensor(var, s[:, :, 2], s[:, :, 5], ALU.add)
        chain.link(vec.tensor_tensor(work, s[:, :, 1], s[:, :, 4], ALU.subtract))
        vec.tensor_scalar(mean, mean, 0.5, None, ALU.mult)
        vec.tensor_scalar(var, var, 1.0 / DIM, EPS_NORM, ALU.mult, ALU.add)
        chain.link(vec.tensor_tensor(work, work, work, ALU.mult))
        chain.link(vec.scalar_tensor_tensor(out=var, in0=work, scalar=0.25, in1=var, op0=ALU.mult, op1=ALU.add))
        chain.link(vec.tensor_scalar(bits, var.bitcast(I32), 1, None, ALU.arith_shift_right))
        chain.link(vec.tensor_scalar(rstd.bitcast(I32), bits, -1.0, float(0x5F3759DF), ALU.mult, ALU.add))
        for _ in range(3):
            chain.link(vec.tensor_tensor(work, rstd, rstd, ALU.mult))
            chain.link(vec.scalar_tensor_tensor(out=work, in0=work, scalar=-0.5, in1=var, op0=ALU.mult, op1=ALU.mult))
            chain.link(vec.scalar_tensor_tensor(out=rstd, in0=work, scalar=1.5, in1=rstd, op0=ALU.add, op1=ALU.mult))

    BATCH_LINKS = 14

    def apply_tile(self, X, out, t):
        return self.nc.vector.tensor_scalar(out, X[:, bass.ds(t, 1), :].rearrange("p a d -> p (a d)"),
                                            self.mean[:, bass.ds(t, 1)], self.rstd[:, bass.ds(t, 1)],
                                            ALU.subtract, ALU.mult)

    def apply(self, x4, xn4, g):
        for j in range(GT):
            last = self.nc.vector.tensor_scalar(xn4[:, j, :], x4[:, j, :], self.mean[:, bass.ds(GT * g + j, 1)],
                                                self.rstd[:, bass.ds(GT * g + j, 1)], ALU.subtract, ALU.mult)
        return last


LORA_E, LORA_R = 8, 16
LER = LORA_E * LORA_R
LA = LER + LORA_E


def lora_ffn(nc, name, sem, X, norm, w_lora, w_dense, w_b, ident, iota8):
    with ExitStack() as mem:
        def sb(n, shape, dt=F32):
            return mem.enter_context(nc.sbuf_tensor(f"{name}_{n}", shape, dt))

        def ps(n, shape):
            return mem.enter_context(nc.psum_tensor(f"{name}_{n}", shape, F32))

        xn, xT = sb("xn", [P, 2, GT, DIM]), sb("xT", [P, 2, KD, GTOK])
        top, idx, idxf = sb("top", [P, GT, 8]), sb("idx", [P, GT, 8], U32), sb("idxf", [P, GT, 2])
        gap, second, total = sb("gap", [P, GT]), sb("second", [P, GT]), sb("total", [P, GT])
        share, onehot, cw = sb("share", [P, GT, 2]), sb("onehot", [P, GT, 2, 8]), sb("cw", [P, GT, 8])
        tw, twT = sb("tw", [P, GT, LER]), sb("twT", [P, GTOK])
        ps_xT, ps_lora, ps_out = ps("ps_xT", [P, KD, GTOK]), ps("ps_lora", [P, 2, 512]), ps("ps_out", [P, 2, 512])
        ps_twT = ps("ps_twT", [P, GTOK])

        route_chain = sem(name + "_route_chain")
        xn_ready, xT_made, xT_ready = sem(name + "_xn_ready"), sem(name + "_xT_made"), sem(name + "_xT_ready")
        lora_made, gap_ready, second_ready = sem(name + "_lora_made"), sem(name + "_gap_ready"), sem(name + "_second_ready")
        tw_ready, twT_made, twT_ready = sem(name + "_tw_ready"), sem(name + "_twT_made"), sem(name + "_twT_ready")
        out_made, added = sem(name + "_out_made"), sem(name + "_added")

        def lora_cols(j, a, b):
            return ps_lora[:, j // 2, (j % 2) * LA + a:(j % 2) * LA + b]

        with nc.Block() as block:
            @block.vector
            def _(dve):
                route = Chain(dve, route_chain, 8)
                rstd_col = norm.rstd[:, 0:1]

                def step(u, p):
                    g = 2 * u + p
                    if live(g, GROUPS):
                        if some(g - 1):
                            dve.wait_ge(xT_made, g - 1)
                        norm.apply(X[:, bass.ds(GT * g, GT), :], xn[:, p], g).then_inc(xn_ready, 1)
                    if live(g - 1, GROUPS):
                        h = g - 1
                        route.item(h)
                        dve.wait_ge(lora_made, h + 1)
                        nc.vector.tensor_copy(total[:, 0:1], rstd_col)
                        for j in range(GT):
                            last = nc.vector.max(top[:, j, :], lora_cols(j, LER, LA))
                        route.link(last)
                        nc.vector.tensor_tensor(gap[:, :], top[:, :, 1], top[:, :, 0],
                                                ALU.subtract).then_inc(gap_ready, 1)
                        for j in range(GT):
                            last = nc.vector.max_index(idx[:, j, :], top[:, j, :], lora_cols(j, LER, LA))
                        route.link(last)
                        route.link(nc.vector.tensor_copy(idxf[:, :, :], idx[:, :, 0:2]))
                        dve.wait_ge(second_ready, h + 1)
                        route.link(nc.vector.tensor_scalar(total[:, :], second[:, :], 1.0, None, ALU.add))
                        route.link(nc.vector.reciprocal(share[:, :, 0], total[:, :]))
                        nc.vector.tensor_tensor(share[:, :, 1], second[:, :], share[:, :, 0], ALU.mult)
                        route.link(nc.vector.tensor_tensor(
                            onehot[:, :, :, :], iota8[:, :, :, :],
                            idxf[:, :, :].unsqueeze(3).to_broadcast([P, GT, 2, 8]), ALU.is_equal))
                        route.link(nc.vector.tensor_tensor(
                            onehot[:, :, :, :], onehot[:, :, :, :],
                            share[:, :, :].unsqueeze(3).to_broadcast([P, GT, 2, 8]), ALU.mult))
                        route.link(nc.vector.tensor_tensor(cw[:, :, :], onehot[:, :, 0, :], onehot[:, :, 1, :], ALU.add))
                        if some(h):
                            dve.wait_ge(twT_made, h)
                        for j in range(GT):
                            last = nc.vector.tensor_tensor(
                                tw[:, j, :].rearrange("p (e r) -> p e r", e=LORA_E),
                                lora_cols(j, 0, LER).rearrange("p (e r) -> p e r", e=LORA_E),
                                cw[:, j, :].unsqueeze(2).to_broadcast([P, LORA_E, LORA_R]), ALU.mult)
                        last.then_inc(tw_ready, 1)
                    if live(g - 2, GROUPS):
                        h = g - 2
                        dve.wait_ge(out_made, h + 1)
                        x4 = X[:, bass.ds(GT * h, GT), :]
                        nc.vector.tensor_tensor(x4, x4, ps_out[:, :, :].rearrange("p a (b d) -> p (a b) d", d=DIM),
                                                ALU.add).then_inc(added, 1)
                        dve.wait_ge(added, h + 1)
                        norm.statistics(x4, h)

                steps(dve, GROUPS, step, tail=2)

            @block.scalar
            def _(act):
                def step(u, p):
                    g = 2 * u + p
                    if live(g, GROUPS):
                        act.wait_ge(xT_made, g + 1)
                        nc.scalar.copy(xT[:, p], ps_xT[:, :, :]).then_inc(xT_ready, 1)
                    if live(g - 1, GROUPS):
                        if some(g):
                            act.wait_ge(gap_ready, g)
                        nc.scalar.activation(second[:, :], gap[:, :], ACT.Exp).then_inc(second_ready, 1)
                        if some(g):
                            act.wait_ge(twT_made, g)
                        nc.scalar.copy(twT[:, :], ps_twT[:, :]).then_inc(twT_ready, 1)

                steps(act, GROUPS, step, tail=1)

            @block.tensor
            def _(pe):
                def step(u, p):
                    g = 2 * u + p
                    if live(g, GROUPS):
                        pe.wait_ge(xn_ready, g + 1)
                        if some(g):
                            pe.wait_ge(xT_ready, g)
                        for j in range(GT):
                            for k in range(KD):
                                last = nc.tensor.transpose(ps_xT[:, k, j * P:(j + 1) * P],
                                                           xn[:, p, j, k * P:(k + 1) * P], ident)
                        last.then_inc(xT_made, 1)
                        pe.wait_ge(xT_ready, g + 1)
                        if some(g):
                            pe.wait_ge(tw_ready, g)
                        for j in range(GT):
                            for k in range(KD):
                                last = nc.tensor.matmul(lora_cols(j, 0, LA), xT[:, p, k, j * P:(j + 1) * P],
                                                        w_lora[:, k, :], start=(k == 0), stop=(k == KD - 1))
                        last.then_inc(lora_made, 1)
                    if live(g - 1, GROUPS):
                        h, q = g - 1, 1 - p
                        if some(h):
                            pe.wait_ge(added, h)
                        for j in range(GT):
                            for k in range(KD):
                                nc.tensor.matmul(ps_out[:, j // 2, (j % 2) * DIM:(j % 2 + 1) * DIM],
                                                 xT[:, q, k, j * P:(j + 1) * P], w_dense[:, k, :],
                                                 start=(k == 0 and j % 2 == 0), stop=False,
                                                 skip_group_check=True)
                        pe.wait_ge(tw_ready, h + 1)
                        if some(h):
                            pe.wait_ge(twT_ready, h)
                        for j in range(GT):
                            last = nc.tensor.transpose(ps_twT[:, j * P:(j + 1) * P], tw[:, j, :], ident)
                        last.then_inc(twT_made, 1)
                        pe.wait_ge(twT_ready, h + 1)
                        for j in range(GT):
                            last = nc.tensor.matmul(ps_out[:, j // 2, (j % 2) * DIM:(j % 2 + 1) * DIM],
                                                    twT[:, j * P:(j + 1) * P], w_b, start=False, stop=True,
                                                    skip_group_check=True)
                        last.then_inc(out_made, 1)

                steps(pe, GROUPS, step, tail=1)


HEADS = 16
HD = DIM // HEADS
GH = 4
HGROUPS = HEADS // GH
QK_SCALE = HD ** -0.5
THRESHOLD = -0.1
DEN_EPS = 1e-6
PARTS = 3
Q_ROWS, K_ROWS = (0, 0, 1, 0, 2, 1), (0, 1, 0, 2, 0, 1)
STACK = HD * len(Q_ROWS)
QBLOCKS = SEQ // GTOK
KTILES = SEQ // P


def project(nc, sem, X, norm, weights, ident, V, parts_dram):
    wq, wk, wv = weights
    with ExitStack() as mem:
        def sb(n, shape, dt=F32):
            return mem.enter_context(nc.sbuf_tensor("pr_" + n, shape, dt))

        def ps(n, shape):
            return mem.enter_context(nc.psum_tensor("pr_" + n, shape, F32))

        xn, xT = sb("xn", [P, 2, GT, DIM]), sb("xT", [P, 2, KD, GTOK])
        parts = sb("parts", [P, 2, 2, KD, PARTS, GTOK], BF16)
        rest = sb("rest", [P, 2, KD, GTOK])
        ps_xT, ps_v = ps("ps_xT", [P, KD, GTOK]), ps("ps_v", [P, GT, DIM])
        ps_qk = ps("ps_qk", [P, 2, KD, GTOK])
        xn_ready, xT_made, xT_ready = sem("pr_xn_ready"), sem("pr_xT_made"), sem("pr_xT_ready")
        qk_made, part1_ready, rest_ready, part2_ready, part3_ready = (
            sem("pr_" + n) for n in ("qk_made", "part1_ready", "rest_ready", "part2_ready", "part3_ready"))
        v_made, v_ready = sem("pr_v_made"), sem("pr_v_ready")
        stored = [sem(f"pr_stored{p}") for p in range(2)]
        scales = (QK_SCALE, 1.0)
        units = [(w, m) for w in range(2) for m in range(KD)]

        with nc.Block() as block:
            @block.vector
            def _(dve):
                def step(u, p):
                    g = 2 * u + p
                    if live(g, GROUPS):
                        if some(g - 1):
                            dve.wait_ge(xT_made, g - 1)
                        norm.apply(X[:, bass.ds(GT * g, GT), :], xn[:, p], g).then_inc(xn_ready, 1)
                    if live(g - 1, GROUPS):
                        for i, (w, m) in enumerate(units):
                            dve.wait_ge(part1_ready, 4 * (g - 1) + i + 1)
                            if some(4 * (g - 2) + i + 1):
                                dve.wait_ge(part3_ready, 4 * (g - 2) + i + 1)
                            nc.vector.scalar_tensor_tensor(
                                out=rest[:, w, m, :], in0=ps_qk[:, w, m, :], scalar=scales[w],
                                in1=parts[:, 1 - p, w, m, 0, :], op0=ALU.mult, op1=ALU.subtract).then_inc(rest_ready, 1)

                steps(dve, GROUPS, step, tail=1)

            @block.scalar
            def _(act):
                def step(u, p):
                    g = 2 * u + p
                    if live(g, GROUPS):
                        act.wait_ge(xT_made, g + 1)
                        nc.scalar.copy(xT[:, p], ps_xT[:, :, :]).then_inc(xT_ready, 1)
                    if live(g - 1, GROUPS):
                        hu, q = back(u, p)
                        for i, (w, m) in enumerate(units):
                            act.wait_ge(qk_made, 4 * (g - 1) + i + 1)
                            if i == 0:
                                if some(32 * hu):
                                    act.wait_ge(stored[q], 32 * hu)
                            nc.scalar.activation(parts[:, q, w, m, 0, :], ps_qk[:, w, m, :], ACT.Copy,
                                                 scale=scales[w]).then_inc(part1_ready, 1)
                        if some(g):
                            act.wait_ge(v_made, g)
                        nc.scalar.copy(V[:, bass.ds(GT * (g - 1), GT), :, 0:HD],
                                       ps_v[:, :, :].rearrange("p t (h d) -> p t h d", d=HD)).then_inc(v_ready, 1)
                        for i, (w, m) in enumerate(units):
                            act.wait_ge(rest_ready, 4 * (g - 1) + i + 1)
                            nc.scalar.copy(parts[:, q, w, m, 1, :], rest[:, w, m, :]).then_inc(part2_ready, 1)

                steps(act, GROUPS, step, tail=1)

            @block.gpsimd
            def _(pool):
                nc.gpsimd.memset(V[:, :, :, HD:], 1.0)

                def step(u, p):
                    g = 2 * u + p
                    for i, (w, m) in enumerate(units):
                        pool.wait_ge(part2_ready, 4 * g + i + 1)
                        nc.gpsimd.tensor_tensor(parts[:, p, w, m, 2, :], rest[:, w, m, :],
                                                parts[:, p, w, m, 1, :], ALU.subtract).then_inc(part3_ready, 1)

                steps(pool, GROUPS, step)

            @block.tensor
            def _(pe):
                def step(u, p):
                    g = 2 * u + p
                    if live(g, GROUPS):
                        pe.wait_ge(xn_ready, g + 1)
                        if some(g):
                            pe.wait_ge(xT_ready, g)
                        for j in range(GT):
                            for k in range(KD):
                                last = nc.tensor.transpose(ps_xT[:, k, j * P:(j + 1) * P],
                                                           xn[:, p, j, k * P:(k + 1) * P], ident)
                        last.then_inc(xT_made, 1)
                    if live(g - 1, GROUPS):
                        h, q = g - 1, 1 - p
                        pe.wait_ge(xT_ready, h + 1)
                        for i, (w, m) in enumerate(units):
                            if some(4 * (h - 1) + i + 1):
                                pe.wait_ge(rest_ready, 4 * (h - 1) + i + 1)
                            for k in range(KD):
                                last = nc.tensor.matmul(ps_qk[:, w, m, :], (wq, wk)[w][:, k, m * P:(m + 1) * P],
                                                        xT[:, q, k, :], start=(k == 0), stop=(k == KD - 1))
                            last.then_inc(qk_made, 1)
                        if some(h):
                            pe.wait_ge(v_ready, h)
                        for j in range(GT):
                            for k in range(KD):
                                last = nc.tensor.matmul(ps_v[:, j, :], xT[:, q, k, j * P:(j + 1) * P],
                                                        wv[:, k, :], start=(k == 0), stop=(k == KD - 1))
                        last.then_inc(v_made, 1)

                steps(pe, GROUPS, step, tail=1)

            @block.sync
            def _(sp):
                def step(u, p):
                    g = 2 * u + p
                    sp.wait_ge(part3_ready, 4 * (g + 1))
                    for w in range(2):
                        sp.dma_start(parts_dram[w, bass.ds(g, 1)].rearrange("o m p c t -> p (o m) c t"),
                                     parts[:, p, w]).then_inc(stored[p], 16)

                steps(sp, GROUPS, step)
                for p in range(2):
                    sp.wait_ge(stored[p], 32 * (GROUPS // 2))


SCORE_UNITS = [(qb, kt) for qb in range(QBLOCKS) for kt in range(GT * (qb + 1))]
S_BANKS, W_BUFS = 6, 8


def attend(nc, sem, V, parts_dram, diag, ident, heads_out):
    items = BATCH * HGROUPS
    units = len(SCORE_UNITS)
    last_of = {qb: max(k for k, (b, _) in enumerate(SCORE_UNITS) if b == qb) for qb in range(QBLOCKS)}
    with ExitStack() as mem:
        def sb(n, shape, dt=F32):
            return mem.enter_context(nc.sbuf_tensor("at_" + n, shape, dt))

        Q = [sb(f"Q{p}", [STACK, GH, SEQ], BF16) for p in range(2)]
        K = [sb(f"K{p}", [STACK, GH, SEQ], BF16) for p in range(2)]
        v = [sb(f"v{p}", [P, KTILES, GH * 2 * HD]) for p in range(2)]
        w = [sb(f"w{n}", [P, GTOK]) for n in range(W_BUFS)]
        o, rec = sb("o", [P, GTOK]), sb("rec", [P, GT * GH])
        ps_s = [mem.enter_context(nc.psum_tensor(f"at_s{n}", [P, GTOK], F32)) for n in range(S_BANKS)]
        ps_o = [mem.enter_context(nc.psum_tensor(f"at_o{n}", [P, GTOK], F32)) for n in range(QBLOCKS)]
        qk_loaded = [sem(f"at_qk_loaded{p}") for p in range(2)]
        v_ready, s_made, pv_done = sem("at_v_ready"), sem("at_s_made"), sem("at_pv_done")
        w_ready = [sem("at_w_even_ready"), sem("at_w_odd_ready")]
        o_copied, oT_made, normed, rec_chain = sem("at_o_copied"), sem("at_oT_made"), sem("at_normed"), sem("at_rec_chain")
        tri, big = diag

        def span(k):
            qb, kt = SCORE_UNITS[k]
            return max(0, kt * P - qb * GTOK)

        def evacuate(eng, it, k, j, write):
            n = GH * k + j
            if some(units * it + k - 1):
                eng.wait_ge(pv_done, units * it + k - 1)
            eng.wait_ge(s_made, GH * units * it + n + 1)
            c = span(k)
            write(w[n % W_BUFS][:, c:], ps_s[n % S_BANKS][:, c:]).then_inc(w_ready[j % 2], 1)

        with nc.Block() as block:
            @block.sync
            def _(sp):
                def step(u, p):
                    it = 2 * u + p
                    if some(GH * units * (it - 1)):
                        sp.wait_ge(s_made, GH * units * (it - 1))
                    for dst, which, rows in ((Q, 0, Q_ROWS), (K, 1, K_ROWS)):
                        for r, part in enumerate(rows):
                            for qb in range(QBLOCKS):
                                src = parts_dram[which, bass.ds((it // HGROUPS) * QBLOCKS + qb, 1),
                                                 bass.ds((it % HGROUPS) // 2, 1), bass.ds((it % 2) * 64, 64), part, :]
                                sp.dma_start(dst[p][r * HD:(r + 1) * HD, :, qb * GTOK:(qb + 1) * GTOK],
                                             src.rearrange("a b (h d) t -> (a b d) h t", d=HD)).then_inc(qk_loaded[p], 16)

                steps(sp, items, step)

            @block.gpsimd
            def _(pool):
                def step(u, p):
                    it = 2 * u + p
                    if some(units * (it - 1)):
                        pool.wait_ge(pv_done, units * (it - 1))
                    src = V[:, bass.ds((it // HGROUPS) * KTILES, KTILES), bass.ds((it % HGROUPS) * GH, GH), :]
                    nc.gpsimd.tensor_copy(v[p][:, :, :].rearrange("p t (h d) -> p t h d", h=GH), src).then_inc(v_ready, 1)

                steps(pool, items, step)

            @block.scalar
            def _(act):
                def copy_out(it, qb):
                    act.wait_ge(pv_done, units * it + last_of[qb] + 1)
                    if some(QBLOCKS * it + qb):
                        act.wait_ge(oT_made, QBLOCKS * it + qb)
                    nc.scalar.copy(o[:, :], ps_o[qb][:, :]).then_inc(o_copied, 1)

                def step(u, p):
                    it = 2 * u + p
                    for k in range(units):
                        if live(it, items):
                            for j in (0, 2):
                                evacuate(act, it, k, j, lambda out, s: nc.scalar.activation(
                                    out, s, ACT.Relu, bias=threshold_col))
                        if k == 0 and live(it - 1, items):
                            copy_out(it - 1, 1)
                        if k == 4 and live(it, items):
                            copy_out(it, 0)

                threshold_col = tri[1]
                steps(act, items, step, tail=1)

            @block.vector
            def _(dve):
                chain = Chain(dve, rec_chain, 2 * QBLOCKS)

                def norm_heads(it, qb, n):
                    dve.wait_ge(oT_made, QBLOCKS * it + qb + 1)
                    oT = ps_o[qb][:, :].rearrange("p (t h c) -> p t h c", t=GT, h=GH)
                    chain.base, chain.done = 2 * (QBLOCKS * it + qb), 0
                    recs = rec[:, :].rearrange("p (t h) -> p t h", t=GT)
                    chain.link(nc.vector.tensor_scalar(recs, oT[:, :, :, HD], DEN_EPS, None, ALU.add))
                    chain.link(nc.vector.reciprocal(recs, recs))
                    out = heads_out[:, bass.ds((it // HGROUPS) * QBLOCKS + qb, 1), bass.ds(it % HGROUPS, 1)]
                    nc.vector.tensor_tensor(out.rearrange("p a b (t h) d -> p (a b t) h d", h=GH), oT[:, :, :, 0:HD],
                                            recs.unsqueeze(3).to_broadcast([P, GT, GH, HD]),
                                            ALU.mult).then_inc(normed, 1)

                def step(u, p):
                    it = 2 * u + p
                    for k in range(units):
                        if live(it, items):
                            for j in (1, 3):
                                evacuate(dve, it, k, j, lambda out, s: nc.vector.tensor_scalar(
                                    out, s, -THRESHOLD, 0.0, ALU.add, ALU.max))
                        if k == 2 and live(it - 1, items):
                            norm_heads(it - 1, 1, k)
                        if k == 6 and live(it, items):
                            norm_heads(it, 0, k)

                steps(dve, items, step, tail=1)

            @block.tensor
            def _(pe):
                def score(it, p, k, j):
                    qb, kt = SCORE_UNITS[k]
                    n, c = GH * k + j, span(k)
                    before = n - S_BANKS
                    if some(2 * units * it + before // 2 + 1):
                        pe.wait_ge(w_ready[j % 2], 2 * units * it + before // 2 + 1)
                    s = ps_s[n % S_BANKS]
                    diagonal = kt >= GT * qb
                    last = nc.tensor.matmul(s[:, c:], K[p][:, j, kt * P:(kt + 1) * P],
                                            Q[p][:, j, qb * GTOK + c:(qb + 1) * GTOK],
                                            start=True, stop=not diagonal, skip_group_check=True)
                    if diagonal:
                        last = nc.tensor.matmul(s[:, c:c + P], big, tri[0], start=False, stop=True,
                                                skip_group_check=True)
                    last.then_inc(s_made, 1)

                def weigh(it, p, k):
                    qb, kt = SCORE_UNITS[k]
                    c = span(k)
                    if k == 0:
                        pe.wait_ge(v_ready, it + 1)
                    if kt == 0:
                        if some(QBLOCKS * (it - 1) + qb + 1):
                            pe.wait_ge(normed, QBLOCKS * (it - 1) + qb + 1)
                    for j in range(GH):
                        n = GH * k + j
                        pe.wait_ge(w_ready[j % 2], 2 * units * it + n // 2 + 1)
                        last = nc.tensor.matmul(ps_o[qb][32 * j:32 * (j + 1), c:],
                                                v[p][:, kt, j * 2 * HD:(j + 1) * 2 * HD], w[n % W_BUFS][:, c:],
                                                start=(kt == 0), stop=(k == last_of[qb]), skip_group_check=True)
                    last.then_inc(pv_done, 1)

                def transpose_out(it, qb):
                    pe.wait_ge(o_copied, QBLOCKS * it + qb + 1)
                    for t in range(GT):
                        last = nc.tensor.transpose(ps_o[qb][:, t * P:(t + 1) * P], o[:, t * P:(t + 1) * P], ident)
                    last.then_inc(oT_made, 1)

                def step(u, p):
                    it = 2 * u + p
                    for k in range(units):
                        if live(it, items):
                            if k == 0:
                                pe.wait_ge(qk_loaded[p], 16 * 2 * len(Q_ROWS) * QBLOCKS * (u + 1))
                            for j in range(GH):
                                score(it, p, k, j)
                        if k == 1 and live(it - 1, items):
                            transpose_out(it - 1, 1)
                        if k == 5 and live(it, items):
                            transpose_out(it, 0)
                        if k == 0 and live(it - 1, items):
                            weigh(it - 1, 1 - p, units - 1)
                        if k > 0 and live(it, items):
                            weigh(it, p, k - 1)

                steps(pe, items, step, tail=1)


def project_out(nc, sem, X, norm, wo, ident, heads_out):
    with ExitStack() as mem:
        aT = mem.enter_context(nc.sbuf_tensor("po_aT", [P, 2, KD, GTOK], F32))
        a = mem.enter_context(nc.sbuf_tensor("po_a", [P, 2, GT, DIM], F32))
        ps_aT = mem.enter_context(nc.psum_tensor("po_ps_aT", [P, KD, GTOK], F32))
        ps_y = [mem.enter_context(nc.psum_tensor(f"po_ps_y{p}", [P, GT, DIM], F32)) for p in range(2)]
        a_ready, aT_made, aT_ready, y_made, added = (sem("po_" + n) for n in ("a_ready", "aT_made", "aT_ready", "y_made", "added"))
        with nc.Block() as block:
            @block.gpsimd
            def _(pool):
                def step(u, p):
                    g = 2 * u + p
                    if some(g - 1):
                        pool.wait_ge(aT_made, g - 1)
                    for hg in range(HGROUPS):
                        last = nc.gpsimd.tensor_copy(
                            a[:, p, :, hg * GH * HD:(hg + 1) * GH * HD],
                            heads_out[:, bass.ds(g, 1), hg].rearrange("p a (t h) d -> p (a t) (h d)", h=GH))
                    last.then_inc(a_ready, 1)

                steps(pool, GROUPS, step)

            @block.scalar
            def _(act):
                def step(u, p):
                    act.wait_ge(aT_made, 2 * u + p + 1)
                    nc.scalar.copy(aT[:, p], ps_aT[:, :, :]).then_inc(aT_ready, 1)

                steps(act, GROUPS, step)

            @block.tensor
            def _(pe):
                def step(u, p):
                    g = 2 * u + p
                    if live(g, GROUPS):
                        pe.wait_ge(a_ready, g + 1)
                        if some(g):
                            pe.wait_ge(aT_ready, g)
                        for j in range(GT):
                            for k in range(KD):
                                last = nc.tensor.transpose(ps_aT[:, k, j * P:(j + 1) * P],
                                                           a[:, p, j, k * P:(k + 1) * P], ident)
                        last.then_inc(aT_made, 1)
                    if live(g - 1, GROUPS):
                        h, q = g - 1, 1 - p
                        pe.wait_ge(aT_ready, h + 1)
                        if some(h - 1):
                            pe.wait_ge(added, h - 1)
                        for j in range(GT):
                            for k in range(KD):
                                last = nc.tensor.matmul(ps_y[q][:, j, :], aT[:, q, k, j * P:(j + 1) * P], wo[:, k, :],
                                                        start=(k == 0), stop=(k == KD - 1))
                        last.then_inc(y_made, 1)

                steps(pe, GROUPS, step, tail=1)

            @block.vector
            def _(dve):
                def step(u, p):
                    g = 2 * u + p
                    dve.wait_ge(y_made, g + 1)
                    x4 = X[:, bass.ds(GT * g, GT), :]
                    nc.vector.tensor_tensor(x4, x4, ps_y[p][:, :, :], ALU.add).then_inc(added, 1)
                    dve.wait_ge(added, g + 1)
                    norm.statistics(x4, g)

                steps(dve, GROUPS, step)


def attention(nc, sem, X, norm, wq, wk, wv, wo, ident, inp):
    parts_dram = nc.dram_tensor("parts", [2, GROUPS, KD, P, PARTS, GTOK], BF16).ap()
    with ExitStack() as mem:
        heads_out = mem.enter_context(nc.sbuf_tensor(
            "heads_out", [P, BATCH * QBLOCKS, HGROUPS, GT * GH, HD], F32))
        with ExitStack() as inner:
            V = inner.enter_context(nc.sbuf_tensor("V", [P, TILES, HEADS, 2 * HD], F32))
            big = inner.enter_context(nc.sbuf_tensor("big", [P, P], BF16))
            tri = inner.enter_context(nc.sbuf_tensor("tri", [P, P], BF16))
            threshold = inner.enter_context(nc.sbuf_tensor("threshold", [P, 1], F32))
            make_mask(nc, sem, big, tri, threshold)
            project(nc, sem, X, norm, (wq, wk, wv), ident, V, parts_dram)
            attend(nc, sem, V, parts_dram, ((tri[:, :], threshold[:, 0:1]), big[:, :]), ident, heads_out)
        project_out(nc, sem, X, norm, wo, ident, heads_out)


def make_mask(nc, sem, big, tri, threshold):
    cleared = sem("mask_cleared")
    with nc.Block() as block:
        @block.gpsimd
        def _(pool):
            nc.gpsimd.memset(threshold[:, :], -THRESHOLD)
            nc.gpsimd.memset(big[:, :], 0.0)
            nc.gpsimd.memset(tri[:, :], 1.0).then_inc(cleared, 1)
            pool.wait_ge(cleared, 1)
            nc.gpsimd.affine_select(out=big[:, :], in_=big[:, :], compare_op=ALU.not_equal, fill=-1e30,
                                    base=0, pattern=[[-1, P]], channel_multiplier=1)
            nc.gpsimd.affine_select(out=tri[:, :], in_=tri[:, :], compare_op=ALU.is_gt, fill=0.0,
                                    base=0, pattern=[[-1, P]], channel_multiplier=1)


EXPERTS, TOP_K = 16, 4
HID = 176
HK = (P, HID - P)
SLOT_TILES = -(-(TOKENS * TOP_K + EXPERTS * (P - 1)) // P // 4) * 4
SLOTS = SLOT_TILES * P
WAYS = 4


def split_weights(nc, sem, name, jobs):
    piece = 1408
    pieces = [(d[:, c:min(c + piece, d.shape[1])], h[:, c:min(c + piece, d.shape[1])], l[:, c:min(c + piece, d.shape[1])])
              for d, h, l in jobs for c in range(0, d.shape[1], piece)]
    with ExitStack() as mem:
        raw = [mem.enter_context(nc.sbuf_tensor(f"{name}_raw{n}", [P, piece], F32)) for n in range(2)]
        loaded = [sem(f"{name}_raw_loaded{n}") for n in range(2)]
        high_ready, low_ready = sem(name + "_high_ready"), sem(name + "_low_ready")
        with nc.Block() as block:
            @block.sync
            def _(sp):
                for n, (d, _, _) in enumerate(pieces):
                    if some(n - 1):
                        sp.wait_ge(low_ready, n - 1)
                    sp.dma_start(raw[n % 2][0:d.shape[0], 0:d.shape[1]], d).then_inc(loaded[n % 2], 16)

            @block.scalar
            def _(act):
                for n, (d, h, _) in enumerate(pieces):
                    act.wait_ge(loaded[n % 2], 16 * (n // 2 + 1))
                    nc.scalar.copy(h, raw[n % 2][0:d.shape[0], 0:d.shape[1]]).then_inc(high_ready, 1)

            @block.vector
            def _(dve):
                for n, (d, h, l) in enumerate(pieces):
                    dve.wait_ge(high_ready, n + 1)
                    nc.vector.tensor_tensor(l, raw[n % 2][0:d.shape[0], 0:d.shape[1]], h.bitcast(F32),
                                            ALU.subtract).then_inc(low_ready, 1)


def expert_tiles(nc, sem, name, count, w13, w2, ident, source, shared=None, routed=None):
    cols = w13[0].shape[-1]
    with ExitStack() as mem:
        def sb(n, shape, dt=F32):
            return mem.enter_context(nc.sbuf_tensor(f"{name}_{n}", shape, dt))

        rows = [sb(f"rows{p}", [P, DIM]) for p in range(WAYS)]
        xT_hi, xT_lo = ([sb(f"xT_{n}{p}", [P, KD, P], F32R) for p in range(2)] for n in ("hi", "lo"))
        first, hid_in = sb("first", [P, HID]), sb("hid_in", [P, HID])
        hid = [sb(f"hid{p}", [P, 2 * P]) for p in range(2)]
        hT_hi, hT_lo = ([sb(f"hT_{n}{p}", [P, 2, P], F32R) for p in range(2)] for n in ("hi", "lo"))
        y = [sb(f"y{p}", [P, DIM]) for p in range(2)] if routed else None

        def ps(n):
            return [mem.enter_context(nc.psum_tensor(f"{name}_ps_{n}{p}", [P, 512], F32)) for p in range(2)]

        ps_x, ps_h, ps_t, ps_y = ps("x"), ps("h"), ps("t"), ps("y")
        names = ("zeroed", "rows_ready", "xT_hi_ready", "xT_lo_ready", "h_made", "first_ready", "prod_ready",
                 "hid_ready", "h_turned", "hT_hi_ready", "hT_lo_ready", "y_made", "y_ready")
        (zeroed, rows_ready, xT_hi_ready, xT_lo_ready, h_made, first_ready, prod_ready,
         hid_ready, h_turned, hT_hi_ready, hT_lo_ready, y_made, y_ready) = (sem(f"{name}_{n}") for n in names)
        x_turned = [sem(f"{name}_x_turned{p}") for p in range(WAYS)]
        rows_loaded = [sem(f"{name}_rows_loaded{p}") for p in range(WAYS)]
        copied = [sem(f"{name}_column_copied{p}") for p in range(WAYS)]
        first_copied = sem(name + "_first_columns_copied")
        stored = [sem(f"{name}_stored{p}") for p in range(2)]

        def run(eng, step, tail=0):
            steps(eng, count, step, tail, WAYS)

        with nc.Block() as block:
            @block.scalar
            def _(act):
                def step(u, p):
                    i = WAYS * u + p
                    if live(i, count):
                        if some(i - 1):
                            act.wait_ge(h_made, i - 1)
                        act.wait_ge(x_turned[p], u + 1)
                        nc.scalar.copy(xT_hi[p % 2][:, :, :], ps_x[p % 2][:, 0:DIM].rearrange("p (k t) -> p k t", k=KD)
                                       ).then_inc(xT_hi_ready, 1)
                    if live(i - 1, count):
                        q = (p - 1) % 2
                        if some(i - 1):
                            act.wait_ge(prod_ready, i - 1)
                        if some(i):
                            act.wait_ge(h_made, i)
                        nc.scalar.activation(first[:, :], ps_h[q][:, 0:HID], ACT.Silu if shared else ACT.Copy
                                             ).then_inc(first_ready, 1)
                    if live(i - 2, count):
                        q = (p - 2) % 2
                        if some(i - 3):
                            act.wait_ge(y_made, i - 3)
                        if some(i - 1):
                            act.wait_ge(h_turned, i - 1)
                        nc.scalar.copy(hT_hi[q][:, :, :], ps_t[q][:, 0:2 * P].rearrange("p (k t) -> p k t", k=2)
                                       ).then_inc(hT_hi_ready, 1)
                    if routed and live(i - 1, count):
                        q = (p - 1) % 2
                        if some(i):
                            act.wait_ge(prod_ready, i)
                        if some(i - 2):
                            act.wait_ge(h_turned, i - 2)
                        if isinstance(i, int) and i - 1 < 2:
                            act.wait_ge(zeroed, 1)
                        nc.scalar.activation(hid[q][:, 0:HID], hid_in[:, :], ACT.Silu).then_inc(hid_ready, 1)

                run(act, step, 3)

            @block.vector
            def _(dve):
                for p in range(2):
                    last = nc.vector.memset(hid[p][:, HID:], 0.0)
                last.then_inc(zeroed, 1)

                def step(u, p):
                    i = WAYS * u + p
                    if shared and live(i, count):
                        if some(u):
                            dve.wait_ge(x_turned[p], u)
                        if some(16 * u):
                            dve.wait_ge(rows_loaded[p], 16 * u)
                        shared["norm"].apply_tile(shared["X"], rows[p][:, :], i).then_inc(rows_ready, 1)
                    if live(i - lead, count):
                        n, q = i - lead, (p - lead) % 2
                        dve.wait_ge(xT_hi_ready, n + 1)
                        nc.vector.tensor_tensor(xT_lo[q][:, :, :], ps_x[q][:, 0:DIM].rearrange("p (k t) -> p k t", k=KD),
                                                xT_hi[q][:, :, :].bitcast(F32), ALU.subtract).then_inc(xT_lo_ready, 1)
                    if live(i - lead - 1, count):
                        n, q = i - lead - 1, (p - lead - 1) % 2
                        dve.wait_ge(first_ready, n + 1)
                        if routed:
                            if some(n):
                                dve.wait_ge(hid_ready, n)
                            out = hid_in[:, :]
                        else:
                            if some(n - 1):
                                dve.wait_ge(h_turned, n - 1)
                            out = hid[q][:, 0:HID]
                            nc.vector.tensor_copy(shared["logits"][:, bass.ds(n, 1), :].rearrange("p a e -> p (a e)"),
                                                  ps_h[q][:, 2 * HID:cols])
                        nc.vector.tensor_tensor(out, first[:, :], ps_h[q][:, HID:2 * HID], ALU.mult).then_inc(prod_ready, 1)
                    if live(i - lead - 2, count):
                        n, q = i - lead - 2, (p - lead - 2) % 2
                        dve.wait_ge(hT_hi_ready, n + 1)
                        nc.vector.tensor_tensor(hT_lo[q][:, :, :], ps_t[q][:, 0:2 * P].rearrange("p (k t) -> p k t", k=2),
                                                hT_hi[q][:, :, :].bitcast(F32), ALU.subtract).then_inc(hT_lo_ready, 1)
                    if live(i - lead - 3, count):
                        n, q = i - lead - 3, (p - lead - 3) % 2
                        dve.wait_ge(y_made, n + 1)
                        if routed:
                            un, qn = back_by(u, p, lead + 3)
                            if some(16 * stores_before(un, qn)):
                                dve.wait_ge(stored[q], 16 * stores_before(un, qn))
                            nc.vector.tensor_copy(y[q][:, :], ps_y[q][:, 0:DIM]).then_inc(y_ready, 1)
                        else:
                            xt = shared["X"][:, bass.ds(n, 1), :].rearrange("p a d -> p (a d)")
                            nc.vector.tensor_tensor(xt, xt, ps_y[q][:, 0:DIM], ALU.add).then_inc(y_ready, 1)

                lead = 1 if shared else 0
                run(dve, step, 3 + lead)

            @block.tensor
            def _(pe):
                expert_of = {}

                def step(u, p):
                    i = WAYS * u + p
                    if routed and p == 0:
                        first = max(WAYS * u - 3, 0) if isinstance(u, int) else WAYS * u - 3
                        number = min(WAYS * u + WAYS - 1, count) - first if isinstance(u, int) else WAYS + 2
                        values = routed["experts"](first, number)
                        back = WAYS * u - first if isinstance(u, int) else 3
                        expert_of.update({m - back: v for m, v in enumerate(values)})
                    if live(i, count):
                        if routed:
                            pe.wait_ge(rows_loaded[p], 16 * (u + 1))
                        else:
                            pe.wait_ge(rows_ready, i + 1)
                        if some(i - 1):
                            pe.wait_ge(xT_lo_ready, i - 1)
                        for k in range(KD):
                            last = nc.tensor.transpose(ps_x[p % 2][:, k * P:(k + 1) * P], rows[p][:, k * P:(k + 1) * P], ident)
                        last.then_inc(x_turned[p], 1)
                    if live(i - 1, count):
                        n, q = i - 1, (p - 1) % 2
                        expert = expert_of[p - 1] if routed else None
                        pe.wait_ge(xT_lo_ready, n + 1)
                        if some(n - 1):
                            pe.wait_ge(prod_ready, n - 1)
                        terms = [(a, b, k) for k in range(KD) for a, b in ((xT_hi, 0), (xT_lo, 0), (xT_hi, 1))]
                        for m, (a, b, k) in enumerate(terms):
                            last = nc.tensor.matmul(ps_h[q][:, 0:cols], a[q][:, k, :], w13_of(b, k, expert),
                                                    start=(m == 0), stop=(m == len(terms) - 1))
                        last.then_inc(h_made, 1)
                    if live(i - 2, count):
                        n, q = i - 2, (p - 2) % 2
                        if routed:
                            pe.wait_ge(hid_ready, n + 1)
                        else:
                            pe.wait_ge(prod_ready, n + 1)
                            if isinstance(n, int) and n < 2:
                                pe.wait_ge(zeroed, 1)
                        if some(n - 1):
                            pe.wait_ge(hT_lo_ready, n - 1)
                        for k in range(2):
                            last = nc.tensor.transpose(ps_t[q][:, k * P:(k + 1) * P], hid[q][:, k * P:(k + 1) * P], ident)
                        last.then_inc(h_turned, 1)
                    if live(i - 3, count):
                        n, q = i - 3, (p - 3) % 2
                        expert = expert_of[p - 3] if routed else None
                        pe.wait_ge(hT_lo_ready, n + 1)
                        if some(n - 1):
                            pe.wait_ge(y_ready, n - 1)
                        terms = [(a, b, k) for k in range(2) for a, b in ((hT_hi, 0), (hT_lo, 0), (hT_hi, 1))]
                        for m, (a, b, k) in enumerate(terms):
                            last = nc.tensor.matmul(ps_y[q][:, 0:DIM], a[q][0:HK[k], k, :], w2_of(b, k, expert),
                                                    start=(m == 0), stop=(m == len(terms) - 1))
                        last.then_inc(y_made, 1)

                def w13_of(part, k, expert):
                    if expert is None:
                        return w13[part][:, k, :]
                    return w13[part][:, k, bass.ds(expert, 1), :].rearrange("p a n -> p (a n)")

                def w2_of(part, k, expert):
                    if expert is None:
                        return w2[part][0:HK[k], k, :]
                    return w2[part][0:HK[k], k, bass.ds(expert, 1), :].rearrange("p a n -> p (a n)")

                run(pe, step, 3)

            if shared:
                @block.sync
                def _(sp):
                    def step(u, p):
                        i = WAYS * u + p
                        sp.wait_ge(rows_ready, i + 1)
                        sp.dma_start(source[bass.ds(i * P, P), :], rows[p][:, :]).then_inc(rows_loaded[p], 16)

                    run(sp, step)
                    for p in range(WAYS):
                        sp.wait_ge(rows_loaded[p], 16 * (count // WAYS))

            if routed:
                @block.gpsimd
                def _(pool):
                    column = routed["column"]

                    def step(u, p):
                        i = WAYS * u + p
                        if some(u):
                            pool.wait_ge(x_turned[p], 1)
                            pool.wait_ge(x_turned[p], u)
                        copy = nc.gpsimd.tensor_copy(column[p][:, :], routed["tokens"][:, bass.ds(i, 1)])
                        if isinstance(u, int):
                            copy.then_inc(first_copied, 1)
                            pool.wait_ge(first_copied, p + 1)
                        else:
                            copy.then_inc(copied[p], 1)
                            if some(u):
                                pool.wait_ge(copied[p], 1)
                                pool.wait_ge(copied[p], u)
                        nc.gpsimd.indirect_dma_start(
                            out=rows[p][:, :], out_offset=None, in_=source[:, :],
                            in_offset=bass.IndirectOffsetOnAxis(ap=column[p][:, 0:1], axis=0)).then_inc(rows_loaded[p], 16)

                    run(pool, step)

                @block.sync
                def _(sp):
                    def step(u, p):
                        i = WAYS * u + p
                        sp.wait_ge(y_ready, i + 1)
                        sp.dma_start(routed["out"][bass.ds(i * P, P), :], y[p % 2][:, :]).then_inc(stored[p % 2], 16)

                    run(sp, step)
                    for p in range(2):
                        sp.wait_ge(stored[p], 16 * (count // 2))


def back_by(u, p, n):
    return u + (p - n) // WAYS, (p - n) % WAYS


def stores_before(u, p):
    return (WAYS // 2) * u + p // 2


def route(nc, sem, name, logits, gate_b, tables, slots, shares, tile_expert, low, high):
    iota16, later, iota_slot, not_first = tables
    TE = TILES * EXPERTS
    with ExitStack() as mem:
        def sb(n, shape, dt=F32):
            return mem.enter_context(nc.sbuf_tensor(f"{name}_{n}", shape, dt))

        top, idx = sb("top", [P, TILES, 8]), sb("idx", [P, TILES, 8], U32)
        scores = sb("scores", [P, TILES, EXPERTS])
        idxf, total, inv = sb("idxf", [P, TOP_K, TILES]), sb("total", [P, TILES]), sb("inv", [P, TILES])
        onehot = sb("onehot", [P, TOP_K, TILES, EXPERTS])
        mask, mask16 = sb("mask", [P, TILES, EXPERTS]), sb("mask16", [P, TILES, EXPERTS], BF16)
        ones, later16 = sb("ones", [P, P], BF16), sb("later16", [P, P], BF16)
        totals, cum = sb("totals", [P, EXPERTS, TILES]), sb("cum", [P, EXPERTS, TILES])
        counts, counts_i = sb("counts", [P, EXPERTS]), sb("counts_i", [P, EXPERTS], I32)
        n_tiles, start, unit = sb("n_tiles", [P, EXPERTS]), sb("start", [P, EXPERTS]), sb("unit", [P, EXPERTS])
        slot = sb("slot", [P, TILES, EXPERTS])
        slotf, part_i = sb("slotf", [P, TOP_K, TILES]), sb("part_i", [P, TOP_K, TILES], I32)
        slot_i = sb("slot_i", [P, TOP_K, TILES], I32)
        reached, tile_e = sb("reached", [P, SLOT_TILES, EXPERTS - 1]), sb("tile_e", [P, SLOT_TILES])
        ps_before = mem.enter_context(nc.psum_tensor(name + "_ps_before", [P, TE], F32))
        ps_total = mem.enter_context(nc.psum_tensor(name + "_ps_total", [P, TE], F32))
        links, logits_ready, mask_ready, counted = (sem(f"{name}_{n}") for n in ("links", "sig_ready", "mask_ready", "counted"))
        vec = nc.vector
        with nc.Block() as block:
            @block.scalar
            def _(act):
                nc.scalar.activation(scores[:, :, :], logits, ACT.Sigmoid).then_inc(logits_ready, 1)

            @block.tensor
            def _(pe):
                pe.wait_ge(mask_ready, 1)
                m = mask16[:, :, :].rearrange("p t e -> p (t e)")
                nc.tensor.matmul(ps_before[:, :], later16[:, :], m, start=True, stop=True)
                nc.tensor.matmul(ps_total[:, :], ones[:, :], m, start=True, stop=True).then_inc(counted, 1)

            @block.vector
            def _(dve):
                c = Chain(dve, links, 64)
                c.item(0)
                vec.memset(ones[:, :], 1.0)
                vec.tensor_copy(later16[:, :], later)
                vec.memset(unit[:, :], 1.0)
                dve.wait_ge(logits_ready, 1)
                c.link(vec.tensor_tensor(scores[:, :, :], scores[:, :, :],
                                         gate_b.unsqueeze(1).to_broadcast([P, TILES, EXPERTS]), ALU.add))
                for t in range(TILES):
                    last = vec.max(top[:, t, :], scores[:, t, :])
                c.link(last)
                for t in range(TILES):
                    last = vec.max_index(idx[:, t, :], top[:, t, :], scores[:, t, :])
                c.link(last)
                vec.tensor_reduce(total[:, :], top[:, :, 0:TOP_K], AX.X, ALU.add)
                c.link(vec.tensor_copy(idxf[:, :, :], idx[:, :, 0:TOP_K].rearrange("p t k -> p k t")))
                vec.tensor_scalar(total[:, :], total[:, :], 2.0, None, ALU.mult)
                for k in range(TOP_K):
                    last = vec.tensor_tensor(onehot[:, k], iota16,
                                             idxf[:, k, :].unsqueeze(2).to_broadcast([P, TILES, EXPERTS]), ALU.is_equal)
                c.link(last)
                vec.reciprocal(inv[:, :], total[:, :])
                vec.tensor_tensor(mask[:, :, :], onehot[:, 0], onehot[:, 1], ALU.add)
                c.link(vec.tensor_tensor(slot[:, :, :], onehot[:, 2], onehot[:, 3], ALU.add))
                vec.tensor_tensor(mask16[:, :, :], mask[:, :, :], slot[:, :, :], ALU.add).then_inc(mask_ready, 1)
                c.link(vec.tensor_tensor(shares, top[:, :, 0:TOP_K],
                                         inv[:, :].unsqueeze(2).to_broadcast([P, TILES, TOP_K]), ALU.mult))
                dve.wait_ge(counted, 1)
                c.link(vec.tensor_copy(totals[:, :, :], ps_total[:, :].rearrange("p (t e) -> p e t", t=TILES)))
                c.link(vec.tensor_tensor_scan(cum[:, :, :].rearrange("p e t -> p (e t)"), not_first,
                                              totals[:, :, :].rearrange("p e t -> p (e t)"), 0.0, ALU.mult, ALU.add))
                c.link(vec.tensor_scalar(counts_i[:, :], cum[:, :, TILES - 1], float(P - 1), None, ALU.add))
                c.link(vec.tensor_scalar(counts_i[:, :], counts_i[:, :], 7, None, ALU.arith_shift_right))
                c.link(vec.tensor_copy(n_tiles[:, :], counts_i[:, :]))
                c.link(vec.tensor_tensor_scan(start[:, :], unit[:, :], n_tiles[:, :], 0.0, ALU.mult, ALU.add))
                c.link(vec.tensor_tensor(start[:, :], start[:, :], n_tiles[:, :], ALU.subtract))
                vec.tensor_scalar(counts[:, :], start[:, :], float(P), None, ALU.mult)
                vec.tensor_tensor(reached[:, :, :], iota_slot.unsqueeze(2).to_broadcast([P, SLOT_TILES, EXPERTS - 1]),
                                  start[:, 1:].unsqueeze(1).to_broadcast([P, SLOT_TILES, EXPERTS - 1]), ALU.is_ge)
                c.link(vec.tensor_tensor(cum[:, :, :], cum[:, :, :], totals[:, :, :], ALU.subtract))
                vec.tensor_reduce(tile_e[:, :], reached[:, :, :], AX.X, ALU.add)
                c.link(vec.tensor_tensor(cum[:, :, :], cum[:, :, :],
                                         counts[:, :].unsqueeze(2).to_broadcast([P, EXPERTS, TILES]), ALU.add))
                vec.tensor_copy(tile_expert, tile_e[:, :])
                c.link(vec.tensor_tensor(slot[:, :, :], ps_before[:, :].rearrange("p (t e) -> p t e", t=TILES),
                                         cum[:, :, :].rearrange("p e t -> p t e"), ALU.add))
                for k in range(TOP_K):
                    last = vec.tensor_tensor(onehot[:, k], onehot[:, k], slot[:, :, :], ALU.mult)
                c.link(last)
                c.link(vec.tensor_reduce(slotf[:, :, :], onehot[:, :, :, :], AX.X, ALU.add))
                vec.tensor_copy(slots, slotf[:, :, :].rearrange("p k t -> p t k"))
                c.link(vec.tensor_copy(slot_i[:, :, :], slotf[:, :, :]))
                c.link(vec.tensor_scalar(part_i[:, :, :], slot_i[:, :, :], P - 1, None, ALU.bitwise_and))
                vec.tensor_scalar(slot_i[:, :, :], slot_i[:, :, :], 7, None, ALU.arith_shift_right)
                c.link(vec.tensor_copy(low, part_i[:, :, :]))
                vec.tensor_copy(high, slot_i[:, :, :])


def invert_and_split(nc, sem, name, iota_slot, token_no, low, high, tokens, inp, w13, w2):
    per_turn = TILES // EXPERTS
    with ExitStack() as mem:
        def sb(n, shape, dt=F32):
            return mem.enter_context(nc.sbuf_tensor(f"{name}_{n}", shape, dt))

        at = [sb(f"at{p}", [P, TOP_K, P], F32R) for p in range(per_turn)]
        of = [sb(f"of{p}", [P, TOP_K, SLOT_TILES], F32R) for p in range(per_turn)]
        raw = [sb(f"raw13_{k}", [P, 2 * HID]) for k in range(KD)] + [sb(f"raw2_{k}", [HK[k], DIM]) for k in range(2)]
        source = [inp["w13"][k * P:(k + 1) * P] for k in range(KD)] + [inp["w2"][k * P:k * P + HK[k]] for k in range(2)]
        loaded, low_ready = ([sem(f"{name}_{n}{j}") for j in range(4)] for n in ("raw_loaded", "low_ready"))
        ps_inv = mem.enter_context(nc.psum_tensor(name + "_ps_inv", [P, SLOT_TILES], F32))
        hot_ready, hot_used, high_ready = (sem(f"{name}_{n}") for n in ("hot_ready", "hot_used", "high_ready"))

        def piece(part, j, e):
            w, k = ((w13, w2)[j // 2][part], j % 2)
            rows = P if j < 2 else HK[k]
            return w[0:rows, k, bass.ds(e, 1), :].rearrange("p a n -> p (a n)")

        def turns(eng, turn):
            turn(0)
            with eng.Fori(1, EXPERTS) as e:
                turn(e)

        with nc.Block() as block:
            @block.sync
            def _(sp):
                def turn(e):
                    for j in range(4):
                        if some(e):
                            sp.wait_ge(low_ready[j], e)
                        cols = raw[j].shape[-1]
                        sp.dma_start(raw[j][:, :], source[j][:, bass.ds(e * cols, cols)]).then_inc(loaded[j], 16)

                turns(sp, turn)

            @block.scalar
            def _(act):
                def turn(e):
                    for j in range(4):
                        act.wait_ge(loaded[j], 16 * (e + 1))
                        nc.scalar.copy(piece(0, j, e), raw[j][:, :]).then_inc(high_ready, 1)

                turns(act, turn)

            @block.gpsimd
            def _(pool):
                def turn(e):
                    for j in range(4):
                        pool.wait_ge(high_ready, 4 * e + j + 1)
                        nc.gpsimd.tensor_tensor(piece(1, j, e), raw[j][:, :], piece(0, j, e).bitcast(F32), ALU.subtract
                                                ).then_inc(low_ready[j], 1)

                turns(pool, turn)

            @block.vector
            def _(dve):
                def turn(e):
                    for p in range(per_turn):
                        t = per_turn * e + p
                        if some(t - 1):
                            dve.wait_ge(hot_used, t - 1)
                        nc.vector.tensor_tensor(at[p][:, :, :], iota_slot[:, 0:P].unsqueeze(1).to_broadcast([P, TOP_K, P]),
                                                low[:, :, bass.ds(t, 1)].to_broadcast([P, TOP_K, P]), ALU.is_equal)
                        for k in range(TOP_K):
                            last = nc.vector.tensor_scalar(of[p][:, k, :], iota_slot, high[:, k, bass.ds(t, 1)],
                                                           token_no[:, bass.ds(t, 1)], ALU.is_equal, ALU.mult)
                        last.then_inc(hot_ready, 1)

                turns(dve, turn)
                dve.wait_ge(hot_used, TILES)
                nc.vector.tensor_copy(tokens, ps_inv[:, :])

            @block.tensor
            def _(pe):
                def turn(e):
                    for p in range(per_turn):
                        t = per_turn * e + p
                        pe.wait_ge(hot_ready, t + 1)
                        for k in range(TOP_K):
                            last = nc.tensor.matmul(ps_inv[:, :], at[p][:, k, :], of[p][:, k, :],
                                                    start=(isinstance(t, int) and t == 0 and k == 0), stop=(k == TOP_K - 1),
                                                    skip_group_check=True)
                        last.then_inc(hot_used, 1)

                turns(pe, turn)


class Combine:

    def __init__(self, nc, sem, name, sb, X, norm, slots, shares, y_dram):
        self.nc, self.X, self.norm, self.slots, self.shares, self.y_dram = nc, X, norm, slots, shares, y_dram
        self.rows = [sb(f"{name}_rows{p}", [P, GT, TOP_K, DIM]) for p in range(2)]
        self.index = [sb(f"{name}_index{p}", [P, GT, TOP_K], I32) for p in range(2)]
        self.index_loaded = [sem(f"{name}_index_loaded{p}") for p in range(2)]
        self.rows_loaded = [[sem(f"{name}_rows_loaded{p}{j}") for j in range(GT)] for p in range(2)]
        self.rows_added = [sem(f"{name}_rows_added{p}") for p in range(2)]
        self.links = sem(name + "_links")

    def copy_index(self, sp):
        def step(u, p):
            if some(u):
                sp.wait_ge(self.rows_added[p], u)
            sp.dma_start(self.index[p][:, :, :], self.slots[:, bass.ds(GT * (2 * u + p), GT), :]
                         ).then_inc(self.index_loaded[p], 16)

        steps(sp, GROUPS, step)

    def gather(self, pool):
        def turn(loads):
            for p in range(2):
                if not isinstance(loads, int):
                    pool.wait_ge(self.index_loaded[p], 16)
                pool.wait_ge(self.index_loaded[p], loads)
                for j in range(GT):
                    for k in range(TOP_K):
                        self.nc.gpsimd.indirect_dma_start(
                            out=self.rows[p][:, j, k, :], out_offset=None, in_=self.y_dram[:, :],
                            in_offset=bass.IndirectOffsetOnAxis(ap=self.index[p][:, j, k:k + 1], axis=0)
                        ).then_inc(self.rows_loaded[p][j], 16)

        turn(16)
        with pool.Fori(2 * 16, 16 * (GROUPS // 2) + 1, 16) as loads:
            turn(loads)

    def add_tiles(self, dve, chain, u, p, tiles):
        for j in tiles:
            dve.wait_ge(self.rows_loaded[p][j], 16 * TOP_K * (u + 1))
        for k in range(TOP_K):
            for j in tiles:
                xt = self.X[:, bass.ds(GT * (2 * u + p) + j, 1), :].rearrange("p a d -> p (a d)")
                last = self.nc.vector.scalar_tensor_tensor(
                    out=xt, in0=self.rows[p][:, j, k, :],
                    scalar=self.shares[:, bass.ds(GT * (2 * u + p) + j, 1), k], in1=xt, op0=ALU.mult, op1=ALU.add)
                if j == tiles[0]:
                    chain.link(last, wait=False)
                else:
                    chain.link(last)

    def finish_group(self, u, p):
        x4 = self.X[:, bass.ds(GT * (2 * u + p), GT), :]
        self.norm.statistics(x4, 2 * u + p).then_inc(self.rows_added[p], 1)


def combine_and_store(nc, sem, name, X, norm, slots, shares, y_dram, out):
    with ExitStack() as mem:
        def sb(n, shape, dt=F32):
            return mem.enter_context(nc.sbuf_tensor(n, shape, dt))

        combine = Combine(nc, sem, name, sb, X, norm, slots, shares, y_dram)
        x_stored = sem(name + "_x_stored")
        with nc.Block() as block:
            @block.gpsimd
            def _(pool):
                combine.gather(pool)

            @block.sync
            def _(sp):
                combine.copy_index(sp)

            @block.scalar
            def _(act):
                def step(u, p):
                    g = 2 * u + p
                    act.wait_ge(combine.rows_added[p], u + 1)
                    act.dma_start(out[bass.ds(GTOK * g, GTOK), :].rearrange("(j p) d -> p j d", p=P),
                                  X[:, bass.ds(GT * g, GT), :]).then_inc(x_stored, 16)

                steps(act, GROUPS, step)
                act.wait_ge(x_stored, 16 * GROUPS)

            @block.vector
            def _(dve):
                chain = Chain(dve, combine.links, GT * TOP_K)

                def step(u, p):
                    chain.item(2 * u + p)
                    combine.add_tiles(dve, chain, u, p, (0, 1))
                    combine.add_tiles(dve, chain, u, p, (2, 3))
                    combine.finish_group(u, p)

                steps(dve, GROUPS, step)


def moe(nc, sem, name, X, norm, ident, inp, dram, slots, shares):
    xhat, y_dram = dram
    with ExitStack() as mem:
        def sb(n, shape, dt=F32):
            return mem.enter_context(nc.sbuf_tensor(f"{name}_{n}", shape, dt))

        tokens, tile_expert = sb("tokens", [P, SLOT_TILES], I32), sb("tile_expert", [P, SLOT_TILES], I32)
        column = [sb(f"column{p}", [P, 1], I32) for p in range(WAYS)]
        iota_slot, token_no = sb("iota_slot", [P, SLOT_TILES]), sb("token_no", [P, TILES])
        low, high = sb("low", [P, TOP_K, TILES]), sb("high", [P, TOP_K, TILES])
        with ExitStack() as scratch:
            def tmp(n, shape, dt=F32):
                return scratch.enter_context(nc.sbuf_tensor(f"{name}_{n}", shape, dt))

            cols = 2 * HID + EXPERTS
            w13 = [tmp(f"ws13_{n}", [P, KD, cols], F32R) for n in ("hi", "lo")]
            w2 = [tmp(f"ws2_{n}", [P, 2, DIM], F32R) for n in ("hi", "lo")]
            logits, gate_b = tmp("logits", [P, TILES, EXPERTS]), tmp("gate_b", [P, EXPERTS])
            iota16, not_first = tmp("iota16", [P, TILES, EXPERTS]), tmp("not_first", [P, EXPERTS * TILES])
            later = tmp("later", [P, P])
            tables(nc, sem, name, inp, gate_b, iota16, iota_slot, token_no, not_first, later)
            split_weights(nc, sem, name + "_ws", [
                (inp["ws13"][k * P:(k + 1) * P, :], w13[0][:, k, :], w13[1][:, k, :]) for k in range(KD)] + [
                (inp["ws2"][k * P:k * P + HK[k], :], w2[0][0:HK[k], k, :], w2[1][0:HK[k], k, :]) for k in range(2)])
            halve(nc, sem, name, [w[0:HK[k], k, :] for w in w2 for k in range(2)])
            expert_tiles(nc, sem, name + "_shared", TILES, w13, w2, ident, xhat,
                         shared={"X": X, "norm": norm, "logits": logits})
            route(nc, sem, name + "_route", logits[:, :, :], gate_b[:, :],
                  (iota16[:, :, :], later[:, :], iota_slot[:, :], not_first[:, :]),
                  slots[:, :, :], shares[:, :, :], tile_expert[:, :], low[:, :, :], high[:, :, :])
        with ExitStack() as big:
            w13 = [big.enter_context(nc.sbuf_tensor(f"{name}_w13_{n}", [P, KD, EXPERTS, 2 * HID], F32R)) for n in ("hi", "lo")]
            w2 = [big.enter_context(nc.sbuf_tensor(f"{name}_w2_{n}", [P, 2, EXPERTS, DIM], F32R)) for n in ("hi", "lo")]

            invert_and_split(nc, sem, name + "_invert", iota_slot[:, :], token_no[:, :], low[:, :, :], high[:, :, :],
                             tokens[:, :], inp, w13, w2)

            def experts(first, number):
                _, values = nc.values_load_multi_w_load_instructions(
                    tile_expert[0:1, bass.ds(first, number)], engines=[mybir.EngineType.PE], min_val=0, max_val=EXPERTS - 1,
                    skip_runtime_bounds_check_because="a sum of EXPERTS - 1 comparisons, so 0 to EXPERTS - 1")
                return values

            expert_tiles(nc, sem, name + "_routed", SLOT_TILES, w13, w2, ident, xhat,
                         routed={"tokens": tokens, "column": column,
                                 "experts": experts, "out": y_dram})


def halve(nc, sem, name, parts):
    with nc.Block() as block:
        @block.vector
        def _(dve):
            for w in parts:
                nc.vector.tensor_scalar(w, w.bitcast(F32), 0.5, None, ALU.mult)


def tables(nc, sem, name, inp, gate_b, iota16, iota_slot, token_no, not_first, later):
    loaded = sem(name + "_tables_loaded")
    pairs = [(gate_b[:, :], inp["gate_b"]), (iota16[:, :, :], inp["iota16"].rearrange("p (t e) -> p t e", e=EXPERTS)),
             (iota_slot[:, :], inp["iota_slot"]), (token_no[:, :], inp["token_no"]), (not_first[:, :], inp["not_first"]),
             (later[:, :], inp["later"])]
    with nc.Block() as block:
        @block.sync
        def _(sp):
            for to, of in pairs:
                sp.dma_start(to, of).then_inc(loaded, 16)
            sp.wait_ge(loaded, 16 * len(pairs))


DECAY = 0.95


def smear(nc, sem, X, norm, ident, inp, slots, shares, y_dram):
    scale = float(nc_sqrt(1.0 - DECAY))
    with ExitStack() as mem:
        def sb(n, shape, dt=F32):
            return mem.enter_context(nc.sbuf_tensor("sm_" + n, shape, dt))

        def ps(n, shape):
            return mem.enter_context(nc.psum_tensor("sm_" + n, shape, F32))

        wg, wv, wq, wo = (sb(n, [P, KD, DIM]) for n in ("wg", "wv", "wq", "wo"))
        bias = sb("bias", [P, 2, KD])
        decay = sb("decay", [P, GTOK])
        xn, xT = sb("xn", [P, 2, GT, DIM]), sb("xT", [P, 2, KD, GTOK])
        gate, que, store = sb("gate", [P, KD, GTOK]), sb("que", [P, KD, GTOK]), sb("store", [P, KD, GTOK])
        kept = sb("kept", [P, 2, KD, GTOK])
        load = sb("load", [P, 2, KD, GTOK])
        ps_xT, ps_y = ps("ps_xT", [P, KD, GTOK]), ps("ps_y", [P, GT, DIM])
        ps_g, ps_v, ps_q = (ps("ps_" + n, [P, GTOK]) for n in "gvq")
        combine = Combine(nc, sem, "sm_combine", sb, X, norm, slots, shares, y_dram)
        root_work, root_bits = sb("root_work", [P, TILES // BATCH]), sb("root_bits", [P, TILES // BATCH], I32)
        root_links = sem("sm_root_links")
        loaded = sem("sm_loaded")
        with nc.Block() as block:
            @block.sync
            def _(sp):
                for to, of in ((wg, "l1_wg"), (wv, "l1_wv"), (wq, "l1_wq"), (wo, "l1_wo")):
                    sp.dma_start(to[:, :, :], inp[of].rearrange("(k p) n -> p k n", p=P)).then_inc(loaded, 16)
                sp.dma_start(bias[:, :, :], inp["l1_bias"].rearrange("p (a b) -> p a b", a=2)).then_inc(loaded, 16)
                sp.wait_ge(loaded, 16 * 5)

            @block.vector
            def _(dve):
                nc.vector.memset(decay[:, :], DECAY)

        names = ("xn_ready", "xT_made", "xT_ready", "g_made", "v_made", "q_made", "gate_ready", "que_ready",
                 "store_ready", "kept_ready", "load_ready", "y_made", "added")
        (xn_ready, xT_made, xT_ready, g_made, v_made, q_made, gate_ready, que_ready,
         store_ready, kept_ready, load_ready, y_made, added) = (sem("sm_" + n) for n in names)
        with nc.Block() as block:
            @block.gpsimd
            def _(pool):
                combine.gather(pool)

            @block.sync
            def _(sp):
                combine.copy_index(sp)

            @block.vector
            def _(dve):
                adds, roots = Chain(dve, combine.links, GT * TOP_K), Chain(dve, root_links, Norm.BATCH_LINKS)

                def memory(h, q, m):
                    n = KD * h + m + 1
                    dve.wait_ge(v_made, n)
                    dve.wait_ge(gate_ready, n)
                    nc.vector.scalar_tensor_tensor(out=store[:, m, :], in0=ps_v[:, :], scalar=scale,
                                                   in1=gate[:, m, :], op0=ALU.mult, op1=ALU.mult
                                                   ).then_inc(store_ready, 1)
                    dve.wait_ge(store_ready, n)
                    initial = kept[:, 0, m, GTOK - 1:GTOK] if q == 1 else 0.0
                    nc.vector.tensor_tensor_scan(kept[:, q, m, :], decay[:, :], store[:, m, :], initial,
                                                 ALU.mult, ALU.add).then_inc(kept_ready, 1)
                    dve.wait_ge(que_ready, n)
                    if m == 0:
                        if some(h - 1):
                            dve.wait_ge(y_made, h - 1)
                    dve.wait_ge(kept_ready, n)
                    nc.vector.scalar_tensor_tensor(out=load[:, q, m, :], in0=kept[:, q, m, :], scalar=scale,
                                                   in1=que[:, m, :], op0=ALU.mult, op1=ALU.mult
                                                   ).then_inc(load_ready, 1)

                def turn(u, p):
                    n = 2 * u + p
                    if live(n, GROUPS):
                        adds.item(n)
                        combine.add_tiles(dve, adds, u, p, (0, 1))
                    if live(n - 2, GROUPS):
                        memory(n - 2, p, 0)
                    if live(n, GROUPS):
                        combine.add_tiles(dve, adds, u, p, (2, 3))
                        combine.finish_group(u, p)
                        if p == 1:
                            dve.wait_ge(combine.rows_added[1], u + 1)
                            roots.item(u)
                            norm.of_batch(roots, u, root_work[:, :], root_bits[:, :])
                    if live(n - 1, GROUPS):
                        h, q = n - 1, 1 - p
                        if some(h - 1):
                            dve.wait_ge(xT_made, h - 1)
                        norm.apply(X[:, bass.ds(GT * h, GT), :], xn[:, q], h).then_inc(xn_ready, 1)
                    if live(n - 2, GROUPS):
                        memory(n - 2, p, 1)
                    if live(n - 3, GROUPS):
                        h = n - 3
                        dve.wait_ge(y_made, h + 1)
                        x4 = X[:, bass.ds(GT * h, GT), :]
                        nc.vector.tensor_tensor(x4, x4, ps_y[:, :, :], ALU.add).then_inc(added, 1)
                        dve.wait_ge(added, h + 1)
                        norm.statistics(x4, h)

                steps(dve, GROUPS, turn, tail=3, head=2)

            @block.scalar
            def _(act):
                def turn(u, p):
                    g = 2 * u + p
                    if live(g - 2, GROUPS):
                        for m in range(KD):
                            n = KD * (g - 2) + m + 1
                            if some(n - KD):
                                act.wait_ge(store_ready, n - KD)
                            act.wait_ge(g_made, n)
                            nc.scalar.activation(gate[:, m, :], ps_g[:, :], ACT.Sigmoid, bias=bias[:, 0, m:m + 1]
                                                 ).then_inc(gate_ready, 1)
                            if some(n - KD):
                                act.wait_ge(load_ready, n - KD)
                            act.wait_ge(q_made, n)
                            nc.scalar.activation(que[:, m, :], ps_q[:, :], ACT.Sigmoid, bias=bias[:, 1, m:m + 1]
                                                 ).then_inc(que_ready, 1)
                    if live(g - 1, GROUPS):
                        act.wait_ge(xT_made, g)
                        nc.scalar.copy(xT[:, 1 - p], ps_xT[:, :, :]).then_inc(xT_ready, 1)

                steps(act, GROUPS, turn, tail=2, head=2)

            @block.tensor
            def _(pe):
                def turn(u, p):
                    g = 2 * u + p
                    if live(g - 2, GROUPS):
                        h = g - 2
                        pe.wait_ge(xT_ready, h + 1)
                        for m in range(KD):
                            n = KD * h + m
                            for w, out, made, read in ((wg, ps_g, g_made, gate_ready), (wv, ps_v, v_made, store_ready),
                                                       (wq, ps_q, q_made, que_ready)):
                                if some(n):
                                    pe.wait_ge(read, n)
                                for k in range(KD):
                                    last = nc.tensor.matmul(out[:, :], w[:, k, m * P:(m + 1) * P], xT[:, p, k, :],
                                                            start=(k == 0), stop=(k == KD - 1))
                                last.then_inc(made, 1)
                    if live(g - 3, GROUPS):
                        h, q = g - 3, 1 - p
                        pe.wait_ge(load_ready, KD * (h + 1))
                        if some(h):
                            pe.wait_ge(added, h)
                        for j in range(GT):
                            for k in range(KD):
                                last = nc.tensor.matmul(ps_y[:, j, :], load[:, q, k, j * P:(j + 1) * P], wo[:, k, :],
                                                        start=(k == 0), stop=(k == KD - 1))
                        last.then_inc(y_made, 1)
                    if live(g - 1, GROUPS):
                        h, q = g - 1, 1 - p
                        pe.wait_ge(xn_ready, h + 1)
                        if some(h):
                            pe.wait_ge(xT_ready, h)
                        for j in range(GT):
                            for k in range(KD):
                                last = nc.tensor.transpose(ps_xT[:, k, j * P:(j + 1) * P],
                                                           xn[:, q, j, k * P:(k + 1) * P], ident)
                        last.then_inc(xT_made, 1)

                steps(pe, GROUPS, turn, tail=3, head=2)


def nc_sqrt(x):
    import numpy as np

    return np.float32(np.sqrt(x))


def load_x(nc, sem, x_dram, X, norm, consts):
    loaded = sem("loaded")
    x_loaded = [sem(f"x_loaded{g}") for g in range(GROUPS)]
    with nc.Block() as block:
        @block.sync
        def _(sp):
            for g in range(GROUPS):
                sp.dma_start(X[:, GT * g:GT * (g + 1), :],
                             x_dram[g * GTOK:(g + 1) * GTOK, :].rearrange("(j p) d -> p j d", p=P)).then_inc(x_loaded[g], 16)
            for to, of in consts:
                sp.dma_start(to, of).then_inc(loaded, 16)
            sp.wait_ge(loaded, 16 * len(consts))

        @block.vector
        def _(dve):
            for g in range(GROUPS):
                dve.wait_ge(x_loaded[g], 16)
                norm.statistics(X[:, GT * g:GT * (g + 1), :], g)


def scale_weights(nc, sem, w_dense, w_b):
    scaled = sem("scaled")
    with nc.Block() as block:
        @block.vector
        def _(dve):
            nc.vector.tensor_scalar(w_dense[:, :, :], w_dense[:, :, :], 0.5, None, ALU.mult).then_inc(scaled, 1)
            nc.vector.tensor_scalar(w_b[:, :], w_b[:, :], 0.5 * 16.0, None, ALU.mult).then_inc(scaled, 1)


def macaron_kernel(nc, out, **inp):
    with ExitStack():
        taken = []

        def sem(name):
            taken.append(nc.alloc_semaphore(name))
            return taken[-1]

        def next_stage():
            nc.clear_and_free_semaphores(taken)
            nc.all_engine_barrier()
            taken.clear()

        with ExitStack() as outer:
            def keep(n, shape, dt=F32):
                return outer.enter_context(nc.sbuf_tensor(n, shape, dt))

            X = keep("X", [P, TILES, DIM])
            ident = keep("ident", [P, P])
            norm = Norm(nc, keep)
            with ExitStack() as mem:
                def sb(n, shape, dt=F32):
                    return mem.enter_context(nc.sbuf_tensor(n, shape, dt))

                w_lora, w_dense, w_b = sb("w_lora", [P, KD, LA]), sb("w_dense", [P, KD, DIM]), sb("w_b", [P, DIM])
                iota8 = sb("iota8", [P, GT, 2, 8])
                wq, wk, wv, wo = (sb(n, [P, KD, DIM]) for n in ("wq", "wk", "wv", "wo"))

                def chunks(w):
                    return w.rearrange("(k p) n -> p k n", p=P)

                load_x(nc, sem, inp["x"], X, norm, [
                    (w_lora[:, :, :], chunks(inp["w_lora"])), (w_dense[:, :, :], chunks(inp["w_dense"])),
                    (w_b[:, :], inp["w_b"]), (ident[:, :], inp["ident"]),
                    (iota8[:, :, :, :], inp["iota8"].rearrange("p (a b c) -> p a b c", a=GT, b=2)),
                    (wq[:, :, :], chunks(inp["wq"])), (wk[:, :, :], chunks(inp["wk"])),
                    (wv[:, :, :], chunks(inp["wv"])), (wo[:, :, :], chunks(inp["wo"]))])
                scale_weights(nc, sem, w_dense, w_b)
                norm.finish(sem, "ffn1")
                lora_ffn(nc, "ffn1", sem, X, norm, w_lora, w_dense, w_b[:, :], ident[:, :], iota8)
                norm.finish(sem, "attn")
                attention(nc, sem, X, norm, wq, wk, wv, wo, ident[:, :], inp)
                norm.finish(sem, "ffn2")
                lora_ffn(nc, "ffn2", sem, X, norm, w_lora, w_dense, w_b[:, :], ident[:, :], iota8)
            slots, shares = keep("slots", [P, TILES, TOP_K], I32), keep("shares", [P, TILES, TOP_K])
            xhat = nc.dram_tensor("xhat", [TOKENS, DIM], F32).ap()
            y_dram = nc.dram_tensor("y_slots", [SLOTS, DIM], F32).ap()
            next_stage()
            norm.finish(sem, "moe1")
            moe(nc, sem, "moe1", X, norm, ident[:, :], inp, (xhat, y_dram), slots, shares)
            next_stage()
            smear(nc, sem, X, norm, ident[:, :], inp, slots, shares, y_dram)
            norm.finish(sem, "moe2")
            moe(nc, sem, "moe2", X, norm, ident[:, :], inp, (xhat, y_dram), slots, shares)
            combine_and_store(nc, sem, "combine", X, norm, slots, shares, y_dram, out)


def lay_out(a):
    import numpy as np

    c = np.ascontiguousarray
    f = np.float32
    d = {k: np.asarray(v) for k, v in a.items()}
    return {
        "x": c(d["L0_attn_x"].reshape(TOKENS, DIM)),
        "w_lora": c(np.concatenate([d["L0_ffn_A_w"].reshape(LER, DIM).T, d["L0_ffn_gate_w"].T], 1)),
        "w_dense": c(d["L0_ffn_weight"].T),
        "w_b": c(d["L0_ffn_B_w"].transpose(0, 2, 1).reshape(LER, DIM)),
        "wq": c(d["L0_attn_Wq"].T), "wk": c(d["L0_attn_Wk"].T), "wv": c(d["L0_attn_Wv"].T), "wo": c(d["L0_attn_Wo"].T),
        "ident": np.eye(P, dtype=f),
        "ws13": c(np.concatenate([d["L1_ffn_w1_shared"], d["L1_ffn_w3_shared"], d["L1_ffn_gate_w"].T], 1)),
        "ws2": c(d["L1_ffn_w2_shared"]),
        "w13": c(np.concatenate([d["L1_ffn_w1_routed"], d["L1_ffn_w3_routed"]], 2).transpose(1, 0, 2).reshape(DIM, -1)),
        "w2": c(d["L1_ffn_w2_routed"].transpose(1, 0, 2).reshape(HID, -1)),
        "gate_b": c(np.tile(d["L1_ffn_gate_b"], (P, 1))),
        "l1_wg": c(d["L1_attn_Wg"]), "l1_wv": c(d["L1_attn_Wv"]), "l1_wq": c(d["L1_attn_Wq"]), "l1_wo": c(d["L1_attn_Wo"]),
        "l1_bias": c(np.concatenate([d["L1_attn_bg"].reshape(KD, P), d["L1_attn_bq"].reshape(KD, P)]).T),
        "iota16": c(np.tile(np.arange(EXPERTS, dtype=f), (P, TILES))),
        "iota_slot": c(np.tile(np.arange(SLOT_TILES, dtype=f), (P, 1))),
        "token_no": c((np.arange(TILES)[None, :] * P + np.arange(P)[:, None]).astype(f)),
        "not_first": c(np.tile((np.arange(TILES) > 0).astype(f), (P, EXPERTS))),
        "later": np.triu(np.ones((P, P), f), 1),
        "iota8": c(np.tile(np.arange(8, dtype=f), (P, GT * 2))),
    }


def kernel(**inputs):
    import numpy as np
    import concourse.bacc as bacc
    from concourse.bass_utils import run_bass_kernel_spmd

    nc = bacc.Bacc("TRN2", target_bir_lowering=False, num_devices=1)
    arrays = lay_out(inputs)
    args = {n: nc.dram_tensor(f"in_{n}", a.shape, mybir.dt.from_np(a.dtype), kind="ExternalInput").ap()
            for n, a in arrays.items()}
    out = nc.dram_tensor("out", [TOKENS, DIM], F32, kind="ExternalOutput").ap()
    macaron_kernel(nc, out, **args)
    r = run_bass_kernel_spmd(nc, [{f"in_{n}": a for n, a in arrays.items()}], core_ids=[0])
    return r.results[0]["out"].reshape(BATCH, SEQ, DIM)
```

```python
import concourse.bass as bass
from concourse import mybir
from contextlib import ExitStack

P = 128
F32, F32R, BF16 = mybir.dt.float32, mybir.dt.float32r, mybir.dt.bfloat16
I32, U32 = mybir.dt.int32, mybir.dt.uint32
ACT, ALU, AX = mybir.ActivationFunctionType, mybir.AluOpType, mybir.AxisListType
EPS_NORM = 1e-5

BATCH, SEQ, DIM = 4, 1024, 256
TOKENS = BATCH * SEQ
TILES = TOKENS // P
KD = DIM // P
GT = 4
GROUPS = TILES // GT
GTOK = GT * P


def some(count):
    return not isinstance(count, int) or count > 0


def live(step, count):
    return not isinstance(step, int) or 0 <= step < count


def steps(eng, count, step, tail=0, ways=2, head=1):
    for n in range(ways * head):
        step(n // ways, n % ways)
    with eng.Fori(head, count // ways) as u:
        for p in range(ways):
            step(u, p)
    for n in range(count, count + tail):
        step(n // ways, n % ways)


def back(u, p):
    return (u, 0) if p else (u - 1, 1)


class Chain:

    def __init__(self, eng, sem, per_item):
        self.eng, self.sem, self.per_item = eng, sem, per_item

    def item(self, n):
        self.base, self.done = n * self.per_item, 0

    def link(self, instruction, wait=True):
        self.done += 1
        assert self.done <= self.per_item
        instruction.then_inc(self.sem, 1)
        if wait:
            self.eng.wait_ge(self.sem, self.base + self.done)


class Norm:

    def __init__(self, nc, sb):
        self.nc = nc
        self.stats, self.mean, self.rstd = sb("stats", [P, TILES, 6]), sb("mean", [P, TILES]), sb("rstd", [P, TILES])
        self.var, self.work = sb("var", [P, TILES]), sb("work", [P, TILES])

    def statistics(self, x4, g):
        for j in range(GT):
            last = self.nc.vector.bn_stats(self.stats[:, bass.ds(GT * g + j, 1), :], x4[:, j, :])
        return last

    def prepare_finish(self, sem, name):
        self.links, self.var_ready, self.root_ready = (sem(f"{name}_{n}") for n in ("norm_links", "var_ready", "root_ready"))

    def finish_on_vector(self, dve):
        s, vec = self.stats, self.nc.vector
        mean, var, rstd, work = self.mean[:, :], self.var[:, :], self.rstd[:, :], self.work[:, :]
        chain = Chain(dve, self.links, 11)
        chain.item(0)
        vec.tensor_tensor(mean, s[:, :, 1], s[:, :, 4], ALU.add)
        vec.tensor_tensor(var, s[:, :, 2], s[:, :, 5], ALU.add)
        chain.link(vec.tensor_tensor(work, s[:, :, 1], s[:, :, 4], ALU.subtract))
        vec.tensor_scalar(mean, mean, 0.5, None, ALU.mult)
        vec.tensor_scalar(var, var, 1.0 / DIM, EPS_NORM, ALU.mult, ALU.add)
        chain.link(vec.tensor_tensor(work, work, work, ALU.mult))
        chain.link(vec.scalar_tensor_tensor(out=var, in0=work, scalar=0.25, in1=var, op0=ALU.mult, op1=ALU.add))
        vec.tensor_copy(work, var).then_inc(self.var_ready, 1)
        dve.wait_ge(self.root_ready, 1)
        chain.link(vec.reciprocal(rstd, work))
        chain.link(vec.tensor_tensor(work, rstd, rstd, ALU.mult))
        chain.link(vec.tensor_tensor(work, work, var, ALU.mult))
        chain.link(vec.tensor_scalar(work, work, -0.5, 1.5, ALU.mult, ALU.add))
        chain.link(vec.tensor_tensor(rstd, rstd, work, ALU.mult))

    def finish_on_scalar(self, act):
        act.wait_ge(self.var_ready, 1)
        self.nc.scalar.activation(self.work[:, :], self.var[:, :], ACT.Sqrt).then_inc(self.root_ready, 1)

    def finish(self, sem, name):
        self.prepare_finish(sem, name)
        with self.nc.Block() as block:
            @block.vector
            def _(dve):
                self.finish_on_vector(dve)

            @block.scalar
            def _(act):
                self.finish_on_scalar(act)

    def of_batch(self, chain, b, work, bits):
        vec, n = self.nc.vector, TILES // BATCH
        s = self.stats[:, bass.ds(n * b, n), :]
        mean, var, rstd = (a[:, bass.ds(n * b, n)] for a in (self.mean, self.var, self.rstd))
        vec.tensor_tensor(mean, s[:, :, 1], s[:, :, 4], ALU.add)
        vec.tensor_tensor(var, s[:, :, 2], s[:, :, 5], ALU.add)
        chain.link(vec.tensor_tensor(work, s[:, :, 1], s[:, :, 4], ALU.subtract))
        vec.tensor_scalar(mean, mean, 0.5, None, ALU.mult)
        vec.tensor_scalar(var, var, 1.0 / DIM, EPS_NORM, ALU.mult, ALU.add)
        chain.link(vec.tensor_tensor(work, work, work, ALU.mult))
        chain.link(vec.scalar_tensor_tensor(out=var, in0=work, scalar=0.25, in1=var, op0=ALU.mult, op1=ALU.add))
        chain.link(vec.tensor_scalar(bits, var.bitcast(I32), 1, None, ALU.arith_shift_right))
        chain.link(vec.tensor_scalar(rstd.bitcast(I32), bits, -1.0, float(0x5F3759DF), ALU.mult, ALU.add))
        for _ in range(3):
            chain.link(vec.tensor_tensor(work, rstd, rstd, ALU.mult))
            chain.link(vec.scalar_tensor_tensor(out=work, in0=work, scalar=-0.5, in1=var, op0=ALU.mult, op1=ALU.mult))
            chain.link(vec.scalar_tensor_tensor(out=rstd, in0=work, scalar=1.5, in1=rstd, op0=ALU.add, op1=ALU.mult))

    BATCH_LINKS = 14

    def apply_tile(self, X, out, t):
        return self.nc.vector.tensor_scalar(out, X[:, bass.ds(t, 1), :].rearrange("p a d -> p (a d)"),
                                            self.mean[:, bass.ds(t, 1)], self.rstd[:, bass.ds(t, 1)],
                                            ALU.subtract, ALU.mult)

    def apply(self, x4, xn4, g):
        for j in range(GT):
            last = self.nc.vector.tensor_scalar(xn4[:, j, :], x4[:, j, :], self.mean[:, bass.ds(GT * g + j, 1)],
                                                self.rstd[:, bass.ds(GT * g + j, 1)], ALU.subtract, ALU.mult)
        return last


LORA_E, LORA_R = 8, 16
LER = LORA_E * LORA_R
LA = LER + LORA_E


def lora_ffn(nc, name, sem, X, norm, w_lora, w_dense, w_b, ident, iota8):
    with ExitStack() as mem:
        def sb(n, shape, dt=F32):
            return mem.enter_context(nc.sbuf_tensor(f"{name}_{n}", shape, dt))

        def ps(n, shape):
            return mem.enter_context(nc.psum_tensor(f"{name}_{n}", shape, F32))

        xn, xT = sb("xn", [P, 2, GT, DIM]), sb("xT", [P, 2, KD, GTOK])
        top, idx, idxf = sb("top", [P, GT, 8]), sb("idx", [P, GT, 8], U32), sb("idxf", [P, GT, 2])
        gap, second, total = sb("gap", [P, GT]), sb("second", [P, GT]), sb("total", [P, GT])
        share, onehot, cw = sb("share", [P, GT, 2]), sb("onehot", [P, GT, 2, 8]), sb("cw", [P, GT, 8])
        tw, twT = sb("tw", [P, GT, LER]), sb("twT", [P, GTOK])
        ps_xT, ps_lora, ps_out = ps("ps_xT", [P, KD, GTOK]), ps("ps_lora", [P, 2, 512]), ps("ps_out", [P, 2, 512])
        ps_twT = ps("ps_twT", [P, GTOK])

        route_chain = sem(name + "_route_chain")
        xn_ready, xT_made, xT_ready = sem(name + "_xn_ready"), sem(name + "_xT_made"), sem(name + "_xT_ready")
        lora_made, gap_ready, second_ready = sem(name + "_lora_made"), sem(name + "_gap_ready"), sem(name + "_second_ready")
        tw_ready, twT_made, twT_ready = sem(name + "_tw_ready"), sem(name + "_twT_made"), sem(name + "_twT_ready")
        dense_made, out_made, added = sem(name + "_dense_made"), sem(name + "_out_made"), sem(name + "_added")

        def lora_cols(j, a, b):
            return ps_lora[:, j // 2, (j % 2) * LA + a:(j % 2) * LA + b]

        with nc.Block() as block:
            @block.vector
            def _(dve):
                route = Chain(dve, route_chain, 8)
                rstd_col = norm.rstd[:, 0:1]

                def turn(u, p):
                    n = 2 * u + p
                    if live(n - 2, GROUPS):
                        h = n - 2
                        route.item(h)
                        dve.wait_ge(lora_made, h + 1)
                        nc.vector.tensor_copy(total[:, 0:1], rstd_col)
                        for j in range(GT):
                            last = nc.vector.max(top[:, j, :], lora_cols(j, LER, LA))
                        route.link(last)
                        nc.vector.tensor_tensor(gap[:, :], top[:, :, 1], top[:, :, 0],
                                                ALU.subtract).then_inc(gap_ready, 1)
                        for j in range(GT):
                            last = nc.vector.max_index(idx[:, j, :], top[:, j, :], lora_cols(j, LER, LA))
                        route.link(last)
                        route.link(nc.vector.tensor_copy(idxf[:, :, :], idx[:, :, 0:2]))
                        dve.wait_ge(second_ready, h + 1)
                        route.link(nc.vector.tensor_scalar(total[:, :], second[:, :], 1.0, None, ALU.add))
                        route.link(nc.vector.reciprocal(share[:, :, 0], total[:, :]))
                        nc.vector.tensor_tensor(share[:, :, 1], second[:, :], share[:, :, 0], ALU.mult)
                        route.link(nc.vector.tensor_tensor(
                            onehot[:, :, :, :], iota8[:, :, :, :],
                            idxf[:, :, :].unsqueeze(3).to_broadcast([P, GT, 2, 8]), ALU.is_equal))
                        route.link(nc.vector.tensor_tensor(
                            onehot[:, :, :, :], onehot[:, :, :, :],
                            share[:, :, :].unsqueeze(3).to_broadcast([P, GT, 2, 8]), ALU.mult))
                        route.link(nc.vector.tensor_tensor(cw[:, :, :], onehot[:, :, 0, :], onehot[:, :, 1, :], ALU.add))
                        if some(h):
                            dve.wait_ge(twT_made, h)
                        for j in range(GT):
                            last = nc.vector.tensor_tensor(
                                tw[:, j, :].rearrange("p (e r) -> p e r", e=LORA_E),
                                lora_cols(j, 0, LER).rearrange("p (e r) -> p e r", e=LORA_E),
                                cw[:, j, :].unsqueeze(2).to_broadcast([P, LORA_E, LORA_R]), ALU.mult)
                        last.then_inc(tw_ready, 1)
                    if live(n, GROUPS):
                        if some(n - 1):
                            dve.wait_ge(xT_made, n - 1)
                        norm.apply(X[:, bass.ds(GT * n, GT), :], xn[:, p], n).then_inc(xn_ready, 1)
                    if live(n - 3, GROUPS):
                        h = n - 3
                        dve.wait_ge(out_made, h + 1)
                        x4 = X[:, bass.ds(GT * h, GT), :]
                        nc.vector.tensor_tensor(x4, x4, ps_out[:, :, :].rearrange("p a (b d) -> p (a b) d", d=DIM),
                                                ALU.add).then_inc(added, 1)
                        dve.wait_ge(added, h + 1)
                        norm.statistics(x4, h)

                steps(dve, GROUPS, turn, tail=3, head=2)

            @block.scalar
            def _(act):
                def step(u, p):
                    g = 2 * u + p
                    if live(g - 2, GROUPS):
                        act.wait_ge(twT_made, g - 1)
                        nc.scalar.copy(twT[:, :], ps_twT[:, :]).then_inc(twT_ready, 1)
                    if live(g - 1, GROUPS):
                        act.wait_ge(gap_ready, g)
                        nc.scalar.activation(second[:, :], gap[:, :], ACT.Exp).then_inc(second_ready, 1)
                    if live(g, GROUPS):
                        if some(g - 1):
                            act.wait_ge(dense_made, g - 1)
                        act.wait_ge(xT_made, g + 1)
                        nc.scalar.copy(xT[:, p], ps_xT[:, :, :]).then_inc(xT_ready, 1)

                steps(act, GROUPS, step, tail=2, head=2)

            @block.tensor
            def _(pe):
                def step(u, p):
                    g = 2 * u + p
                    if live(g, GROUPS):
                        pe.wait_ge(xn_ready, g + 1)
                        if some(g):
                            pe.wait_ge(xT_ready, g)
                        for j in range(GT):
                            for k in range(KD):
                                last = nc.tensor.transpose(ps_xT[:, k, j * P:(j + 1) * P],
                                                           xn[:, p, j, k * P:(k + 1) * P], ident)
                        last.then_inc(xT_made, 1)
                    if live(g - 1, GROUPS):
                        h, q = g - 1, 1 - p
                        pe.wait_ge(xT_ready, h + 1)
                        if some(h):
                            pe.wait_ge(tw_ready, h)
                        for j in range(GT):
                            for k in range(KD):
                                last = nc.tensor.matmul(lora_cols(j, 0, LA), xT[:, q, k, j * P:(j + 1) * P],
                                                        w_lora[:, k, :], start=(k == 0), stop=(k == KD - 1))
                        last.then_inc(lora_made, 1)
                    if live(g - 2, GROUPS):
                        h = g - 2
                        pe.wait_ge(tw_ready, h + 1)
                        if some(h):
                            pe.wait_ge(twT_ready, h)
                        for j in range(GT):
                            last = nc.tensor.transpose(ps_twT[:, j * P:(j + 1) * P], tw[:, j, :], ident)
                        last.then_inc(twT_made, 1)
                        if some(h):
                            pe.wait_ge(added, h)
                        for j in range(GT):
                            for k in range(KD):
                                last = nc.tensor.matmul(ps_out[:, j // 2, (j % 2) * DIM:(j % 2 + 1) * DIM],
                                                        xT[:, p, k, j * P:(j + 1) * P], w_dense[:, k, :],
                                                        start=(k == 0 and j % 2 == 0), stop=False,
                                                        skip_group_check=True)
                        last.then_inc(dense_made, 1)
                        pe.wait_ge(twT_ready, h + 1)
                        for j in range(GT):
                            last = nc.tensor.matmul(ps_out[:, j // 2, (j % 2) * DIM:(j % 2 + 1) * DIM],
                                                    twT[:, j * P:(j + 1) * P], w_b, start=False, stop=True,
                                                    skip_group_check=True)
                        last.then_inc(out_made, 1)

                steps(pe, GROUPS, step, tail=2, head=2)


HEADS = 16
HD = DIM // HEADS
GH = 4
HGROUPS = HEADS // GH
QK_SCALE = HD ** -0.5
THRESHOLD = -0.1
DEN_EPS = 1e-6
PARTS = 3
Q_ROWS, K_ROWS = (0, 0, 1, 0, 2, 1), (0, 1, 0, 2, 0, 1)
STACK = HD * len(Q_ROWS)
QBLOCKS = SEQ // GTOK
KTILES = SEQ // P


def load_stacks(sp, it, p, QK, parts_dram, qk_loaded):
    for dst, which, rows in ((QK[0], 0, Q_ROWS), (QK[1], 1, K_ROWS)):
        for r, part in enumerate(rows):
            for qb in range(QBLOCKS):
                src = parts_dram[which, bass.ds((it // HGROUPS) * QBLOCKS + qb, 1),
                                 bass.ds((it % HGROUPS) // 2, 1), bass.ds((it % 2) * 64, 64), part, :]
                sp.dma_start(dst[r * HD:(r + 1) * HD, :, qb * GTOK:(qb + 1) * GTOK],
                             src.rearrange("a b (h d) t -> (a b d) h t", d=HD)).then_inc(qk_loaded[p], 16)


def project(nc, sem, X, norm, weights, ident, V, parts_dram, QK, qk_loaded):
    wq, wk, wv = weights
    with ExitStack() as mem:
        def sb(n, shape, dt=F32):
            return mem.enter_context(nc.sbuf_tensor("pr_" + n, shape, dt))

        def ps(n, shape):
            return mem.enter_context(nc.psum_tensor("pr_" + n, shape, F32))

        xn = sb("xn", [P, 2, GT, DIM])
        xT, xT_lo = sb("xT", [P, 2, KD, GTOK], F32R), sb("xT_lo", [P, 2, KD, GTOK], F32R)
        parts = sb("parts", [P, 2, 2, KD, PARTS, GTOK], BF16)
        rest = sb("rest", [P, 2, KD, GTOK])
        ps_xT, ps_v = ps("ps_xT", [P, KD, GTOK]), ps("ps_v", [P, GT, DIM])
        ps_qk = ps("ps_qk", [P, 2, KD, GTOK])
        xn_ready, xT_made, xT_ready = sem("pr_xn_ready"), sem("pr_xT_made"), sem("pr_xT_ready")
        qk_made, part1_ready, rest_ready, part2_ready, part3_ready = (
            sem("pr_" + n) for n in ("qk_made", "part1_ready", "rest_ready", "part2_ready", "part3_ready"))
        v_made, v_ready, xT_lo_ready = sem("pr_v_made"), sem("pr_v_ready"), sem("pr_xT_lo_ready")
        stored = [sem(f"pr_stored{p}") for p in range(2)]
        scales = (QK_SCALE, 1.0)
        units = [(w, m) for w in range(2) for m in range(KD)]

        with nc.Block() as block:
            @block.vector
            def _(dve):
                def step(u, p):
                    g = 2 * u + p
                    if live(g, GROUPS):
                        if some(g - 1):
                            dve.wait_ge(xT_made, g - 1)
                        norm.apply(X[:, bass.ds(GT * g, GT), :], xn[:, p], g).then_inc(xn_ready, 1)
                        dve.wait_ge(xT_ready, g + 1)
                        nc.vector.tensor_tensor(xT_lo[:, p], ps_xT[:, :, :], xT[:, p].bitcast(F32), ALU.subtract
                                                ).then_inc(xT_lo_ready, 1)
                    if live(g - 1, GROUPS):
                        for i, (w, m) in enumerate(units):
                            dve.wait_ge(part1_ready, 4 * (g - 1) + i + 1)
                            if some(4 * (g - 2) + i + 1):
                                dve.wait_ge(part3_ready, 4 * (g - 2) + i + 1)
                            nc.vector.scalar_tensor_tensor(
                                out=rest[:, w, m, :], in0=ps_qk[:, w, m, :], scalar=scales[w],
                                in1=parts[:, 1 - p, w, m, 0, :], op0=ALU.mult, op1=ALU.subtract).then_inc(rest_ready, 1)

                steps(dve, GROUPS, step, tail=1)

            @block.scalar
            def _(act):
                def step(u, p):
                    g = 2 * u + p
                    if live(g, GROUPS):
                        act.wait_ge(xT_made, g + 1)
                        nc.scalar.copy(xT[:, p], ps_xT[:, :, :]).then_inc(xT_ready, 1)
                    if live(g - 1, GROUPS):
                        hu, q = back(u, p)
                        for i, (w, m) in enumerate(units):
                            act.wait_ge(qk_made, 4 * (g - 1) + i + 1)
                            if i == 0:
                                if some(32 * hu):
                                    act.wait_ge(stored[q], 32 * hu)
                            nc.scalar.activation(parts[:, q, w, m, 0, :], ps_qk[:, w, m, :], ACT.Copy,
                                                 scale=scales[w]).then_inc(part1_ready, 1)
                        for i, (w, m) in enumerate(units):
                            act.wait_ge(rest_ready, 4 * (g - 1) + i + 1)
                            nc.scalar.copy(parts[:, q, w, m, 1, :], rest[:, w, m, :]).then_inc(part2_ready, 1)
                        if some(g):
                            act.wait_ge(v_made, g)
                        nc.scalar.copy(V[:, bass.ds(GT * (g - 1), GT), :, :],
                                       ps_v[:, :, :].rearrange("p t (h d) -> p t h d", d=HD)).then_inc(v_ready, 1)

                steps(act, GROUPS, step, tail=1, head=2)

            @block.gpsimd
            def _(pool):
                def step(u, p):
                    g = 2 * u + p
                    for i, (w, m) in enumerate(units):
                        pool.wait_ge(part2_ready, 4 * g + i + 1)
                        nc.gpsimd.tensor_tensor(parts[:, p, w, m, 2, :], rest[:, w, m, :],
                                                parts[:, p, w, m, 1, :], ALU.subtract).then_inc(part3_ready, 1)

                steps(pool, GROUPS, step)

            @block.tensor
            def _(pe):
                def step(u, p):
                    g = 2 * u + p
                    if live(g, GROUPS):
                        pe.wait_ge(xn_ready, g + 1)
                        if some(g):
                            pe.wait_ge(xT_lo_ready, g)
                        for j in range(GT):
                            for k in range(KD):
                                last = nc.tensor.transpose(ps_xT[:, k, j * P:(j + 1) * P],
                                                           xn[:, p, j, k * P:(k + 1) * P], ident)
                        last.then_inc(xT_made, 1)
                    if live(g - 1, GROUPS):
                        h, q = g - 1, 1 - p
                        pe.wait_ge(xT_lo_ready, h + 1)
                        terms = [(k, part, x) for k in range(KD) for part, x in ((0, xT), (1, xT), (0, xT_lo))]
                        for i, (w, m) in enumerate(units):
                            if some(4 * (h - 1) + i + 1):
                                pe.wait_ge(rest_ready, 4 * (h - 1) + i + 1)
                            for n, (k, part, x) in enumerate(terms):
                                last = nc.tensor.matmul(ps_qk[:, w, m, :], (wq, wk)[w][part][:, k, m * P:(m + 1) * P],
                                                        x[:, q, k, :], start=(n == 0), stop=(n == len(terms) - 1))
                            last.then_inc(qk_made, 1)
                        if some(h):
                            pe.wait_ge(v_ready, h)
                        for j in range(GT):
                            for n, (k, part, x) in enumerate(terms):
                                last = nc.tensor.matmul(ps_v[:, j, :], x[:, q, k, j * P:(j + 1) * P],
                                                        wv[part][:, k, :], start=(n == 0), stop=(n == len(terms) - 1))
                        last.then_inc(v_made, 1)

                steps(pe, GROUPS, step, tail=1)

            @block.sync
            def _(sp):
                def step(u, p):
                    g = 2 * u + p
                    sp.wait_ge(part3_ready, 4 * (g + 1))
                    if isinstance(g, int) and g == 2:
                        for n in range(2):
                            sp.wait_ge(stored[n], 32)
                    for w in range(2):
                        sp.dma_start(parts_dram[w, bass.ds(g, 1)].rearrange("o m p c t -> p (o m) c t"),
                                     parts[:, p, w]).then_inc(stored[p], 16)
                    if isinstance(g, int) and g == 2:
                        load_stacks(sp, 0, 0, QK, parts_dram, qk_loaded)

                steps(sp, GROUPS, step, head=2)
                for p in range(2):
                    sp.wait_ge(stored[p], 32 * (GROUPS // 2))


SCORE_UNITS = [(qb, kt) for qb in range(QBLOCKS) for kt in range(GT * (qb + 1))]
S_BANKS, W_BUFS = 6, 8


def attend(nc, sem, V, parts_dram, QK, qk_loaded, diag, ident, heads_out):
    items = BATCH * HGROUPS
    units = len(SCORE_UNITS)
    last_of = {qb: max(k for k, (b, _) in enumerate(SCORE_UNITS) if b == qb) for qb in range(QBLOCKS)}
    with ExitStack() as mem:
        def sb(n, shape, dt=F32):
            return mem.enter_context(nc.sbuf_tensor("at_" + n, shape, dt))

        Q, K = ([QK[n], sb("QK"[n] + "1", [STACK, GH, SEQ], BF16)] for n in range(2))
        v = [sb(f"v{p}", [P, KTILES, GH * 2 * HD]) for p in range(2)]
        w = [sb(f"w{n}", [P, GTOK]) for n in range(W_BUFS)]
        o, rec = sb("o", [P, GTOK]), sb("rec", [P, GT * GH])
        ps_s = [mem.enter_context(nc.psum_tensor(f"at_s{n}", [P, GTOK], F32)) for n in range(S_BANKS)]
        ps_o = [mem.enter_context(nc.psum_tensor(f"at_o{n}", [P, GTOK], F32)) for n in range(QBLOCKS)]
        v_ready, s_made, pv_done = sem("at_v_ready"), sem("at_s_made"), sem("at_pv_done")
        w_ready = [sem("at_w_even_ready"), sem("at_w_odd_ready")]
        o_copied, oT_made, normed, rec_chain = sem("at_o_copied"), sem("at_oT_made"), sem("at_normed"), sem("at_rec_chain")
        tri, big = diag

        def span(k):
            qb, kt = SCORE_UNITS[k]
            return max(0, kt * P - qb * GTOK)

        def evacuate(eng, it, k, j, write):
            n = GH * k + j
            if some(units * it + k - 1):
                eng.wait_ge(pv_done, units * it + k - 1)
            eng.wait_ge(s_made, GH * units * it + n + 1)
            c = span(k)
            write(w[n % W_BUFS][:, c:], ps_s[n % S_BANKS][:, c:]).then_inc(w_ready[j % 2], 1)

        with nc.Block() as block:
            @block.sync
            def _(sp):
                def step(u, p):
                    it = 2 * u + p
                    if some(GH * units * (it - 1)):
                        sp.wait_ge(s_made, GH * units * (it - 1))
                    if some(it):
                        load_stacks(sp, it, p, (Q[p], K[p]), parts_dram, qk_loaded)

                steps(sp, items, step)

            @block.gpsimd
            def _(pool):
                def step(u, p):
                    it = 2 * u + p
                    if some(units * (it - 1)):
                        pool.wait_ge(pv_done, units * (it - 1))
                    src = V[:, bass.ds((it // HGROUPS) * KTILES, KTILES), bass.ds((it % HGROUPS) * GH, GH), :]
                    nc.gpsimd.tensor_copy(v[p][:, :, :].rearrange("p t (h d) -> p t h d", h=GH)[:, :, :, 0:HD], src
                                          ).then_inc(v_ready, 1)

                for p in range(2):
                    nc.gpsimd.memset(v[p][:, :, :].rearrange("p t (h d) -> p t h d", h=GH)[:, :, :, HD:], 1.0)
                steps(pool, items, step)

            @block.scalar
            def _(act):
                def copy_out(it, qb):
                    act.wait_ge(pv_done, units * it + last_of[qb] + 1)
                    if some(QBLOCKS * it + qb):
                        act.wait_ge(oT_made, QBLOCKS * it + qb)
                    nc.scalar.copy(o[:, :], ps_o[qb][:, :]).then_inc(o_copied, 1)

                def step(u, p):
                    it = 2 * u + p
                    for k in range(units):
                        if live(it, items):
                            for j in (0, 2):
                                evacuate(act, it, k, j, lambda out, s: nc.scalar.activation(
                                    out, s, ACT.Relu, bias=threshold_col))
                        if k == 0 and live(it - 1, items):
                            copy_out(it - 1, 1)
                        if k == 4 and live(it, items):
                            copy_out(it, 0)

                threshold_col = tri[1]
                steps(act, items, step, tail=1)

            @block.vector
            def _(dve):
                chain = Chain(dve, rec_chain, 2 * QBLOCKS)

                def norm_heads(it, qb, n):
                    dve.wait_ge(oT_made, QBLOCKS * it + qb + 1)
                    oT = ps_o[qb][:, :].rearrange("p (t h c) -> p t h c", t=GT, h=GH)
                    chain.base, chain.done = 2 * (QBLOCKS * it + qb), 0
                    recs = rec[:, :].rearrange("p (t h) -> p t h", t=GT)
                    chain.link(nc.vector.tensor_scalar(recs, oT[:, :, :, HD], DEN_EPS, None, ALU.add))
                    chain.link(nc.vector.reciprocal(recs, recs))
                    out = heads_out[:, bass.ds((it // HGROUPS) * QBLOCKS + qb, 1), bass.ds(it % HGROUPS, 1)]
                    nc.vector.tensor_tensor(out.rearrange("p a b (t h) d -> p (a b t) h d", h=GH), oT[:, :, :, 0:HD],
                                            recs.unsqueeze(3).to_broadcast([P, GT, GH, HD]),
                                            ALU.mult).then_inc(normed, 1)

                def step(u, p):
                    it = 2 * u + p
                    for k in range(units):
                        if live(it, items):
                            for j in (1, 3):
                                evacuate(dve, it, k, j, lambda out, s: nc.vector.tensor_scalar(
                                    out, s, -THRESHOLD, 0.0, ALU.add, ALU.max))
                        if k == 2 and live(it - 1, items):
                            norm_heads(it - 1, 1, k)
                        if k == 6 and live(it, items):
                            norm_heads(it, 0, k)

                steps(dve, items, step, tail=1)

            @block.tensor
            def _(pe):
                def score(it, p, k, j):
                    qb, kt = SCORE_UNITS[k]
                    n, c = GH * k + j, span(k)
                    before = n - S_BANKS
                    if some(2 * units * it + before // 2 + 1):
                        pe.wait_ge(w_ready[j % 2], 2 * units * it + before // 2 + 1)
                    s = ps_s[n % S_BANKS]
                    diagonal = kt >= GT * qb
                    last = nc.tensor.matmul(s[:, c:], K[p][:, j, kt * P:(kt + 1) * P],
                                            Q[p][:, j, qb * GTOK + c:(qb + 1) * GTOK],
                                            start=True, stop=not diagonal, skip_group_check=True)
                    if diagonal:
                        last = nc.tensor.matmul(s[:, c:c + P], big, tri[0], start=False, stop=True,
                                                skip_group_check=True)
                    last.then_inc(s_made, 1)

                def weigh(it, p, k):
                    qb, kt = SCORE_UNITS[k]
                    c = span(k)
                    if k == 0:
                        pe.wait_ge(v_ready, it + 1)
                    if kt == 0:
                        if some(QBLOCKS * (it - 1) + qb + 1):
                            pe.wait_ge(normed, QBLOCKS * (it - 1) + qb + 1)
                    for j in range(GH):
                        n = GH * k + j
                        pe.wait_ge(w_ready[j % 2], 2 * units * it + n // 2 + 1)
                        last = nc.tensor.matmul(ps_o[qb][32 * j:32 * (j + 1), c:],
                                                v[p][:, kt, j * 2 * HD:(j + 1) * 2 * HD], w[n % W_BUFS][:, c:],
                                                start=(kt == 0), stop=(k == last_of[qb]), skip_group_check=True)
                    last.then_inc(pv_done, 1)

                def transpose_out(it, qb):
                    pe.wait_ge(o_copied, QBLOCKS * it + qb + 1)
                    for t in range(GT):
                        last = nc.tensor.transpose(ps_o[qb][:, t * P:(t + 1) * P], o[:, t * P:(t + 1) * P], ident)
                    last.then_inc(oT_made, 1)

                def step(u, p):
                    it = 2 * u + p
                    for k in range(units):
                        if live(it, items):
                            if k == 0:
                                pe.wait_ge(qk_loaded[p], 16 * 2 * len(Q_ROWS) * QBLOCKS * (u + 1))
                            for j in range(GH):
                                score(it, p, k, j)
                        if k == 1 and live(it - 1, items):
                            transpose_out(it - 1, 1)
                        if k == 5 and live(it, items):
                            transpose_out(it, 0)
                        if k == 0 and live(it - 1, items):
                            weigh(it - 1, 1 - p, units - 1)
                        if k > 0 and live(it, items):
                            weigh(it, p, k - 1)

                steps(pe, items, step, tail=1)


def project_out(nc, sem, X, norm, wo, ident, heads_out):
    with ExitStack() as mem:
        aT, aT_lo = (mem.enter_context(nc.sbuf_tensor("po_aT" + n, [P, 2, KD, GTOK], F32R)) for n in ("_hi", "_lo"))
        a = mem.enter_context(nc.sbuf_tensor("po_a", [P, 2, GT, DIM], F32))
        ps_aT = mem.enter_context(nc.psum_tensor("po_ps_aT", [P, KD, GTOK], F32))
        ps_y = [mem.enter_context(nc.psum_tensor(f"po_ps_y{p}", [P, GT, DIM], F32)) for p in range(2)]
        a_ready, aT_made, aT_ready, aT_lo_ready, y_made, added = (
            sem("po_" + n) for n in ("a_ready", "aT_made", "aT_ready", "aT_lo_ready", "y_made", "added"))
        with nc.Block() as block:
            @block.gpsimd
            def _(pool):
                def step(u, p):
                    g = 2 * u + p
                    if some(g - 1):
                        pool.wait_ge(aT_made, g - 1)
                    for hg in range(HGROUPS):
                        last = nc.gpsimd.tensor_copy(
                            a[:, p, :, hg * GH * HD:(hg + 1) * GH * HD],
                            heads_out[:, bass.ds(g, 1), hg].rearrange("p a (t h) d -> p (a t) (h d)", h=GH))
                    last.then_inc(a_ready, 1)

                steps(pool, GROUPS, step)

            @block.scalar
            def _(act):
                def step(u, p):
                    act.wait_ge(aT_made, 2 * u + p + 1)
                    nc.scalar.copy(aT[:, p], ps_aT[:, :, :]).then_inc(aT_ready, 1)

                steps(act, GROUPS, step)

            @block.tensor
            def _(pe):
                terms = [(k, x, part) for k in range(KD) for x, part in ((aT, 0), (aT, 1), (aT_lo, 0))]

                def step(u, p):
                    g = 2 * u + p
                    if live(g, GROUPS):
                        pe.wait_ge(a_ready, g + 1)
                        if some(g):
                            pe.wait_ge(aT_lo_ready, g)
                        for j in range(GT):
                            for k in range(KD):
                                last = nc.tensor.transpose(ps_aT[:, k, j * P:(j + 1) * P],
                                                           a[:, p, j, k * P:(k + 1) * P], ident)
                        last.then_inc(aT_made, 1)
                    if live(g - 1, GROUPS):
                        h, q = g - 1, 1 - p
                        pe.wait_ge(aT_lo_ready, h + 1)
                        if some(h - 1):
                            pe.wait_ge(added, h - 1)
                        for j in range(GT):
                            for n, (k, x, part) in enumerate(terms):
                                last = nc.tensor.matmul(ps_y[q][:, j, :], x[:, q, k, j * P:(j + 1) * P], wo[part][:, k, :],
                                                        start=(n == 0), stop=(n == len(terms) - 1))
                        last.then_inc(y_made, 1)

                steps(pe, GROUPS, step, tail=1)

            @block.vector
            def _(dve):
                def step(u, p):
                    g = 2 * u + p
                    if live(g, GROUPS):
                        dve.wait_ge(aT_ready, g + 1)
                        if some(g - 1):
                            dve.wait_ge(y_made, g - 1)
                        nc.vector.tensor_tensor(aT_lo[:, p], ps_aT[:, :, :], aT[:, p].bitcast(F32), ALU.subtract
                                                ).then_inc(aT_lo_ready, 1)
                    if live(g - 1, GROUPS):
                        dve.wait_ge(y_made, g)
                        x4 = X[:, bass.ds(GT * (g - 1), GT), :]
                        nc.vector.tensor_tensor(x4, x4, ps_y[1 - p][:, :, :], ALU.add).then_inc(added, 1)
                        dve.wait_ge(added, g)
                        norm.statistics(x4, g - 1)

                steps(dve, GROUPS, step, tail=1)


def attention(nc, sem, X, norm, wq, wk, wv, wo, ident, inp):
    parts_dram = nc.dram_tensor("parts", [2, GROUPS, KD, P, PARTS, GTOK], BF16).ap()
    with ExitStack() as mem:
        heads_out = mem.enter_context(nc.sbuf_tensor(
            "heads_out", [P, BATCH * QBLOCKS, HGROUPS, GT * GH, HD], F32))
        with ExitStack() as inner:
            V = inner.enter_context(nc.sbuf_tensor("V", [P, TILES, HEADS, HD], F32))
            big = inner.enter_context(nc.sbuf_tensor("big", [P, P], BF16))
            tri = inner.enter_context(nc.sbuf_tensor("tri", [P, P], BF16))
            threshold = inner.enter_context(nc.sbuf_tensor("threshold", [P, 1], F32))
            make_mask(nc, sem, big, tri, threshold)
            QK = [inner.enter_context(nc.sbuf_tensor(n + "0", [STACK, GH, SEQ], BF16)) for n in "QK"]
            qk_loaded = [sem(f"at_qk_loaded{p}") for p in range(2)]
            project(nc, sem, X, norm, (wq, wk, wv), ident, V, parts_dram, QK, qk_loaded)
            attend(nc, sem, V, parts_dram, QK, qk_loaded, ((tri[:, :], threshold[:, 0:1]), big[:, :]), ident, heads_out)
        project_out(nc, sem, X, norm, wo, ident, heads_out)


def make_mask(nc, sem, big, tri, threshold):
    cleared = sem("mask_cleared")
    with nc.Block() as block:
        @block.gpsimd
        def _(pool):
            nc.gpsimd.memset(threshold[:, :], -THRESHOLD)
            nc.gpsimd.memset(big[:, :], 0.0)
            nc.gpsimd.memset(tri[:, :], 1.0).then_inc(cleared, 1)
            pool.wait_ge(cleared, 1)
            nc.gpsimd.affine_select(out=big[:, :], in_=big[:, :], compare_op=ALU.not_equal, fill=-1e30,
                                    base=0, pattern=[[-1, P]], channel_multiplier=1)
            nc.gpsimd.affine_select(out=tri[:, :], in_=tri[:, :], compare_op=ALU.is_gt, fill=0.0,
                                    base=0, pattern=[[-1, P]], channel_multiplier=1)


EXPERTS, TOP_K = 16, 4
HID = 176
HK = (P, HID - P)
SLOT_TILES = -(-(TOKENS * TOP_K + EXPERTS * (P - 1)) // P // 4) * 4
PAIRS = TOKENS * TOP_K
Y_ROWS = PAIRS + SLOT_TILES * P
PT = TOP_K * TILES
SCATTER_LAG = 6
WAYS = 4


def split_weights(nc, sem, name, norm, jobs, tables):
    norm.prepare_finish(sem, name)
    with ExitStack() as mem:
        raw = [mem.enter_context(nc.sbuf_tensor(f"{name}_raw{n}", list(d.shape), F32)) for n, (d, _, _, _) in enumerate(jobs)]
        loaded = [sem(f"{name}_raw_loaded{n}") for n in range(len(jobs))]
        high_ready, tables_loaded = sem(name + "_high_ready"), sem(name + "_tables_loaded")
        with nc.Block() as block:
            @block.sync
            def _(sp):
                for n, (d, _, _, _) in enumerate(jobs):
                    sp.dma_start(raw[n][:, :], d).then_inc(loaded[n], 16)
                for to, of in tables:
                    sp.dma_start(to, of).then_inc(tables_loaded, 16)
                sp.wait_ge(tables_loaded, 16 * len(tables))

            @block.scalar
            def _(act):
                norm.finish_on_scalar(act)
                for n, (_, high, _, factor) in enumerate(jobs):
                    act.wait_ge(loaded[n], 16)
                    nc.scalar.activation(high, raw[n][:, :], ACT.Copy, scale=factor).then_inc(high_ready, 1)

            @block.vector
            def _(dve):
                norm.finish_on_vector(dve)
                for n, (_, high, low, factor) in enumerate(jobs):
                    dve.wait_ge(high_ready, n + 1)
                    nc.vector.scalar_tensor_tensor(out=low, in0=raw[n][:, :], scalar=factor, in1=high.bitcast(F32),
                                                   op0=ALU.mult, op1=ALU.subtract)


def expert_tiles(nc, sem, name, count, w13, w2, ident, source, shared=None, routed=None):
    cols = w13[0].shape[-1]
    with ExitStack() as mem:
        def sb(n, shape, dt=F32):
            return mem.enter_context(nc.sbuf_tensor(f"{name}_{n}", shape, dt))

        rows = [sb(f"rows{p}", [P, DIM]) for p in range(WAYS)]
        xT_hi, xT_lo = ([sb(f"xT_{n}{p}", [P, KD, P], F32R) for p in range(2)] for n in ("hi", "lo"))
        first, hid_in = sb("first", [P, HID]), sb("hid_in", [P, HID])
        hid = [sb(f"hid{p}", [P, 2 * P]) for p in range(2)]
        hT_hi, hT_lo = ([sb(f"hT_{n}{p}", [P, 2, P], F32R) for p in range(2)] for n in ("hi", "lo"))
        y = routed["y"] if routed else None
        column, y_column = ([sb(f"{n}{p}", [P, 1], I32) for p in range(WAYS)] for n in ("column", "y_column"))

        def ps(n):
            return [mem.enter_context(nc.psum_tensor(f"{name}_ps_{n}{p}", [P, 512], F32)) for p in range(2)]

        ps_x, ps_h, ps_t, ps_y = ps("x"), ps("h"), ps("t"), ps("y")
        names = ("zeroed", "rows_ready", "xT_hi_ready", "xT_lo_ready", "h_made", "first_ready", "prod_ready",
                 "hid_ready", "h_turned", "hT_hi_ready", "hT_lo_ready", "y_made", "y_ready")
        (zeroed, rows_ready, xT_hi_ready, xT_lo_ready, h_made, first_ready, prod_ready,
         hid_ready, h_turned, hT_hi_ready, hT_lo_ready, y_made, y_ready) = (sem(f"{name}_{n}") for n in names)
        x_turned = [sem(f"{name}_x_turned{p}") for p in range(WAYS)]
        rows_loaded = [sem(f"{name}_rows_loaded{p}") for p in range(WAYS)]
        first_columns_ready = sem(name + "_first_columns_ready")
        column_ready, y_filled, y_scattered = ([sem(f"{name}_{n}{p}") for p in range(WAYS)]
                                               for n in ("column_ready", "y_filled", "y_scattered"))

        def early(p):
            return int(p + SCATTER_LAG >= 2 * WAYS)

        def run(eng, step, tail=0):
            steps(eng, count, step, tail, WAYS, 2)

        with nc.Block() as block:
            @block.scalar
            def _(act):
                def step(u, p):
                    i = WAYS * u + p
                    if live(i, count):
                        if some(i - 1):
                            act.wait_ge(h_made, i - 1)
                        act.wait_ge(x_turned[p], u + 1)
                        nc.scalar.copy(xT_hi[p % 2][:, :, :], ps_x[p % 2][:, 0:DIM].rearrange("p (k t) -> p k t", k=KD)
                                       ).then_inc(xT_hi_ready, 1)
                    if live(i - 1, count):
                        q = (p - 1) % 2
                        if some(i - 1):
                            act.wait_ge(prod_ready, i - 1)
                        if some(i):
                            act.wait_ge(h_made, i)
                        nc.scalar.activation(first[:, :], ps_h[q][:, 0:HID], ACT.Silu if shared else ACT.Copy
                                             ).then_inc(first_ready, 1)
                    if live(i - 2, count):
                        q = (p - 2) % 2
                        if some(i - 3):
                            act.wait_ge(y_made, i - 3)
                        if some(i - 1):
                            act.wait_ge(h_turned, i - 1)
                        nc.scalar.copy(hT_hi[q][:, :, :], ps_t[q][:, 0:2 * P].rearrange("p (k t) -> p k t", k=2)
                                       ).then_inc(hT_hi_ready, 1)
                    if routed and live(i - 1, count):
                        q = (p - 1) % 2
                        if some(i):
                            act.wait_ge(prod_ready, i)
                        if some(i - 2):
                            act.wait_ge(h_turned, i - 2)
                        if isinstance(i, int) and i - 1 < 2:
                            act.wait_ge(zeroed, 1)
                        nc.scalar.activation(hid[q][:, 0:HID], hid_in[:, :], ACT.Silu).then_inc(hid_ready, 1)

                run(act, step, 3)

            def column_copy(p, i):
                return nc.vector.tensor_scalar(column[p][:, :], routed["gather_rows"][:, bass.ds(i, 1)], 0, None, ALU.add)

            @block.vector
            def _(dve):
                for p in range(2):
                    last = nc.vector.memset(hid[p][:, HID:], 0.0)
                last.then_inc(zeroed, 1)
                if routed:
                    for p in range(WAYS):
                        column_copy(p, p).then_inc(first_columns_ready, 1)
                        if early(p):
                            nc.vector.memset(y[p][:, :], 0.0).then_inc(y_filled[p], 1)

                def step(u, p):
                    i = WAYS * u + p
                    if shared and live(i, count):
                        if some(u):
                            dve.wait_ge(x_turned[p], u)
                        if some(16 * u):
                            dve.wait_ge(rows_loaded[p], 16 * u)
                        shared["norm"].apply_tile(shared["X"], rows[p][:, :], i).then_inc(rows_ready, 1)
                    if live(i - lead, count):
                        n, q = i - lead, (p - lead) % 2
                        dve.wait_ge(xT_hi_ready, n + 1)
                        nc.vector.tensor_tensor(xT_lo[q][:, :, :], ps_x[q][:, 0:DIM].rearrange("p (k t) -> p k t", k=KD),
                                                xT_hi[q][:, :, :].bitcast(F32), ALU.subtract).then_inc(xT_lo_ready, 1)
                        if routed:
                            column_copy(p, n + WAYS).then_inc(column_ready[p], 1)
                    if live(i - lead - 1, count):
                        n, q = i - lead - 1, (p - lead - 1) % 2
                        dve.wait_ge(first_ready, n + 1)
                        if routed:
                            if some(n):
                                dve.wait_ge(hid_ready, n)
                            out = hid_in[:, :]
                        else:
                            if some(n - 1):
                                dve.wait_ge(h_turned, n - 1)
                            out = hid[q][:, 0:HID]
                            nc.vector.tensor_copy(shared["logits"][:, bass.ds(n, 1), :].rearrange("p a e -> p (a e)"),
                                                  ps_h[q][:, 2 * HID:cols])
                        nc.vector.tensor_tensor(out, first[:, :], ps_h[q][:, HID:2 * HID], ALU.mult).then_inc(prod_ready, 1)
                    if live(i - lead - 2, count):
                        n, q = i - lead - 2, (p - lead - 2) % 2
                        dve.wait_ge(hT_hi_ready, n + 1)
                        nc.vector.tensor_tensor(hT_lo[q][:, :, :], ps_t[q][:, 0:2 * P].rearrange("p (k t) -> p k t", k=2),
                                                hT_hi[q][:, :, :].bitcast(F32), ALU.subtract).then_inc(hT_lo_ready, 1)
                    if live(i - lead - 3, count):
                        n, q = i - lead - 3, (p - lead - 3) % 2
                        dve.wait_ge(y_made, n + 1)
                        if routed:
                            un, qn = back_by(u, p, lead + 3)
                            if some(16 * un):
                                dve.wait_ge(y_scattered[qn], 16 * un)
                            nc.vector.tensor_copy(y[qn][:, :], ps_y[q][:, 0:DIM]).then_inc(y_ready, 1)
                            nc.vector.tensor_scalar(y_column[qn][:, :], routed["scatter_rows"][:, bass.ds(n, 1)], 0, None,
                                                    ALU.add).then_inc(y_filled[qn], 1)
                        else:
                            xt = shared["X"][:, bass.ds(n, 1), :].rearrange("p a d -> p (a d)")
                            nc.vector.tensor_tensor(xt, xt, ps_y[q][:, 0:DIM], ALU.add).then_inc(y_ready, 1)

                lead = 1 if shared else 0
                run(dve, step, 3 + lead)

            @block.tensor
            def _(pe):
                expert_of = {}

                def step(u, p):
                    i = WAYS * u + p
                    if routed and p == 0:
                        first = max(WAYS * u - 3, 0) if isinstance(u, int) else WAYS * u - 3
                        number = min(WAYS * u + WAYS - 1, count) - first if isinstance(u, int) else WAYS + 2
                        values = routed["experts"](first, number)
                        back = WAYS * u - first if isinstance(u, int) else 3
                        expert_of.update({m - back: v for m, v in enumerate(values)})
                    if live(i, count):
                        if routed:
                            pe.wait_ge(rows_loaded[p], 16 * (u + 1))
                        else:
                            pe.wait_ge(rows_ready, i + 1)
                        if some(i - 1):
                            pe.wait_ge(xT_lo_ready, i - 1)
                        for k in range(KD):
                            last = nc.tensor.transpose(ps_x[p % 2][:, k * P:(k + 1) * P], rows[p][:, k * P:(k + 1) * P], ident)
                        last.then_inc(x_turned[p], 1)
                    if live(i - 1, count):
                        n, q = i - 1, (p - 1) % 2
                        expert = expert_of[p - 1] if routed else None
                        pe.wait_ge(xT_lo_ready, n + 1)
                        if some(n - 1):
                            pe.wait_ge(prod_ready, n - 1)
                        terms = [(a, b, k) for k in range(KD) for a, b in ((xT_hi, 0), (xT_lo, 0), (xT_hi, 1))]
                        for m, (a, b, k) in enumerate(terms):
                            last = nc.tensor.matmul(ps_h[q][:, 0:cols], a[q][:, k, :], w13_of(b, k, expert),
                                                    start=(m == 0), stop=(m == len(terms) - 1))
                        last.then_inc(h_made, 1)
                    if live(i - 2, count):
                        n, q = i - 2, (p - 2) % 2
                        if routed:
                            pe.wait_ge(hid_ready, n + 1)
                        else:
                            pe.wait_ge(prod_ready, n + 1)
                            if isinstance(n, int) and n < 2:
                                pe.wait_ge(zeroed, 1)
                        if some(n - 1):
                            pe.wait_ge(hT_lo_ready, n - 1)
                        for k in range(2):
                            last = nc.tensor.transpose(ps_t[q][:, k * P:(k + 1) * P], hid[q][:, k * P:(k + 1) * P], ident)
                        last.then_inc(h_turned, 1)
                    if live(i - 3, count):
                        n, q = i - 3, (p - 3) % 2
                        expert = expert_of[p - 3] if routed else None
                        pe.wait_ge(hT_lo_ready, n + 1)
                        if some(n - 1):
                            pe.wait_ge(y_ready, n - 1)
                        terms = [(a, b, k) for k in range(2) for a, b in ((hT_hi, 0), (hT_lo, 0), (hT_hi, 1))]
                        for m, (a, b, k) in enumerate(terms):
                            last = nc.tensor.matmul(ps_y[q][:, 0:DIM], a[q][0:HK[k], k, :], w2_of(b, k, expert),
                                                    start=(m == 0), stop=(m == len(terms) - 1))
                        last.then_inc(y_made, 1)

                def w13_of(part, k, expert):
                    if expert is None:
                        return w13[part][:, k, :]
                    return w13[part][:, k, bass.ds(expert, 1), :].rearrange("p a n -> p (a n)")

                def w2_of(part, k, expert):
                    if expert is None:
                        return w2[part][0:HK[k], k, :]
                    return w2[part][0:HK[k], k, bass.ds(expert, 1), :].rearrange("p a n -> p (a n)")

                run(pe, step, 3)

            if shared:
                @block.sync
                def _(sp):
                    def step(u, p):
                        i = WAYS * u + p
                        sp.wait_ge(rows_ready, i + 1)
                        sp.dma_start(source[bass.ds(i * P, P), :], rows[p][:, :]).then_inc(rows_loaded[p], 16)

                    run(sp, step)
                    for p in range(WAYS):
                        sp.wait_ge(rows_loaded[p], 16 * (count // WAYS))

            if routed:
                @block.gpsimd
                def _(pool):
                    def step(u, p):
                        i = WAYS * u + p
                        if live(i, count):
                            if isinstance(u, int) and u == 0:
                                pool.wait_ge(first_columns_ready, p + 1)
                            else:
                                pool.wait_ge(column_ready[p], 1)
                                pool.wait_ge(column_ready[p], u)
                            nc.gpsimd.indirect_dma_start(
                                out=rows[p][:, :], out_offset=None, in_=source[:, :],
                                in_offset=bass.IndirectOffsetOnAxis(ap=column[p][:, 0:1], axis=0)).then_inc(rows_loaded[p], 16)
                        if live(i - SCATTER_LAG, count):
                            un, q = back_by(u, p, SCATTER_LAG)
                            pool.wait_ge(y_filled[q], 1)
                            pool.wait_ge(y_filled[q], u if not isinstance(u, int) else un + 1 + early(q))
                            nc.gpsimd.indirect_dma_start(
                                out=routed["out"][:, :], out_offset=bass.IndirectOffsetOnAxis(ap=y_column[q][:, 0:1], axis=0),
                                in_=y[q][:, :], in_offset=None).then_inc(y_scattered[q], 16)

                    run(pool, step, SCATTER_LAG)
                    for p in range(WAYS):
                        pool.wait_ge(y_scattered[p], 16 * (count // WAYS))


def back_by(u, p, n):
    return u + (p - n) // WAYS, (p - n) % WAYS


def route(nc, sem, name, logits, gate_b, tables, shares, tile_expert, low, high):
    iota16, later, iota_slot, not_first = tables
    TE = TILES * EXPERTS
    with ExitStack() as mem:
        def sb(n, shape, dt=F32):
            return mem.enter_context(nc.sbuf_tensor(f"{name}_{n}", shape, dt))

        top, idx = sb("top", [P, TILES, 8]), sb("idx", [P, TILES, 8], U32)
        scores = sb("scores", [P, TILES, EXPERTS])
        idxf, total, inv = sb("idxf", [P, TOP_K, TILES]), sb("total", [P, TILES]), sb("inv", [P, TILES])
        onehot = sb("onehot", [P, TOP_K, TILES, EXPERTS])
        mask, mask16 = sb("mask", [P, TILES, EXPERTS]), sb("mask16", [P, TILES, EXPERTS], BF16)
        ones, later16 = sb("ones", [P, P], BF16), sb("later16", [P, P], BF16)
        totals, cum = sb("totals", [P, EXPERTS, TILES]), sb("cum", [P, EXPERTS, TILES])
        counts, counts_i = sb("counts", [P, EXPERTS]), sb("counts_i", [P, EXPERTS], I32)
        n_tiles, start, unit = sb("n_tiles", [P, EXPERTS]), sb("start", [P, EXPERTS]), sb("unit", [P, EXPERTS])
        slot = sb("slot", [P, TILES, EXPERTS])
        slotf, part_i = sb("slotf", [P, TOP_K, TILES]), sb("part_i", [P, TOP_K, TILES], I32)
        slot_i = sb("slot_i", [P, TOP_K, TILES], I32)
        reached, tile_e = sb("reached", [P, SLOT_TILES, EXPERTS - 1]), sb("tile_e", [P, SLOT_TILES])
        ps_before = mem.enter_context(nc.psum_tensor(name + "_ps_before", [P, TE], F32))
        ps_total = mem.enter_context(nc.psum_tensor(name + "_ps_total", [P, TE], F32))
        links, logits_ready, mask_ready, counted = (sem(f"{name}_{n}") for n in ("links", "sig_ready", "mask_ready", "counted"))
        vec = nc.vector
        with nc.Block() as block:
            @block.scalar
            def _(act):
                nc.scalar.activation(scores[:, :, :], logits, ACT.Sigmoid).then_inc(logits_ready, 1)

            @block.tensor
            def _(pe):
                pe.wait_ge(mask_ready, 1)
                m = mask16[:, :, :].rearrange("p t e -> p (t e)")
                nc.tensor.matmul(ps_before[:, :], later16[:, :], m, start=True, stop=True)
                nc.tensor.matmul(ps_total[:, :], ones[:, :], m, start=True, stop=True).then_inc(counted, 1)

            @block.vector
            def _(dve):
                c = Chain(dve, links, 64)
                c.item(0)
                vec.memset(ones[:, :], 1.0)
                vec.tensor_copy(later16[:, :], later)
                vec.memset(unit[:, :], 1.0)
                dve.wait_ge(logits_ready, 1)
                c.link(vec.tensor_tensor(scores[:, :, :], scores[:, :, :],
                                         gate_b.unsqueeze(1).to_broadcast([P, TILES, EXPERTS]), ALU.add))
                for t in range(TILES):
                    last = vec.max(top[:, t, :], scores[:, t, :])
                c.link(last)
                for t in range(TILES):
                    last = vec.max_index(idx[:, t, :], top[:, t, :], scores[:, t, :])
                c.link(last)
                vec.tensor_reduce(total[:, :], top[:, :, 0:TOP_K], AX.X, ALU.add)
                c.link(vec.tensor_copy(idxf[:, :, :], idx[:, :, 0:TOP_K].rearrange("p t k -> p k t")))
                vec.tensor_scalar(total[:, :], total[:, :], 2.0, None, ALU.mult)
                for k in range(TOP_K):
                    last = vec.tensor_tensor(onehot[:, k], iota16,
                                             idxf[:, k, :].unsqueeze(2).to_broadcast([P, TILES, EXPERTS]), ALU.is_equal)
                c.link(last)
                vec.reciprocal(inv[:, :], total[:, :])
                vec.tensor_tensor(mask[:, :, :], onehot[:, 0], onehot[:, 1], ALU.add)
                c.link(vec.tensor_tensor(slot[:, :, :], onehot[:, 2], onehot[:, 3], ALU.add))
                vec.tensor_tensor(mask16[:, :, :], mask[:, :, :], slot[:, :, :], ALU.add).then_inc(mask_ready, 1)
                c.link(vec.tensor_tensor(shares, top[:, :, 0:TOP_K],
                                         inv[:, :].unsqueeze(2).to_broadcast([P, TILES, TOP_K]), ALU.mult))
                dve.wait_ge(counted, 1)
                c.link(vec.tensor_copy(totals[:, :, :], ps_total[:, :].rearrange("p (t e) -> p e t", t=TILES)))
                c.link(vec.tensor_tensor_scan(cum[:, :, :].rearrange("p e t -> p (e t)"), not_first,
                                              totals[:, :, :].rearrange("p e t -> p (e t)"), 0.0, ALU.mult, ALU.add))
                c.link(vec.tensor_scalar(counts_i[:, :], cum[:, :, TILES - 1], float(P - 1), None, ALU.add))
                c.link(vec.tensor_scalar(counts_i[:, :], counts_i[:, :], 7, None, ALU.arith_shift_right))
                c.link(vec.tensor_copy(n_tiles[:, :], counts_i[:, :]))
                c.link(vec.tensor_tensor_scan(start[:, :], unit[:, :], n_tiles[:, :], 0.0, ALU.mult, ALU.add))
                c.link(vec.tensor_tensor(start[:, :], start[:, :], n_tiles[:, :], ALU.subtract))
                vec.tensor_scalar(counts[:, :], start[:, :], float(P), None, ALU.mult)
                vec.tensor_tensor(reached[:, :, :], iota_slot.unsqueeze(2).to_broadcast([P, SLOT_TILES, EXPERTS - 1]),
                                  start[:, 1:].unsqueeze(1).to_broadcast([P, SLOT_TILES, EXPERTS - 1]), ALU.is_ge)
                c.link(vec.tensor_tensor(cum[:, :, :], cum[:, :, :], totals[:, :, :], ALU.subtract))
                vec.tensor_reduce(tile_e[:, :], reached[:, :, :], AX.X, ALU.add)
                c.link(vec.tensor_tensor(cum[:, :, :], cum[:, :, :],
                                         counts[:, :].unsqueeze(2).to_broadcast([P, EXPERTS, TILES]), ALU.add))
                vec.tensor_copy(tile_expert, tile_e[:, :])
                c.link(vec.tensor_tensor(slot[:, :, :], ps_before[:, :].rearrange("p (t e) -> p t e", t=TILES),
                                         cum[:, :, :].rearrange("p e t -> p t e"), ALU.add))
                for k in range(TOP_K):
                    last = vec.tensor_tensor(onehot[:, k], onehot[:, k], slot[:, :, :], ALU.mult)
                c.link(last)
                c.link(vec.tensor_reduce(slotf[:, :, :], onehot[:, :, :, :], AX.X, ALU.add))
                c.link(vec.tensor_copy(slot_i[:, :, :], slotf[:, :, :]))
                c.link(vec.tensor_scalar(part_i[:, :, :], slot_i[:, :, :], P - 1, None, ALU.bitwise_and))
                vec.tensor_scalar(slot_i[:, :, :], slot_i[:, :, :], 7, None, ALU.arith_shift_right)
                c.link(vec.tensor_copy(low, part_i[:, :, :]))
                vec.tensor_copy(high, slot_i[:, :, :])


def invert_and_split(nc, sem, name, iota_slot, pair_no, pad_row, low, high, gather_rows, scatter_rows, inp, w13, w2):
    per_turn = TILES // EXPERTS
    with ExitStack() as mem:
        def sb(n, shape, dt=F32):
            return mem.enter_context(nc.sbuf_tensor(f"{name}_{n}", shape, dt))

        at = [sb(f"at{p}", [P, 2, P]) for p in range(2)]
        of = [sb(f"of{p}", [P, 2, SLOT_TILES]) for p in range(2)]
        pair, is_pad = of[0][:, 0, :], of[0][:, 1, :]
        end_links = sem(name + "_end_links")
        ps_inv = mem.enter_context(nc.psum_tensor(name + "_ps_inv", [P, SLOT_TILES], F32))
        sizes = [(P, 2 * HID)] * KD + [(HK[k], DIM) for k in range(2)]
        source = [inp["w13"][k * P:(k + 1) * P] for k in range(KD)] + [inp["w2"][k * P:k * P + HK[k]] for k in range(2)]
        raw = [[sb(f"raw{p}{j}", size) for j, size in enumerate(sizes)] for p in range(2)]
        loaded, low_ready = ([[sem(f"{name}_{n}{p}{j}") for j in range(4)] for p in range(2)]
                             for n in ("raw_loaded", "low_ready"))

        hot_ready, hot_used, high_ready = (sem(f"{name}_{n}") for n in ("hot_ready", "hot_used", "high_ready"))

        def units(e):
            return [(per_turn * e + t, q, 2 * (per_turn * e + t) + q) for t in range(per_turn) for q in range(2)]

        def piece(part, j, e):
            w, k = ((w13, w2)[j // 2][part], j % 2)
            return w[0:sizes[j][0], k, bass.ds(e, 1), :].rearrange("p a n -> p (a n)")

        with nc.Block() as block:
            @block.sync
            def _(sp):
                def turn(u, p):
                    e = 2 * u + p
                    for j in range(4):
                        if some(u):
                            sp.wait_ge(low_ready[p][j], u)
                        cols = sizes[j][1]
                        sp.dma_start(raw[p][j][:, :], source[j][:, bass.ds(e * cols, cols)]).then_inc(loaded[p][j], 16)

                steps(sp, EXPERTS, turn)

            @block.scalar
            def _(act):
                def turn(u, p):
                    e = 2 * u + p
                    for j in range(4):
                        act.wait_ge(loaded[p][j], 16 * (u + 1))
                        nc.scalar.copy(piece(0, j, e), raw[p][j][:, :]).then_inc(high_ready, 1)

                steps(act, EXPERTS, turn)

            @block.gpsimd
            def _(pool):
                def turn(u, p):
                    e = 2 * u + p
                    for j in range(4):
                        pool.wait_ge(high_ready, 4 * e + j + 1)
                        nc.gpsimd.tensor_tensor(piece(1, j, e), raw[p][j][:, :], piece(0, j, e).bitcast(F32), ALU.subtract
                                                ).then_inc(low_ready[p][j], 1)

                steps(pool, EXPERTS, turn)

            @block.vector
            def _(dve):
                def turn(u, p):
                    for t, q, n in units(2 * u + p):
                        if some(n - 1):
                            dve.wait_ge(hot_used, n - 1)
                        nc.vector.tensor_tensor(at[q][:, :, :], iota_slot[:, 0:P].unsqueeze(1).to_broadcast([P, 2, P]),
                                                low[:, 2 * q:2 * q + 2, bass.ds(t, 1)].to_broadcast([P, 2, P]), ALU.is_equal)
                        for k in range(2):
                            last = nc.vector.tensor_scalar(of[q][:, k, :], iota_slot, high[:, 2 * q + k, bass.ds(t, 1)],
                                                           pair_no[:, 2 * q + k, bass.ds(t, 1)], ALU.is_equal, ALU.mult)
                        last.then_inc(hot_ready, 1)

                steps(dve, EXPERTS, turn)
                dve.wait_ge(hot_used, 2 * TILES)
                chain = Chain(dve, end_links, 4)
                chain.item(0)
                chain.link(nc.vector.tensor_copy(pair, ps_inv[:, :]))
                nc.vector.memset(gather_rows[:, SLOT_TILES:], 0)
                nc.vector.tensor_scalar(gather_rows[:, 0:SLOT_TILES], pair, -1.0, 0.0, ALU.add, ALU.max)
                chain.link(nc.vector.scalar_tensor_tensor(out=is_pad, in0=pair, scalar=0.0, in1=pad_row,
                                                          op0=ALU.is_equal, op1=ALU.mult))
                chain.link(nc.vector.tensor_tensor(is_pad, is_pad, pair, ALU.add))
                nc.vector.tensor_scalar(gather_rows[:, 0:SLOT_TILES], gather_rows[:, 0:SLOT_TILES], 2, None,
                                        ALU.arith_shift_right)
                nc.vector.tensor_scalar(scatter_rows, is_pad, -1.0, None, ALU.add)

            @block.tensor
            def _(pe):
                def turn(u, p):
                    for t, q, n in units(2 * u + p):
                        pe.wait_ge(hot_ready, n + 1)
                        for k in range(2):
                            last = nc.tensor.matmul(ps_inv[:, :], at[q][:, k, :], of[q][:, k, :],
                                                    start=(isinstance(n, int) and n == 0 and k == 0), stop=(k == 1),
                                                    skip_group_check=True)
                        last.then_inc(hot_used, 1)

                steps(pe, EXPERTS, turn)


class Combine:

    def __init__(self, nc, sem, name, sb, X, norm, shares, y_dram, pool_tiles):
        self.tiles = range(GT - pool_tiles)
        self.pool_tiles = range(GT - pool_tiles, GT)
        self.nc, self.X, self.norm, self.shares = nc, X, norm, shares
        self.source = y_dram[0:PAIRS, :].rearrange("(t p k) d -> t p k d", p=P, k=TOP_K)
        self.rows = [sb(f"{name}_rows{p}", [P, GT, TOP_K, DIM]) for p in range(2)]
        self.rows_loaded = [[sem(f"{name}_rows_loaded{p}{j}") for j in range(GT)] for p in range(2)]
        self.rows_added = [sem(f"{name}_rows_added{p}") for p in range(2)]
        self.links, self.pool_links, self.last_added = (sem(f"{name}_{n}") for n in ("links", "pool_links", "last_tiles_added"))

    def load(self, sp):
        def step(u, p):
            if some(u):
                sp.wait_ge(self.rows_added[p], u)
            for j in range(GT):
                sp.dma_start(self.rows[p][:, j], self.source[bass.ds(GT * (2 * u + p) + j, 1)].rearrange(
                    "t p k d -> p (t k) d")).then_inc(self.rows_loaded[p][j], 16)

        steps(sp, GROUPS, step)

    def add_last_tiles(self, pool):
        chain = Chain(pool, self.pool_links, 3 * len(self.pool_tiles))
        both = self.nc.gpsimd.tensor_tensor

        def step(u, p):
            g = 2 * u + p
            chain.item(g)
            for j in self.pool_tiles:
                t, rows = GT * g + j, self.rows[p][:, j]
                share = self.shares[:, bass.ds(t, 1), :].rearrange("p a k -> p (a k)").unsqueeze(2)
                pool.wait_ge(self.rows_loaded[p][j], 16 * (u + 1))
                chain.link(both(rows, rows, share.to_broadcast([P, TOP_K, DIM]), ALU.mult))
                chain.link(both(rows[:, 0:2], rows[:, 0:2], rows[:, 2:4], ALU.add))
                chain.link(both(rows[:, 0], rows[:, 0], rows[:, 1], ALU.add))
                xt = self.X[:, bass.ds(t, 1), :].rearrange("p a d -> p (a d)")
                last = both(xt, xt, rows[:, 0], ALU.add)
            last.then_inc(self.last_added, 1)

        steps(pool, GROUPS, step)

    def sums(self, dve):
        return Chain(dve, self.links, len(self.tiles) * TOP_K)

    def add_tiles(self, dve, chain, u, p, tiles):
        for j in tiles:
            dve.wait_ge(self.rows_loaded[p][j], 16 * (u + 1))
        for k in range(TOP_K):
            for j in tiles:
                xt = self.X[:, bass.ds(GT * (2 * u + p) + j, 1), :].rearrange("p a d -> p (a d)")
                last = self.nc.vector.scalar_tensor_tensor(
                    out=xt, in0=self.rows[p][:, j, k, :],
                    scalar=self.shares[:, bass.ds(GT * (2 * u + p) + j, 1), k], in1=xt, op0=ALU.mult, op1=ALU.add)
                chain.link(last, wait=(j == tiles[-1]))

    def finish_group(self, dve, u, p):
        dve.wait_ge(self.last_added, 2 * u + p + 1)
        x4 = self.X[:, bass.ds(GT * (2 * u + p), GT), :]
        self.norm.statistics(x4, 2 * u + p).then_inc(self.rows_added[p], 1)


def combine_and_store(nc, sem, name, X, norm, shares, y_dram, out):
    with ExitStack() as mem:
        def sb(n, shape, dt=F32):
            return mem.enter_context(nc.sbuf_tensor(n, shape, dt))

        combine = Combine(nc, sem, name, sb, X, norm, shares, y_dram, pool_tiles=1)
        x_stored, done = sem(name + "_x_stored"), sb(name + "_done", [1, 1])
        with nc.Block() as block:
            @block.sync
            def _(sp):
                combine.load(sp)

            @block.gpsimd
            def _(pool):
                combine.add_last_tiles(pool)

            @block.scalar
            def _(act):
                def step(u, p):
                    g = 2 * u + p
                    act.wait_ge(combine.rows_added[p], u + 1)
                    act.dma_start(out[bass.ds(GTOK * g, GTOK), :].rearrange("(j p) d -> p j d", p=P),
                                  X[:, bass.ds(GT * g, GT), :]).then_inc(x_stored, 16)

                steps(act, GROUPS, step)
                act.wait_ge(x_stored, 16 * GROUPS)

            @block.vector
            def _(dve):
                chain = combine.sums(dve)

                def step(u, p):
                    chain.item(2 * u + p)
                    combine.add_tiles(dve, chain, u, p, combine.tiles)
                    dve.wait_ge(combine.last_added, 2 * u + p + 1)
                    nc.vector.memset(done[:, :], 1.0).then_inc(combine.rows_added[p], 1)

                steps(dve, GROUPS, step)


def moe(nc, sem, name, X, norm, ident, inp, dram, shares):
    xhat, y_dram = dram
    with ExitStack() as mem:
        def sb(n, shape, dt=F32):
            return mem.enter_context(nc.sbuf_tensor(f"{name}_{n}", shape, dt))

        tile_expert = sb("tile_expert", [P, SLOT_TILES], I32)
        gather_rows, scatter_rows = sb("gather_rows", [P, SLOT_TILES + WAYS], I32), sb("scatter_rows", [P, SLOT_TILES], I32)
        y = [sb(f"y{p}", [P, DIM]) for p in range(WAYS)]
        low, high = (y[0][:, n * PT:(n + 1) * PT].rearrange("p (k t) -> p k t", k=TOP_K) for n in range(2))
        pair_no = y[1][:, 0:PT].rearrange("p (k t) -> p k t", k=TOP_K)
        pad_row, iota_slot = y[2][:, 0:SLOT_TILES], y[3][:, 0:SLOT_TILES]
        with ExitStack() as scratch:
            def tmp(n, shape, dt=F32):
                return scratch.enter_context(nc.sbuf_tensor(f"{name}_{n}", shape, dt))

            cols = 2 * HID + EXPERTS
            w13 = [tmp(f"ws13_{n}", [P, KD, cols], F32R) for n in ("hi", "lo")]
            w2 = [tmp(f"ws2_{n}", [P, 2, DIM], F32R) for n in ("hi", "lo")]
            logits, gate_b = tmp("logits", [P, TILES, EXPERTS]), tmp("gate_b", [P, EXPERTS])
            iota16, not_first = tmp("iota16", [P, TILES, EXPERTS]), tmp("not_first", [P, EXPERTS * TILES])
            later = tmp("later", [P, P])
            split_weights(nc, sem, name + "_ws", norm, [
                (inp["ws13"][k * P:(k + 1) * P, :], w13[0][:, k, :], w13[1][:, k, :], 1.0) for k in range(KD)] + [
                (inp["ws2"][k * P:k * P + HK[k], :], w2[0][0:HK[k], k, :], w2[1][0:HK[k], k, :], 0.5) for k in range(2)],
                tables=[(gate_b[:, :], inp["gate_b"]), (iota16[:, :, :], inp["iota16"].rearrange("p (t e) -> p t e", e=EXPERTS)),
                        (iota_slot, inp["iota_slot"]), (pair_no, inp["pair_no"].rearrange("p (k t) -> p k t", k=TOP_K)),
                        (pad_row, inp["pad_row"]), (not_first[:, :], inp["not_first"]), (later[:, :], inp["later"])])
            expert_tiles(nc, sem, name + "_shared", TILES, w13, w2, ident, xhat,
                         shared={"X": X, "norm": norm, "logits": logits})
            route(nc, sem, name + "_route", logits[:, :, :], gate_b[:, :],
                  (iota16[:, :, :], later[:, :], iota_slot, not_first[:, :]),
                  shares[:, :, :], tile_expert[:, :], low, high)
        with ExitStack() as big:
            w13 = [big.enter_context(nc.sbuf_tensor(f"{name}_w13_{n}", [P, KD, EXPERTS, 2 * HID], F32R)) for n in ("hi", "lo")]
            w2 = [big.enter_context(nc.sbuf_tensor(f"{name}_w2_{n}", [P, 2, EXPERTS, DIM], F32R)) for n in ("hi", "lo")]

            invert_and_split(nc, sem, name + "_invert", iota_slot, pair_no, pad_row, low, high,
                             gather_rows[:, :], scatter_rows[:, :], inp, w13, w2)

            def experts(first, number):
                _, values = nc.values_load_multi_w_load_instructions(
                    tile_expert[0:1, bass.ds(first, number)], engines=[mybir.EngineType.PE], min_val=0, max_val=EXPERTS - 1,
                    skip_runtime_bounds_check_because="a sum of EXPERTS - 1 comparisons, so 0 to EXPERTS - 1")
                return values

            expert_tiles(nc, sem, name + "_routed", SLOT_TILES, w13, w2, ident, xhat,
                         routed={"gather_rows": gather_rows, "scatter_rows": scatter_rows,
                                 "experts": experts, "y": y, "out": y_dram})


DECAY = 0.95


def smear(nc, sem, X, norm, ident, inp, shares, y_dram):
    scale = float(nc_sqrt(1.0 - DECAY))
    with ExitStack() as mem:
        def sb(n, shape, dt=F32):
            return mem.enter_context(nc.sbuf_tensor("sm_" + n, shape, dt))

        def ps(n, shape):
            return mem.enter_context(nc.psum_tensor("sm_" + n, shape, F32))

        wg, wv, wq, wo = (sb(n, [P, KD, DIM]) for n in ("wg", "wv", "wq", "wo"))
        bias = sb("bias", [P, 2, KD])
        decay = sb("decay", [P, GTOK])
        xn, xT = sb("xn", [P, 2, GT, DIM]), sb("xT", [P, 2, KD, GTOK])
        gate, que, store = sb("gate", [P, KD, GTOK]), sb("que", [P, KD, GTOK]), sb("store", [P, KD, GTOK])
        kept = sb("kept", [P, 2, KD, GTOK])
        load = sb("load", [P, 2, KD, GTOK])
        ps_xT, ps_y = ps("ps_xT", [P, KD, GTOK]), ps("ps_y", [P, GT, DIM])
        ps_g, ps_v, ps_q = (ps("ps_" + n, [P, GTOK]) for n in "gvq")
        combine = Combine(nc, sem, "sm_combine", sb, X, norm, shares, y_dram, pool_tiles=2)
        root_work, root_bits = sb("root_work", [P, TILES // BATCH]), sb("root_bits", [P, TILES // BATCH], I32)
        root_links = sem("sm_root_links")
        loaded, decay_ready = sem("sm_loaded"), sem("sm_decay_ready")
        names = ("xn_ready", "xT_made", "xT_ready", "g_made", "v_made", "q_made", "gate_ready", "que_ready",
                 "store_ready", "kept_ready", "load_ready", "y_made", "added")
        (xn_ready, xT_made, xT_ready, g_made, v_made, q_made, gate_ready, que_ready,
         store_ready, kept_ready, load_ready, y_made, added) = (sem("sm_" + n) for n in names)
        with nc.Block() as block:
            @block.sync
            def _(sp):
                combine.load(sp)

            @block.gpsimd
            def _(pool):
                combine.add_last_tiles(pool)

            @block.vector
            def _(dve):
                nc.vector.memset(decay[:, :], DECAY).then_inc(decay_ready, 1)
                adds, roots = combine.sums(dve), Chain(dve, root_links, Norm.BATCH_LINKS)

                def memory(h, q, m):
                    n = KD * h + m + 1
                    dve.wait_ge(v_made, n)
                    dve.wait_ge(gate_ready, n)
                    nc.vector.scalar_tensor_tensor(out=store[:, m, :], in0=ps_v[:, :], scalar=scale,
                                                   in1=gate[:, m, :], op0=ALU.mult, op1=ALU.mult
                                                   ).then_inc(store_ready, 1)
                    dve.wait_ge(store_ready, n)
                    if isinstance(n, int) and n == 1:
                        dve.wait_ge(decay_ready, 1)
                    initial = kept[:, 0, m, GTOK - 1:GTOK] if q == 1 else 0.0
                    nc.vector.tensor_tensor_scan(kept[:, q, m, :], decay[:, :], store[:, m, :], initial,
                                                 ALU.mult, ALU.add).then_inc(kept_ready, 1)
                    dve.wait_ge(que_ready, n)
                    if m == 0:
                        if some(h - 1):
                            dve.wait_ge(y_made, h - 1)
                    dve.wait_ge(kept_ready, n)
                    nc.vector.scalar_tensor_tensor(out=load[:, q, m, :], in0=kept[:, q, m, :], scalar=scale,
                                                   in1=que[:, m, :], op0=ALU.mult, op1=ALU.mult
                                                   ).then_inc(load_ready, 1)

                def turn(u, p):
                    n = 2 * u + p
                    if live(n, GROUPS):
                        adds.item(n)
                        combine.add_tiles(dve, adds, u, p, combine.tiles)
                    if live(n - 2, GROUPS):
                        memory(n - 2, p, 0)
                    if live(n, GROUPS):
                        combine.finish_group(dve, u, p)
                        if p == 1:
                            dve.wait_ge(combine.rows_added[1], u + 1)
                            roots.item(u)
                            norm.of_batch(roots, u, root_work[:, :], root_bits[:, :])
                    if live(n - 1, GROUPS):
                        h, q = n - 1, 1 - p
                        if some(h - 1):
                            dve.wait_ge(xT_made, h - 1)
                        norm.apply(X[:, bass.ds(GT * h, GT), :], xn[:, q], h).then_inc(xn_ready, 1)
                    if live(n - 2, GROUPS):
                        memory(n - 2, p, 1)
                    if live(n - 3, GROUPS):
                        h = n - 3
                        dve.wait_ge(y_made, h + 1)
                        x4 = X[:, bass.ds(GT * h, GT), :]
                        nc.vector.tensor_tensor(x4, x4, ps_y[:, :, :], ALU.add).then_inc(added, 1)
                        dve.wait_ge(added, h + 1)
                        norm.statistics(x4, h)

                steps(dve, GROUPS, turn, tail=3, head=2)

            @block.scalar
            def _(act):
                for to, of in ((wg, "l1_wg"), (wv, "l1_wv"), (wq, "l1_wq"), (wo, "l1_wo")):
                    act.dma_start(to[:, :, :], inp[of].rearrange("(k p) n -> p k n", p=P)).then_inc(loaded, 16)
                act.dma_start(bias[:, :, :], inp["l1_bias"].rearrange("p (a b) -> p a b", a=2)).then_inc(loaded, 16)
                act.wait_ge(loaded, 16 * 5)

                def turn(u, p):
                    g = 2 * u + p
                    if live(g - 2, GROUPS):
                        for m in range(KD):
                            n = KD * (g - 2) + m + 1
                            if some(n - KD):
                                act.wait_ge(store_ready, n - KD)
                            act.wait_ge(g_made, n)
                            nc.scalar.activation(gate[:, m, :], ps_g[:, :], ACT.Sigmoid, bias=bias[:, 0, m:m + 1]
                                                 ).then_inc(gate_ready, 1)
                            if some(n - KD):
                                act.wait_ge(load_ready, n - KD)
                            act.wait_ge(q_made, n)
                            nc.scalar.activation(que[:, m, :], ps_q[:, :], ACT.Sigmoid, bias=bias[:, 1, m:m + 1]
                                                 ).then_inc(que_ready, 1)
                    if live(g - 1, GROUPS):
                        act.wait_ge(xT_made, g)
                        nc.scalar.copy(xT[:, 1 - p], ps_xT[:, :, :]).then_inc(xT_ready, 1)

                steps(act, GROUPS, turn, tail=2, head=2)

            @block.tensor
            def _(pe):
                def turn(u, p):
                    g = 2 * u + p
                    if live(g - 2, GROUPS):
                        h = g - 2
                        if isinstance(h, int) and h == 0:
                            pe.wait_ge(loaded, 16 * 5)
                        pe.wait_ge(xT_ready, h + 1)
                        for m in range(KD):
                            n = KD * h + m
                            for w, out, made, read in ((wg, ps_g, g_made, gate_ready), (wv, ps_v, v_made, store_ready),
                                                       (wq, ps_q, q_made, que_ready)):
                                if some(n):
                                    pe.wait_ge(read, n)
                                for k in range(KD):
                                    last = nc.tensor.matmul(out[:, :], w[:, k, m * P:(m + 1) * P], xT[:, p, k, :],
                                                            start=(k == 0), stop=(k == KD - 1))
                                last.then_inc(made, 1)
                    if live(g - 3, GROUPS):
                        h, q = g - 3, 1 - p
                        pe.wait_ge(load_ready, KD * (h + 1))
                        if some(h):
                            pe.wait_ge(added, h)
                        for j in range(GT):
                            for k in range(KD):
                                last = nc.tensor.matmul(ps_y[:, j, :], load[:, q, k, j * P:(j + 1) * P], wo[:, k, :],
                                                        start=(k == 0), stop=(k == KD - 1))
                        last.then_inc(y_made, 1)
                    if live(g - 1, GROUPS):
                        h, q = g - 1, 1 - p
                        pe.wait_ge(xn_ready, h + 1)
                        if some(h):
                            pe.wait_ge(xT_ready, h)
                        for j in range(GT):
                            for k in range(KD):
                                last = nc.tensor.transpose(ps_xT[:, k, j * P:(j + 1) * P],
                                                           xn[:, q, j, k * P:(k + 1) * P], ident)
                        last.then_inc(xT_made, 1)

                steps(pe, GROUPS, turn, tail=3, head=2)


def nc_sqrt(x):
    import numpy as np

    return np.float32(np.sqrt(x))


def load_x(nc, sem, x_dram, X, norm, consts, split, scaled):
    with ExitStack() as mem:
        raw = [mem.enter_context(nc.sbuf_tensor(f"raw{n}", [P, KD, DIM], F32)) for n in range(len(split))]
        loaded, high_ready, statistics_ready = sem("loaded"), sem("high_ready"), sem("x_statistics_ready")
        norm.prepare_finish(sem, "ffn1")
        raw_loaded = [sem(f"raw_loaded{n}") for n in range(len(split))]
        x_loaded = [sem(f"x_loaded{g}") for g in range(GROUPS)]
        with nc.Block() as block:
            @block.sync
            def _(sp):
                for n, (of, _, _) in enumerate(split):
                    sp.dma_start(raw[n][:, :, :], of).then_inc(raw_loaded[n], 16)
                for g in range(GROUPS):
                    sp.dma_start(X[:, GT * g:GT * (g + 1), :],
                                 x_dram[g * GTOK:(g + 1) * GTOK, :].rearrange("(j p) d -> p j d", p=P)).then_inc(x_loaded[g], 16)
                for to, of in consts:
                    sp.dma_start(to, of).then_inc(loaded, 16)
                sp.wait_ge(loaded, 16 * len(consts))

            @block.scalar
            def _(act):
                for n, (_, high, _) in enumerate(split):
                    act.wait_ge(raw_loaded[n], 16)
                    nc.scalar.copy(high, raw[n][:, :, :]).then_inc(high_ready, 1)
                norm.finish_on_scalar(act)

            @block.vector
            def _(dve):
                for n, (_, high, low) in enumerate(split):
                    dve.wait_ge(high_ready, n + 1)
                    nc.vector.tensor_tensor(low, raw[n][:, :, :], high.bitcast(F32), ALU.subtract)
                for g in range(GROUPS):
                    dve.wait_ge(x_loaded[g], 16)
                    last = norm.statistics(X[:, GT * g:GT * (g + 1), :], g)
                last.then_inc(statistics_ready, 1)
                dve.wait_ge(statistics_ready, 1)
                norm.finish_on_vector(dve)
                dve.wait_ge(loaded, 16 * len(consts))
                for w, factor in scaled:
                    nc.vector.tensor_scalar(w, w, factor, None, ALU.mult)


def macaron_kernel(nc, out, **inp):
    with ExitStack():
        taken = []

        def sem(name):
            taken.append(nc.alloc_semaphore(name))
            return taken[-1]

        def next_stage():
            nc.clear_and_free_semaphores(taken)
            nc.all_engine_barrier()
            taken.clear()

        with ExitStack() as outer:
            def keep(n, shape, dt=F32):
                return outer.enter_context(nc.sbuf_tensor(n, shape, dt))

            X = keep("X", [P, TILES, DIM])
            ident = keep("ident", [P, P])
            norm = Norm(nc, keep)
            with ExitStack() as mem:
                def sb(n, shape, dt=F32):
                    return mem.enter_context(nc.sbuf_tensor(n, shape, dt))

                w_lora, w_dense, w_b = sb("w_lora", [P, KD, LA]), sb("w_dense", [P, KD, DIM]), sb("w_b", [P, DIM])
                iota8 = sb("iota8", [P, GT, 2, 8])
                wq, wk, wv, wo = ([sb(n + part, [P, KD, DIM], F32R) for part in ("_hi", "_lo")] for n in ("wq", "wk", "wv", "wo"))

                def chunks(w):
                    return w.rearrange("(k p) n -> p k n", p=P)

                load_x(nc, sem, inp["x"], X, norm, [
                    (w_lora[:, :, :], chunks(inp["w_lora"])), (w_dense[:, :, :], chunks(inp["w_dense"])),
                    (w_b[:, :], inp["w_b"]), (ident[:, :], inp["ident"]),
                    (iota8[:, :, :, :], inp["iota8"].rearrange("p (a b c) -> p a b c", a=GT, b=2))], [
                    (chunks(inp[n]), w[0][:, :, :], w[1][:, :, :]) for n, w in (("wq", wq), ("wk", wk), ("wv", wv), ("wo", wo))], [
                    (w_dense[:, :, :], 0.5), (w_b[:, :], 0.5 * 16.0)])
                lora_ffn(nc, "ffn1", sem, X, norm, w_lora, w_dense, w_b[:, :], ident[:, :], iota8)
                norm.finish(sem, "attn")
                attention(nc, sem, X, norm, wq, wk, wv, wo, ident[:, :], inp)
                norm.finish(sem, "ffn2")
                lora_ffn(nc, "ffn2", sem, X, norm, w_lora, w_dense, w_b[:, :], ident[:, :], iota8)
            shares = keep("shares", [P, TILES, TOP_K])
            xhat = nc.dram_tensor("xhat", [TOKENS, DIM], F32).ap()
            y_dram = nc.dram_tensor("y_rows", [Y_ROWS, DIM], F32).ap()
            next_stage()
            moe(nc, sem, "moe1", X, norm, ident[:, :], inp, (xhat, y_dram), shares)
            next_stage()
            smear(nc, sem, X, norm, ident[:, :], inp, shares, y_dram)
            moe(nc, sem, "moe2", X, norm, ident[:, :], inp, (xhat, y_dram), shares)
            combine_and_store(nc, sem, "combine", X, norm, shares, y_dram, out)


def lay_out(a):
    import numpy as np

    c = np.ascontiguousarray
    f = np.float32
    d = {k: np.asarray(v) for k, v in a.items()}
    return {
        "x": c(d["L0_attn_x"].reshape(TOKENS, DIM)),
        "w_lora": c(np.concatenate([d["L0_ffn_A_w"].reshape(LER, DIM).T, d["L0_ffn_gate_w"].T], 1)),
        "w_dense": c(d["L0_ffn_weight"].T),
        "w_b": c(d["L0_ffn_B_w"].transpose(0, 2, 1).reshape(LER, DIM)),
        "wq": c(d["L0_attn_Wq"].T), "wk": c(d["L0_attn_Wk"].T), "wv": c(d["L0_attn_Wv"].T), "wo": c(d["L0_attn_Wo"].T),
        "ident": np.eye(P, dtype=f),
        "ws13": c(np.concatenate([d["L1_ffn_w1_shared"], d["L1_ffn_w3_shared"], d["L1_ffn_gate_w"].T], 1)),
        "ws2": c(d["L1_ffn_w2_shared"]),
        "w13": c(np.concatenate([d["L1_ffn_w1_routed"], d["L1_ffn_w3_routed"]], 2).transpose(1, 0, 2).reshape(DIM, -1)),
        "w2": c(d["L1_ffn_w2_routed"].transpose(1, 0, 2).reshape(HID, -1)),
        "gate_b": c(np.tile(d["L1_ffn_gate_b"], (P, 1))),
        "l1_wg": c(d["L1_attn_Wg"]), "l1_wv": c(d["L1_attn_Wv"]), "l1_wq": c(d["L1_attn_Wq"]), "l1_wo": c(d["L1_attn_Wo"]),
        "l1_bias": c(np.concatenate([d["L1_attn_bg"].reshape(KD, P), d["L1_attn_bq"].reshape(KD, P)]).T),
        "iota16": c(np.tile(np.arange(EXPERTS, dtype=f), (P, TILES))),
        "iota_slot": c(np.tile(np.arange(SLOT_TILES, dtype=f), (P, 1))),
        "pair_no": c((1 + np.arange(TOP_K)[None, :, None] + TOP_K * (P * np.arange(TILES)[None, None, :]
                      + np.arange(P)[:, None, None])).reshape(P, -1).astype(f)),
        "pad_row": c((1 + PAIRS + P * np.arange(SLOT_TILES)[None, :] + np.arange(P)[:, None]).astype(f)),
        "not_first": c(np.tile((np.arange(TILES) > 0).astype(f), (P, EXPERTS))),
        "later": np.triu(np.ones((P, P), f), 1),
        "iota8": c(np.tile(np.arange(8, dtype=f), (P, GT * 2))),
    }


def kernel(**inputs):
    import numpy as np
    import concourse.bacc as bacc
    from concourse.bass_utils import run_bass_kernel_spmd

    nc = bacc.Bacc("TRN2", target_bir_lowering=False, num_devices=1)
    arrays = lay_out(inputs)
    args = {n: nc.dram_tensor(f"in_{n}", a.shape, mybir.dt.from_np(a.dtype), kind="ExternalInput").ap()
            for n, a in arrays.items()}
    out = nc.dram_tensor("out", [TOKENS, DIM], F32, kind="ExternalOutput").ap()
    macaron_kernel(nc, out, **args)
    r = run_bass_kernel_spmd(nc, [{f"in_{n}": a for n, a in arrays.items()}], core_ids=[0])
    return r.results[0]["out"].reshape(BATCH, SEQ, DIM)
```
